# Optimizing a Trainium2 kernel written in Bass

```python
import numpy as np
import jax
import jax.numpy as jnp

def _softmax(x, axis=-1):
    return jax.nn.softmax(x, axis=axis)

def _gelu(x):
    return jax.nn.gelu(x, approximate=True)

def _silu(x):
    return jax.nn.silu(x)

def _sigmoid(x):
    return jax.nn.sigmoid(x)

def _layernorm(x, axis=-1, eps=1e-05):
    m = jnp.mean(x, axis=axis, keepdims=True)
    v = jnp.var(x, axis=axis, keepdims=True)
    return (x - m) / jnp.sqrt(v + eps)

def _scatter_add(tgt, idx, src, axis=0):
    return tgt.at[idx].add(src)

def _segment_sum(src, seg, n):
    return jax.ops.segment_sum(src, seg, n)
kernel_name = 'mk_perceiver_d2_seqx_r8_117eb7'

def setup_inputs(seed: int=0):
    np.random.seed(seed)
    _w = jnp.asarray

    def _rec_inputs():
        import jax
        import jax.numpy as jnp
        _rk = jax.random.key(seed)
        x = 7.22e-05 + 1 * jax.random.normal(jax.random.fold_in(_rk, 1), (2, 128, 128), jnp.float32)
        _lenS = 128 - jax.random.randint(jax.random.fold_in(_rk, 7), (2,), 0, max(1, 128 // 4) + 1, jnp.int32)
        _lenS2 = 2048 - jax.random.randint(jax.random.fold_in(_rk, 8), (2,), 0, max(1, 2048 // 4) + 1, jnp.int32)
        _ctx_1024P = jax.random.normal(jax.random.fold_in(_rk, 11), (2, 16, 128), jnp.float32)
        _ctx_1024c = jax.random.dirichlet(jax.random.fold_in(_rk, 511), 0.3 * jnp.ones((16,), jnp.float32), (2, 2048))
        _ctx_1024t = jnp.einsum('bsk,bkd->bsd', _ctx_1024c, _ctx_1024P)
        _ctx_1024t = _ctx_1024t * jax.lax.rsqrt(jnp.mean(jnp.square(_ctx_1024t)) + 1e-12) * 0.953939
        ctx_1024 = 4.13588e-05 + 0.999923 * (_ctx_1024t + 0.3 * jax.random.normal(jax.random.fold_in(_rk, 611), (2, 2048, 128), jnp.float32))
        _validS = jnp.arange(128)[None, :] < _lenS[:, None]
        _validS2 = jnp.arange(2048)[None, :] < _lenS2[:, None]
        _causal = jnp.tril(jnp.ones((128, 128), dtype=bool))
        mask_BxS2_ik0 = jnp.where(jnp.broadcast_to(_validS2[:, :], (2, 2048)), 0, 1).astype(jnp.int32)
        return (x, ctx_1024, mask_BxS2_ik0)
    x, ctx_1024, mask_BxS2_ik0 = _rec_inputs()

    def _L0_xattn_setup():
        import jax, jax.numpy as jnp
        import numpy as np
        EMBED_DIM = 128
        NUM_HEADS = 16
        HEAD_DIM = EMBED_DIM // NUM_HEADS
        key = jax.random.key(seed)
        ks = jax.random.split(key, 11)
        s = 1.0 / np.sqrt(EMBED_DIM)
        inp = {'query': jax.random.normal(ks[0], (4, 256, EMBED_DIM), jnp.float32), 'key': jax.random.normal(ks[1], (4, 256, EMBED_DIM), jnp.float32), 'value': jax.random.normal(ks[2], (4, 256, EMBED_DIM), jnp.float32), 'Wq': jax.random.uniform(ks[3], (EMBED_DIM, EMBED_DIM), jnp.float32, -s, s), 'bq': jax.random.uniform(ks[4], (EMBED_DIM,), jnp.float32, -s, s), 'Wk': jax.random.uniform(ks[5], (EMBED_DIM, EMBED_DIM), jnp.float32, -s, s), 'bk': jax.random.uniform(ks[6], (EMBED_DIM,), jnp.float32, -s, s), 'Wv': jax.random.uniform(ks[7], (EMBED_DIM, EMBED_DIM), jnp.float32, -s, s), 'bv': jax.random.uniform(ks[8], (EMBED_DIM,), jnp.float32, -s, s), 'Wo': jax.random.uniform(ks[9], (EMBED_DIM, EMBED_DIM), jnp.float32, -s, s), 'bo': jax.random.uniform(ks[10], (EMBED_DIM,), jnp.float32, -s, s)}
        return inp
    _L0_xattn_all = _L0_xattn_setup()
    _L0_xattn_in = {k: v for k, v in _L0_xattn_all.items() if k in ('Wq', 'bq', 'Wk', 'bk', 'Wv', 'bv', 'Wo', 'bo')}
    del _L0_xattn_all

    def _L0_attn_setup():
        import jax, jax.numpy as jnp
        import numpy as np
        D_MODEL = 128
        N_HEADS = 16
        HEAD_DIM = D_MODEL // N_HEADS
        ROPE_BASE = 10000.0

        def _rope(q, k):
            S, Dh = (q.shape[1], q.shape[-1])
            inv_freq = 1.0 / ROPE_BASE ** (jnp.arange(0, Dh, 2, dtype=jnp.float32) / Dh)
            t = jnp.arange(S, dtype=jnp.float32)
            freqs = jnp.outer(t, inv_freq)
            emb = jnp.concatenate([freqs, freqs], axis=-1)
            cos = jnp.cos(emb)[None, :, None, :]
            sin = jnp.sin(emb)[None, :, None, :]

            def rotate_half(v):
                v1, v2 = (v[..., :Dh // 2], v[..., Dh // 2:])
                return jnp.concatenate([-v2, v1], axis=-1)
            return (q * cos + rotate_half(q) * sin, k * cos + rotate_half(k) * sin)
        key = jax.random.key(seed)
        ks = jax.random.split(key, 5)
        B, S = (1, 512)
        scale = 1.0 / np.sqrt(D_MODEL)
        x = jax.random.normal(ks[0], (B, S, D_MODEL), dtype=jnp.float32)
        Wq = jax.random.normal(ks[1], (D_MODEL, D_MODEL), dtype=jnp.float32) * scale
        Wk = jax.random.normal(ks[2], (D_MODEL, D_MODEL), dtype=jnp.float32) * scale
        Wv = jax.random.normal(ks[3], (D_MODEL, D_MODEL), dtype=jnp.float32) * scale
        Wo = jax.random.normal(ks[4], (D_MODEL, D_MODEL), dtype=jnp.float32) * scale
        return {'x': x, 'Wq': Wq, 'Wk': Wk, 'Wv': Wv, 'Wo': Wo}
    _L0_attn_all = _L0_attn_setup()
    _L0_attn_in = {k: v for k, v in _L0_attn_all.items() if k in ('Wq', 'Wk', 'Wv', 'Wo')}
    del _L0_attn_all

    def _L0_ffn_setup():
        import jax, jax.numpy as jnp
        import numpy as np
        E = 8
        K = 2
        CAPACITY_FACTOR = 1.25
        key = jax.random.key(seed)
        ks = jax.random.split(key, 4)
        B, T, C, H = (8, 256, 128, 512)
        x = jax.random.normal(ks[0], (B, T, C), jnp.float32)
        Wr = jax.random.normal(ks[1], (C, E), jnp.float32) * 0.02
        br = jnp.zeros((E,), jnp.float32)
        W1 = jax.random.normal(ks[2], (E, C, H), jnp.float32) * 0.02
        b1 = jnp.zeros((E, H), jnp.float32)
        W2 = jax.random.normal(ks[3], (E, H, C), jnp.float32) * 0.02
        b2 = jnp.zeros((E, C), jnp.float32)
        return {'x': x, 'Wr': Wr, 'br': br, 'W1': W1, 'b1': b1, 'W2': W2, 'b2': b2}
    _L0_ffn_all = _L0_ffn_setup()
    _L0_ffn_in = {k: v for k, v in _L0_ffn_all.items() if k in ('Wr', 'br', 'W1', 'b1', 'W2', 'b2')}
    del _L0_ffn_all

    def _L1_xattn_setup():
        import jax, jax.numpy as jnp
        import numpy as np
        B, N, N2 = (4, 256, 128)
        DIM, DIM_Y, H = (128, 128, 16)
        HD = DIM // H
        SCALE = HD ** (-0.5)
        key = jax.random.key(seed)
        ks = jax.random.split(key, 6)
        s = 0.02
        return {'x': jax.random.normal(ks[0], (B, N, DIM), dtype=jnp.float32), 'y': jax.random.normal(ks[1], (B, N2, DIM_Y), dtype=jnp.float32), 'pad_mask': jax.random.randint(ks[2], (B, N2), 0, 2, dtype=jnp.int32), 'Wq': jax.random.normal(ks[3], (DIM, DIM), dtype=jnp.float32) * s, 'Wkv': jax.random.normal(ks[4], (DIM_Y, 2 * DIM), dtype=jnp.float32) * s, 'Wproj': jax.random.normal(ks[5], (DIM, DIM), dtype=jnp.float32) * s, 'bproj': jnp.zeros((DIM,), dtype=jnp.float32)}
    _L1_xattn_all = _L1_xattn_setup()
    _L1_xattn_in = {k: v for k, v in _L1_xattn_all.items() if k in ('Wq', 'Wkv', 'Wproj', 'bproj')}
    del _L1_xattn_all

    def _L1_attn_setup():
        import jax, jax.numpy as jnp
        import numpy as np
        from jax import lax
        D_MODEL, D_CONV, EXPAND = (128, 4, 2)
        D_INNER = D_MODEL * EXPAND
        B, N = (4, 256)
        key = jax.random.key(seed)
        ks = jax.random.split(key, 10)
        s = 0.02
        return {'x': jax.random.normal(ks[0], (B, N, D_MODEL), jnp.float32), 'W_in': jax.random.normal(ks[1], (D_MODEL, 2 * D_INNER), jnp.float32) * s, 'b_in': jnp.zeros((2 * D_INNER,), jnp.float32), 'conv_w': jax.random.normal(ks[2], (D_INNER, 1, D_CONV), jnp.float32) * 0.2, 'conv_b': jnp.zeros((D_INNER,), jnp.float32), 'W_bc': jax.random.normal(ks[3], (D_INNER, 2 * D_INNER), jnp.float32) * s, 'b_bc': jnp.zeros((2 * D_INNER,), jnp.float32), 'log_decay': jnp.zeros((D_INNER,), jnp.float32), 'W_out': jax.random.normal(ks[4], (D_INNER, D_MODEL), jnp.float32) * s, 'b_out': jnp.zeros((D_MODEL,), jnp.float32)}
    _L1_attn_all = _L1_attn_setup()
    _L1_attn_in = {k: v for k, v in _L1_attn_all.items() if k in ('W_in', 'b_in', 'conv_w', 'conv_b', 'W_bc', 'b_bc', 'log_decay', 'W_out', 'b_out')}
    del _L1_attn_all

    def _L1_ffn_setup():
        import jax, jax.numpy as jnp
        import numpy as np
        HIDDEN = 128
        INNER = 512

        def _weight_quant(w):
            scale = 1.0 / jnp.clip(jnp.mean(jnp.abs(w)), 1e-05)
            wq = jnp.clip(jnp.round(w * scale), -1.0, 1.0) / scale
            return w + jax.lax.stop_gradient(wq - w)

        def _act_quant(x):
            scale = 127.0 / jnp.clip(jnp.max(jnp.abs(x), axis=-1, keepdims=True), 1e-05)
            xq = jnp.clip(jnp.round(x * scale), -128.0, 127.0) / scale
            return x + jax.lax.stop_gradient(xq - x)

        def _bitlinear(x, w):
            return jnp.einsum('bsi,oi->bso', _act_quant(x), _weight_quant(w))
        key = jax.random.key(seed)
        k0, k1, k2, k3 = jax.random.split(key, 4)
        x = jax.random.normal(k0, (4, 256, HIDDEN), dtype=jnp.float32)
        w_gate = jax.random.normal(k1, (INNER, HIDDEN), dtype=jnp.float32) / np.sqrt(HIDDEN)
        w_up = jax.random.normal(k2, (INNER, HIDDEN), dtype=jnp.float32) / np.sqrt(HIDDEN)
        w_down = jax.random.normal(k3, (HIDDEN, INNER), dtype=jnp.float32) / np.sqrt(INNER)
        return {'x': x, 'w_gate': w_gate, 'w_up': w_up, 'w_down': w_down}
    _L1_ffn_all = _L1_ffn_setup()
    _L1_ffn_in = {k: v for k, v in _L1_ffn_all.items() if k in ('w_gate', 'w_up', 'w_down')}
    del _L1_ffn_all
    return {'x': x, 'ctx_1024': ctx_1024, 'mask_BxS2_ik0': mask_BxS2_ik0, 'L0_xattn_Wq': _L0_xattn_in['Wq'], 'L0_xattn_bq': _L0_xattn_in['bq'], 'L0_xattn_Wk': _L0_xattn_in['Wk'], 'L0_xattn_bk': _L0_xattn_in['bk'], 'L0_xattn_Wv': _L0_xattn_in['Wv'], 'L0_xattn_bv': _L0_xattn_in['bv'], 'L0_xattn_Wo': _L0_xattn_in['Wo'], 'L0_xattn_bo': _L0_xattn_in['bo'], 'L0_attn_Wq': _L0_attn_in['Wq'], 'L0_attn_Wk': _L0_attn_in['Wk'], 'L0_attn_Wv': _L0_attn_in['Wv'], 'L0_attn_Wo': _L0_attn_in['Wo'], 'L0_ffn_Wr': _L0_ffn_in['Wr'], 'L0_ffn_br': _L0_ffn_in['br'], 'L0_ffn_W1': _L0_ffn_in['W1'], 'L0_ffn_b1': _L0_ffn_in['b1'], 'L0_ffn_W2': _L0_ffn_in['W2'], 'L0_ffn_b2': _L0_ffn_in['b2'], 'L1_xattn_Wq': _L1_xattn_in['Wq'], 'L1_xattn_Wkv': _L1_xattn_in['Wkv'], 'L1_xattn_Wproj': _L1_xattn_in['Wproj'], 'L1_xattn_bproj': _L1_xattn_in['bproj'], 'L1_attn_W_in': _L1_attn_in['W_in'], 'L1_attn_b_in': _L1_attn_in['b_in'], 'L1_attn_conv_w': _L1_attn_in['conv_w'], 'L1_attn_conv_b': _L1_attn_in['conv_b'], 'L1_attn_W_bc': _L1_attn_in['W_bc'], 'L1_attn_b_bc': _L1_attn_in['b_bc'], 'L1_attn_log_decay': _L1_attn_in['log_decay'], 'L1_attn_W_out': _L1_attn_in['W_out'], 'L1_attn_b_out': _L1_attn_in['b_out'], 'L1_ffn_w_gate': _L1_ffn_in['w_gate'], 'L1_ffn_w_up': _L1_ffn_in['w_up'], 'L1_ffn_w_down': _L1_ffn_in['w_down']}

def reference(x, ctx_1024, mask_BxS2_ik0, L0_xattn_Wq, L0_xattn_bq, L0_xattn_Wk, L0_xattn_bk, L0_xattn_Wv, L0_xattn_bv, L0_xattn_Wo, L0_xattn_bo, L0_attn_Wq, L0_attn_Wk, L0_attn_Wv, L0_attn_Wo, L0_ffn_Wr, L0_ffn_br, L0_ffn_W1, L0_ffn_b1, L0_ffn_W2, L0_ffn_b2, L1_xattn_Wq, L1_xattn_Wkv, L1_xattn_Wproj, L1_xattn_bproj, L1_attn_W_in, L1_attn_b_in, L1_attn_conv_w, L1_attn_conv_b, L1_attn_W_bc, L1_attn_b_bc, L1_attn_log_decay, L1_attn_W_out, L1_attn_b_out, L1_ffn_w_gate, L1_ffn_w_up, L1_ffn_w_down):
    import jax
    import jax.numpy as jnp

    def _L0_xattn_ref(query, key, value, Wq, bq, Wk, bk, Wv, bv, Wo, bo):
        import jax, jax.numpy as jnp
        import numpy as np
        EMBED_DIM = 128
        NUM_HEADS = 16
        HEAD_DIM = EMBED_DIM // NUM_HEADS
        B, T, E = query.shape
        S = key.shape[1]
        H, D = (NUM_HEADS, HEAD_DIM)
        q = (query @ Wq.T + bq).reshape(B, T, H, D).transpose(0, 2, 1, 3)
        k = (key @ Wk.T + bk).reshape(B, S, H, D).transpose(0, 2, 1, 3)
        v = (value @ Wv.T + bv).reshape(B, S, H, D).transpose(0, 2, 1, 3)
        scores = jnp.einsum('bhtd,bhsd->bhts', q, k) / np.sqrt(D)
        causal = jnp.triu(jnp.full((T, S), -jnp.inf, jnp.float32), k=1)
        scores = scores + causal[None, None]
        attn = jax.nn.softmax(scores, axis=-1)
        out = jnp.einsum('bhts,bhsd->bhtd', attn, v)
        out = out.transpose(0, 2, 1, 3).reshape(B, T, E)
        out = out @ Wo.T + bo
        return out

    def _L0_attn_ref(x, Wq, Wk, Wv, Wo):
        import jax, jax.numpy as jnp
        import numpy as np
        D_MODEL = 128
        N_HEADS = 16
        HEAD_DIM = D_MODEL // N_HEADS
        ROPE_BASE = 10000.0

        def _rope(q, k):
            S, Dh = (q.shape[1], q.shape[-1])
            inv_freq = 1.0 / ROPE_BASE ** (jnp.arange(0, Dh, 2, dtype=jnp.float32) / Dh)
            t = jnp.arange(S, dtype=jnp.float32)
            freqs = jnp.outer(t, inv_freq)
            emb = jnp.concatenate([freqs, freqs], axis=-1)
            cos = jnp.cos(emb)[None, :, None, :]
            sin = jnp.sin(emb)[None, :, None, :]

            def rotate_half(v):
                v1, v2 = (v[..., :Dh // 2], v[..., Dh // 2:])
                return jnp.concatenate([-v2, v1], axis=-1)
            return (q * cos + rotate_half(q) * sin, k * cos + rotate_half(k) * sin)
        B, S, _ = x.shape
        H, Dh = (N_HEADS, HEAD_DIM)
        q = (x @ Wq.T).reshape(B, S, H, Dh)
        k = (x @ Wk.T).reshape(B, S, H, Dh)
        v = (x @ Wv.T).reshape(B, S, H, Dh)
        q, k = _rope(q, k)
        scale = 1.0 / np.sqrt(Dh)
        scores = jnp.einsum('bqhd,bkhd->bhqk', q, k) * scale
        causal = jnp.triu(jnp.ones((S, S), dtype=bool), k=1)
        scores = jnp.where(causal, -jnp.inf, scores)
        attn = jax.nn.softmax(scores, axis=-1)
        out = jnp.einsum('bhqk,bkhd->bqhd', attn, v).reshape(B, S, H * Dh)
        return out @ Wo.T

    def _L0_ffn_ref(x, Wr, br, W1, b1, W2, b2):
        import jax, jax.numpy as jnp
        import numpy as np
        E = 8
        K = 2
        CAPACITY_FACTOR = 1.25
        B, T, C = x.shape
        cap = max(1, int(T / E * CAPACITY_FACTOR))
        probs = jax.nn.softmax(x @ Wr + br, axis=-1)
        topk_p, topk_e = jax.lax.top_k(probs, K)
        e_flat = topk_e.reshape(B, T * K)
        p_flat = topk_p.reshape(B, T * K)
        oh = jax.nn.one_hot(e_flat, E, dtype=jnp.int32)
        pos_all = jnp.cumsum(oh, axis=1) - oh
        pos = jnp.take_along_axis(pos_all, e_flat[:, :, None], axis=2)[:, :, 0]
        keep = pos < cap
        b_idx = jnp.arange(B)[:, None]
        flat_idx = (e_flat * B + b_idx) * cap + jnp.minimum(pos, cap - 1)
        x_rep = jnp.broadcast_to(x[:, :, None, :], (B, T, K, C)).reshape(B, T * K, C)
        buf = jnp.zeros((E * B * cap, C), x.dtype).at[flat_idx.reshape(-1)].add((x_rep * keep[:, :, None].astype(x.dtype)).reshape(-1, C))
        buf = buf.reshape(E, B * cap, C)
        h = jax.nn.relu(jnp.einsum('enc,ech->enh', buf, W1) + b1[:, None, :])
        y = jnp.einsum('enh,ehc->enc', h, W2) + b2[:, None, :]
        y_tok = y.reshape(E * B * cap, C)[flat_idx.reshape(-1)].reshape(B, T * K, C)
        y_tok = y_tok * (p_flat * keep.astype(x.dtype))[:, :, None]
        return y_tok.reshape(B, T, K, C).sum(axis=2)

    def _L1_xattn_ref(x, y, pad_mask, Wq, Wkv, Wproj, bproj):
        import jax, jax.numpy as jnp
        import numpy as np
        B, N, N2 = (4, 256, 128)
        DIM, DIM_Y, H = (128, 128, 16)
        HD = DIM // H
        SCALE = HD ** (-0.5)
        b, n, c = x.shape
        n2 = y.shape[1]
        q = (x @ Wq).reshape(b, n, H, HD).transpose(0, 2, 1, 3)
        kv = (y @ Wkv).reshape(b, n2, 2, H, HD).transpose(2, 0, 3, 1, 4)
        k, v = (kv[0], kv[1])
        scores = jnp.einsum('bhnd,bhmd->bhnm', q * SCALE, k)
        keep = pad_mask.astype(bool)[:, None, None, :]
        scores = jnp.where(keep, scores, -jnp.inf)
        attn = jax.nn.softmax(scores, axis=-1)
        out = jnp.einsum('bhnm,bhmd->bhnd', attn, v)
        out = out.transpose(0, 2, 1, 3).reshape(b, n, c)
        return out @ Wproj + bproj

    def _L1_attn_ref(x, W_in, b_in, conv_w, conv_b, W_bc, b_bc, log_decay, W_out, b_out):
        import jax, jax.numpy as jnp
        import numpy as np
        from jax import lax
        D_MODEL, D_CONV, EXPAND = (128, 4, 2)
        D_INNER = D_MODEL * EXPAND
        B, N = (4, 256)
        Bsz, Nlen, _ = x.shape
        d_inner = conv_w.shape[0]
        d_conv = conv_w.shape[-1]
        ug = x @ W_in + b_in
        u, gate = jnp.split(ug, 2, axis=-1)
        u_t = jnp.transpose(u, (0, 2, 1))
        u_conv = lax.conv_general_dilated(u_t, conv_w, window_strides=(1,), padding=[(d_conv - 1, 0)], dimension_numbers=('NCH', 'OIH', 'NCH'), feature_group_count=d_inner)
        u_conv = u_conv + conv_b[None, :, None]
        u_conv = jnp.transpose(u_conv, (0, 2, 1))
        u_conv = jax.nn.silu(u_conv)
        bc = u_conv @ W_bc + b_bc
        b, c = jnp.split(bc, 2, axis=-1)
        a = jnp.exp(-jax.nn.softplus(log_decay)).astype(x.dtype)

        def step(state, bc_t):
            b_t, c_t = bc_t
            state = state * a + b_t
            return (state, state * c_t)
        xs = (jnp.moveaxis(b, 1, 0), jnp.moveaxis(c, 1, 0))
        init = jnp.zeros((Bsz, d_inner), x.dtype)
        _, ys = lax.scan(step, init, xs)
        y = jnp.moveaxis(ys, 0, 1)
        y = y * jax.nn.sigmoid(gate)
        return y @ W_out + b_out

    def _L1_ffn_ref(x, w_gate, w_up, w_down):
        import jax, jax.numpy as jnp
        import numpy as np
        HIDDEN = 128
        INNER = 512

        def _weight_quant(w):
            scale = 1.0 / jnp.clip(jnp.mean(jnp.abs(w)), 1e-05)
            wq = jnp.clip(jnp.round(w * scale), -1.0, 1.0) / scale
            return w + jax.lax.stop_gradient(wq - w)

        def _act_quant(x):
            scale = 127.0 / jnp.clip(jnp.max(jnp.abs(x), axis=-1, keepdims=True), 1e-05)
            xq = jnp.clip(jnp.round(x * scale), -128.0, 127.0) / scale
            return x + jax.lax.stop_gradient(xq - x)

        def _bitlinear(x, w):
            return jnp.einsum('bsi,oi->bso', _act_quant(x), _weight_quant(w))
        gate = jax.nn.silu(_bitlinear(x, w_gate))
        up = _bitlinear(x, w_up)
        return _bitlinear(gate * up, w_down)
    x = x + _L0_xattn_ref(_layernorm(x, axis=-1), ctx_1024, ctx_1024, L0_xattn_Wq, L0_xattn_bq, L0_xattn_Wk, L0_xattn_bk, L0_xattn_Wv, L0_xattn_bv, L0_xattn_Wo, L0_xattn_bo)
    x = x + _L0_attn_ref(_layernorm(x, axis=-1), L0_attn_Wq, L0_attn_Wk, L0_attn_Wv, L0_attn_Wo)
    x = x + _L0_ffn_ref(_layernorm(x, axis=-1), L0_ffn_Wr, L0_ffn_br, L0_ffn_W1, L0_ffn_b1, L0_ffn_W2, L0_ffn_b2)
    x = x + _L1_xattn_ref(_layernorm(x, axis=-1), ctx_1024, mask_BxS2_ik0, L1_xattn_Wq, L1_xattn_Wkv, L1_xattn_Wproj, L1_xattn_bproj)
    x = x + _L1_attn_ref(_layernorm(x, axis=-1), L1_attn_W_in, L1_attn_b_in, L1_attn_conv_w, L1_attn_conv_b, L1_attn_W_bc, L1_attn_b_bc, L1_attn_log_decay, L1_attn_W_out, L1_attn_b_out)
    x = x + _L1_ffn_ref(_layernorm(x, axis=-1), L1_ffn_w_gate, L1_ffn_w_up, L1_ffn_w_down)
    return x

_drawn_inputs = setup_inputs


def setup_inputs(seed=0):
    import zlib

    import numpy as np

    out = dict(_drawn_inputs(seed))
    spreads = {'L0_ffn_br': (0.0, 0.399),
     'L0_ffn_b1': (0.0, 0.8),
     'L0_ffn_b2': (0.0, 0.502),
     'L1_xattn_bproj': (0.0, 0.1),
     'L1_attn_b_in': (0.0, 0.8),
     'L1_attn_conv_b': (0.0, 0.8),
     'L1_attn_b_bc': (0.0, 0.8),
     'L1_attn_log_decay': (0.0, 0.8),
     'L1_attn_b_out': (0.0, 0.8)}
    factors = {'L0_xattn_bq': 8.0,
     'L0_xattn_bk': 64.0,
     'L0_ffn_Wr': 3.341,
     'L0_ffn_W1': 5.506,
     'L0_ffn_W2': 4.408,
     'L1_xattn_Wq': 64.0,
     'L1_attn_W_in': 8.0,
     'L1_attn_conv_w': 8.0,
     'L1_attn_W_bc': 8.0,
     'L1_attn_W_out': 8.0,
     'L1_ffn_w_gate': 8.0,
     'L1_ffn_w_up': 8.0,
     'L1_ffn_w_down': 8.0}
    for name, (base, spread) in spreads.items():
        noise = np.random.default_rng([zlib.crc32(name.encode()), seed]).standard_normal(out[name].shape)
        drawn = base * np.exp(spread * noise) if base else spread * noise
        out[name] = jnp.asarray(drawn.astype(out[name].dtype))
    for name, factor in factors.items():
        out[name] = (out[name] * factor).astype(out[name].dtype)
    return out
```

```python
import concourse.bass as bass
from concourse import mybir
from contextlib import ExitStack
import numpy as np

ALU = mybir.AluOpType
ACT = mybir.ActivationFunctionType
AX = mybir.AxisListType
F32 = mybir.dt.float32
BF16 = mybir.dt.bfloat16
I32 = mybir.dt.int32
U32 = mybir.dt.uint32

P = 128
B = 2
H, DH = 16, 8
G = 4
J = H // G
CTX = 2048
NT = CTX // P
NS = 2
E, SLOTS, CAP = 8, 32, 20
HC = 4
EPS = 1e-5
SCALE = DH ** -0.5
NEG = -1e30
MAGIC = 1.5 * 2 ** 23


def columns(**widths):
    at, out = 0, {}
    for name, w in widths.items():
        out[name] = (at, at + w)
        at += w
    return out, at


FIRST, FIRST_W = columns(wq=P, wk=P, wv=P, bq=1, bk=1, ctx=B * P)
CONST, CONST_W = columns(ident=P, causal=P, before=P, cos=P, sin=P, delta=J, slot=SLOTS, tile=1, batch=B, expert=E)
CONSTB, CONSTB_W = columns(ident=P, causal=P, before=P)
SELF, SELF_W = columns(wq=P, wqs=P, wk=P, wks=P, wv=P, wo=G * P)
ROWS, ROWS_W = columns(bv=P, bo=P, br=E, bproj=P, bout=P)
MOE, MOE_W = columns(wr=E, b1=E * HC, b2=2 * P)
CROSS, CROSS_W = columns(wq=P, wk=P, wv=P, wo=G * P)
SCAN, SCAN_W = columns(win=4 * P, bin=4, cw=8, cb=2, bbc=4, ld=2, wout=2 * P, wbc=8 * P)
FFN, FFN_W = columns(gate=4 * P, up=4 * P, down=4 * P)


def program(nc, d):
    with ExitStack() as ctx:
        def sb(name, shape, dt=F32):
            return ctx.enter_context(nc.sbuf_tensor(name, shape, dt))

        def ps(name, shape, dt=F32):
            return ctx.enter_context(nc.psum_tensor(name, shape, dt))

        made = {}

        def sem(name):
            if name not in made:
                made[name] = ctx.enter_context(nc.semaphore(name))
            return made[name]

        X = sb("X", [P, B, P])
        first = sb("first", [P, FIRST_W])
        const = sb("const", [P, CONST_W])
        constb = sb("constb", [P, CONSTB_W], BF16)
        selfw = sb("selfw", [P, SELF_W])
        woA = sb("woA", [P, G, P])
        rows = sb("rows", [1, ROWS_W])
        moe = sb("moe", [P, MOE_W])
        w1 = sb("w1", [P, E, HC * P])
        w2 = sb("w2", [P, E * HC, P])
        cross = sb("cross", [P, CROSS_W])
        scanw = sb("scanw", [P, SCAN_W])
        ffn = sb("ffn", [P, FFN_W])
        mask = sb("mask", [B * NT, P], I32)

        def part(t, table, name):
            a, b = table[name]
            return t[:, a:b]

        ident = part(const, CONST, "ident")
        identb = part(constb, CONSTB, "ident")
        delta = part(const, CONST, "delta")

        ones = sb("ones", [P, P])
        twos = sb("twos", [1, P])
        onesb = sb("onesb", [P, P], BF16)
        neghalf = sb("neghalf", [P, B])

        stats = sb("stats", [P, B, 6])
        mv = sb("mv", [P, B, 2])
        veps = sb("veps", [P, B])
        rstd = sb("rstd", [P, B])
        xn = sb("xn", [P, B, P])
        xnT = sb("xnT", [P, B * P])

        QT = sb("QT", [P, B * P])
        KT = sb("KT", [P, NS * B * P])
        rope = sb("rope", [P, 4, B * P])
        KB = sb("KB", [P, B, J, P])
        KBx = sb("KBx", [P, B * NS, J, P])
        VA = sb("VA", [P, B, H, 32])
        VB = sb("VB", [P, B, H, 32])
        VX = sb("VX", [P, B * NS, H, 32])
        MX = sb("MX", [P, B * G, J])
        PR = sb("PR", [P, 4, NS * J, P])
        PT = sb("PT", [P, 4, NS * J, P])
        rden = sb("rden", [P, G * P])
        ON = sb("ON", [P, B, G, P])

        keepm = sb("keepm", [B * NT, P])
        act32 = sb("act32", [B * NT, 1])
        actv = sb("actv", [B * NT, 1])
        actb = sb("actb", [B * NT, B])
        lst = sb("lst", [1, B, NT])
        lstin = sb("lstin", [1, B, NT])
        lsttmp = sb("lsttmp", [1, B, NT])
        idf = sb("idf", [1, B, NT])
        ids = sb("ids", [1, B, NT], I32)
        have = sb("have", [1, B, NS])
        cnti = sb("cnti", [1, B], I32)
        most = sb("most", [1, 1], I32)
        cnt = sb("cnt", [P, B])
        anyk = sb("anyk", [P, B])
        ranyk = sb("ranyk", [P, B])
        nanf = sb("nanf", [P, B])
        ctxS = sb("ctxS", [P, B * NS, P])
        maskS = sb("maskS", [1, B * NS, P], I32)
        keepS = sb("keepS", [1, B * NS, P])
        biasS = sb("biasS", [P, B * NS, P], BF16)

        gctx = sb("gctx", [P, P])
        gmask = sb("gmask", [1, P], I32)
        gkeep = sb("gkeep", [1, P])
        gbias = sb("gbias", [P, P], BF16)
        gKB = sb("gKB", [P, J, P])
        gV = sb("gV", [P, H, DH + 1])
        gm = sb("gm", [P, H])
        gmt = sb("gmt", [P, H])
        gmn = sb("gmn", [P, H])
        gal = sb("gal", [P, H])
        gacc = sb("gacc", [P, H, DH + 1])
        gsc = sb("gsc", [P, H, DH + 1])
        gpad = sb("gpad", [P, 2, H, 32])

        lg = sb("lg", [P, B, E])
        lmax = sb("lmax", [P, B])
        lsum = sb("lsum", [P, B])
        prob = sb("prob", [P, B, E])
        top = sb("top", [P, B, 8])
        topi = sb("topi", [P, B, 8], U32)
        topf = sb("topf", [P, B, 2])
        oh1 = sb("oh1", [P, B, E])
        oh = sb("oh", [P, B, E])
        ohb = sb("ohb", [P, B, E], BF16)
        gates = sb("gates", [P, B, E])
        eq = sb("eq", [P, B * E, SLOTS])
        disp = sb("disp", [P, B * E, SLOTS])
        comb = sb("comb", [P, B * E, SLOTS])
        combT = sb("combT", [P, B, 2, P])
        buf = sb("buf", [P, E, B, SLOTS])
        hid = PR[:, 0:2, :, :].rearrange("p a j k -> p (a j k)").rearrange("p (e h s) -> p e h s", e=E, h=HC)
        ysb = sb("ysb", [P, B, 2, P])

        upad = sb("upad", [P, 2, B, P + 3])
        conv = sb("conv", [P, 2, B, P])
        th = sb("th", [P, 2, B * P])
        su = sb("su", [P, 2, B * P])
        thg = sb("thg", [P, 2, B * P])
        bT = sb("bT", [P, 2, B * P])
        cT = sb("cT", [P, 2, B * P])
        st = sb("st", [P, 2, B * P])
        decay = sb("decay", [P, 2, B, P])
        avec = sb("avec", [P, 4])
        bgh = sb("bgh", [P, 2])

        wabs = sb("wabs", [P, 3])
        wjunk = sb("wjunk", [P, HC * P])
        wmean = sb("wmean", [P, 3])
        wscale = sb("wscale", [P, 3])
        wtmp = sb("wtmp", [P, HC * P])
        wq3 = sb("wq3", [P, 3, HC * P], BF16)
        amax = sb("amax", [P, B])
        sx = sb("sx", [P, B])
        fx = sb("fx", [P, B])
        ch = sb("ch", [P, B])
        kk = sb("kk", [P, B])
        kd = sb("kd", [P, B])
        qf = sb("qf", [P, B, P])
        xq = sb("xq", [P, B, P], BF16)
        xqT = sb("xqT", [P, B * P], BF16)
        thf = PT[:, 0, :, :].rearrange("p j k -> p (j k)").rearrange("p (b n) -> p b n", b=B)
        hm = PT[:, 1, :, :].rearrange("p j k -> p (j k)").rearrange("p (b n) -> p b n", b=B)
        hq = sb("hq", [P, B, HC * P], BF16)
        hqT = sb("hqT", [P, B, HC, P], BF16)
        hmax = sb("hmax", [P, B])
        sh = sb("sh", [P, B])

        S = ps("S", [P, 4, 512])
        T = ps("T", [P, 2, 512])
        O = ps("O", [P, 512])
        D = ps("D", [P, 512])

        block = ctx.enter_context(nc.Block())

        @block.sync
        def _(e):
            e.dma_start(X[:, :, :], d["x"].rearrange("b t c -> t b c")).then_inc(sem("x_in"), 16)
            e.dma_start(first[:, :], d["first"]).then_inc(sem("first_in"), 16)
            e.dma_start(mask[:, :], d["mask"].rearrange("b (j k) -> (b j) k", k=P)).then_inc(sem("mask_in"), 16)
            e.dma_start(rows[:, :], d["rows"]).then_inc(sem("rows_in"), 16)
            e.dma_start(woA[:, :, :], d["woA"]).then_inc(sem("woA_in"), 16)
            e.dma_start(selfw[:, :], d["selfw"]).then_inc(sem("self_in"), 16)
            e.dma_start(cross[:, :], d["cross"]).then_inc(sem("cross_in"), 16)
            e.wait_ge(sem("list_made"), 1)
            for b in range(B):
                for s in range(NS):
                    t = e.value_load(ids[0:1, b, s:s + 1], min_val=0, max_val=NT - 1)
                    e.dma_start(ctxS[:, b * NS + s, :],
                                d["ctxT"][:, b, bass.ds(t * P, P)]).then_inc(sem("ctxS_in"), 16)
                    e.dma_start(maskS[:, b * NS + s, :],
                                d["mask"][b:b + 1, bass.ds(t * P, P)]).then_inc(sem("maskS_in"), 16)
            e.dma_start(moe[:, :], d["moe"]).then_inc(sem("moe_in"), 16)
            for i in range(4):
                e.dma_start(w1[:, 2 * i:2 * i + 2, :], d["w1"][:, 2 * i:2 * i + 2, :]).then_inc(sem(f"w1_in{i}"), 16)
            for i in range(2):
                e.dma_start(w2[:, 16 * i:16 * i + 16, :],
                            d["w2"][:, 16 * i:16 * i + 16, :]).then_inc(sem(f"w2_in{i}"), 16)
            e.dma_start(scanw[:, :], d["scanw"]).then_inc(sem("scan_in"), 16)
            e.dma_start(ffn[:, :], d["ffn"]).then_inc(sem("ffn_in"), 16)
            with e.If(e.value_load(most[0:1, 0:1], min_val=0, max_val=NT) > NS):
                for b in range(B):
                    n = e.value_load(cnti[0:1, b:b + 1], min_val=0, max_val=NT)
                    with e.Fori(0, NT) as i:
                        with e.If(n > i):
                            t = e.value_load(ids[0:1, b, bass.ds(i, 1)], min_val=0, max_val=NT - 1)
                            e.wait_ge(sem(f"g_kvs{b}"), i + 1)
                            e.dma_start(gctx[:, :], d["ctxT"][:, b, bass.ds(t * P, P)]).then_inc(sem(f"gctx_in{b}"), 16)
                            e.dma_start(gmask[:, :], d["mask"][b:b + 1, bass.ds(t * P, P)]).then_inc(sem(f"gmask_in{b}"), 16)
            for b in range(B):
                e.wait_ge(sem("x_out"), b + 1)
                e.dma_start(d["out"][b], X[:, b, :]).then_inc(sem("stored"), 16)
            e.wait_ge(sem("stored"), 32)

        @block.gpsimd
        def _(e):
            e.memset(neghalf[:, :], -0.5).then_inc(sem("pool_const"), 1)
            e.memset(ones[:, :], 1.0).then_inc(sem("pool_const"), 1)
            e.memset(twos[:, :], 2.0).then_inc(sem("pool_const"), 1)
            e.memset(onesb[:, :], 1.0).then_inc(sem("pool_const"), 1)
            for t in (VA, VB, VX, upad, decay, gpad, gV, biasS, gbias):
                n = len(t.shape)
                e.memset(t[tuple([slice(None)] * n)], 0.0).then_inc(sem("pool_zero"), 1)

            def power(n):
                e.wait_ge(sem("veps"), n + 1)
                e.tensor_tensor(rstd[:, :], veps[:, :], neghalf[:, :], ALU.pow).then_inc(sem("rstd"), 1)

            e.wait_ge(sem("pool_const"), 4)
            power(0)
            power(1)
            e.wait_ge(sem("scan_in"), 16)
            e.tensor_scalar(bgh[:, :], part(scanw, SCAN, "bin")[:, 2:4], 0.5, None, ALU.mult).then_inc(sem("bgh"), 1)
            e.wait_ge(sem("avec"), 1)
            e.wait_ge(sem("pool_zero"), 7)
            for ct in range(2):
                for b in range(B):
                    e.tensor_copy(decay[:, ct, b, 1:P],
                                  avec[:, 2 + ct:3 + ct].to_broadcast([P, P - 1])).then_inc(sem("decay"), 1)
            power(2)
            e.wait_ge(sem("wscale"), 1)
            for m in range(3):
                w = ffn[:, m * HC * P:(m + 1) * HC * P]
                if m:
                    e.wait_ge(sem("w_round"), 3 * m)
                e.tensor_scalar(wtmp[:, :], w, wscale[:, m:m + 1], MAGIC, ALU.mult, ALU.add).then_inc(sem("w_round"), 1)
                e.wait_ge(sem("w_round"), 3 * m + 1)
                e.tensor_scalar(wtmp[:, :], wtmp[:, :], MAGIC, 1.0, ALU.subtract, ALU.min).then_inc(sem("w_round"), 1)
                e.wait_ge(sem("w_round"), 3 * m + 2)
                e.tensor_scalar(wq3[:, m, :], wtmp[:, :], -1.0, None, ALU.max).then_inc(sem("w_round"), 1)
            power(3)
            power(4)
            power(5)

        @block.scalar
        def _(e):
            e.dma_start(const[:, :], d["const"]).then_inc(sem("const_in"), 16)
            e.wait_ge(sem("const_in"), 16)
            e.activation(constb[:, :], const[:, 0:CONSTB_W], ACT.Copy).then_inc(sem("constb"), 1)

            def softmax(p, ns):
                def exps(i):
                    e.wait_ge(sem(p + "shifted"), i + 1)
                    t = PR[:, i % 4, 0:ns * J, :]
                    e.activation(t, t, ACT.Exp).then_inc(sem(p + "exp"), 1)

                def evac(i):
                    for s in range(ns):
                        u = i * ns + s
                        e.wait_ge(sem(p + "transposed"), u + 1)
                        if i >= 4:
                            e.wait_ge(sem(p + "pv"), i - 3)
                        e.activation(PT[:, i % 4, s * J:(s + 1) * J, :], T[:, u % 2, :].rearrange("p (j k) -> p j k", j=J),
                                     ACT.Copy).then_inc(sem(p + "pt"), 1)

                exps(0)
                for i in range(1, B * G):
                    exps(i)
                    evac(i - 1)
                evac(B * G - 1)

            e.wait_ge(sem("pool_zero"), 1)
            for b in range(B):
                e.wait_ge(sem("A_v"), B)
                e.activation(VA[:, b, :, 0:DH], S[:, 1, b * P:(b + 1) * P].rearrange("p (h d) -> p h d", d=DH),
                             ACT.Copy).then_inc(sem("A_va"), 1)
            softmax("A_", 1)
            e.wait_ge(sem("pool_zero"), 3)
            e.wait_ge(sem("D_v"), 1)
            for s in range(B * NS):
                e.activation(VX[:, s, :, 0:DH], D[:, s * P:(s + 1) * P].rearrange("p (h d) -> p h d", d=DH),
                             ACT.Copy).then_inc(sem("D_vx"), 1)
            for b in range(B):
                e.wait_ge(sem("B_v"), B)
                e.activation(VB[:, b, :, 0:DH], D[:, b * P:(b + 1) * P].rearrange("p (h d) -> p h d", d=DH),
                             ACT.Copy).then_inc(sem("B_vb"), 1)
            softmax("B_", 1)
            e.wait_ge(sem("scan_in"), 16)
            e.activation(avec[:, 0:2], part(scanw, SCAN, "ld"), ACT.Exp).then_inc(sem("decay_exp"), 1)
            e.wait_ge(sem("ffn_in"), 16)
            for m in range(3):
                if m:
                    e.wait_ge(sem("wabs"), m)
                e.activation(wjunk[:, :], ffn[:, m * HC * P:(m + 1) * HC * P], ACT.Abs,
                             accum_out=wabs[:, m:m + 1]).then_inc(sem("wabs"), 1)
            e.wait_ge(sem("C_lg"), 1)
            e.activation(lg[:, :, :], lg[:, :, :], ACT.Exp).then_inc(sem("C_exp"), 1)
            for b in range(B):
                e.wait_ge(sem("C_buf"), b + 1)
                e.activation(buf[:, :, b, :], T[:, b, 0:E * SLOTS].rearrange("p (e s) -> p e s", e=E),
                             ACT.Copy).then_inc(sem("C_bufs"), 1)
            e.wait_ge(sem("C_ct"), 1)
            e.activation(combT[:, :, :, :].rearrange("p b h t -> p (b h t)"), D[:, :], ACT.Copy).then_inc(sem("C_cts"), 1)
            for i in range(4):
                e.wait_ge(sem("C_hb"), i + 1)
                t = hid[:, 2 * i:2 * i + 2, :, :]
                e.activation(t, t, ACT.Relu).then_inc(sem("C_h"), 1)
            softmax("D_", NS)
            with e.If(e.value_load(most[0:1, 0:1], min_val=0, max_val=NT) > NS):
                for b in range(B):
                    n = e.value_load(cnti[0:1, b:b + 1], min_val=0, max_val=NT)
                    with e.Fori(0, NT) as i:
                        with e.If(n > i):
                            e.wait_ge(sem(f"g_shift{b}"), i + 1)
                            e.activation(gal[:, :], gal[:, :], ACT.Exp)
                            t = PR[:, 0:2, :, :].rearrange("p a j k -> p (a j k)")
                            e.activation(t, t, ACT.Exp).then_inc(sem(f"g_exp{b}"), 1)
            for ct in range(2):
                e.wait_ge(sem("E_u"), ct + 1)
                e.activation(upad[:, ct, :, 3:P + 3], S[:, ct, 0:B * P].rearrange("p (b t) -> p b t", b=B),
                             ACT.Identity, bias=part(scanw, SCAN, "bin")[:, ct:ct + 1]).then_inc(sem("E_up"), 1)
            e.wait_ge(sem("bgh"), 1)
            for ct in range(2):
                e.wait_ge(sem("E_g"), ct + 1)
                e.activation(thg[:, ct, :], S[:, 2 + ct, 0:B * P], ACT.Tanh, scale=0.5,
                             bias=bgh[:, ct:ct + 1]).then_inc(sem("E_thg"), 1)
            for ct in range(2):
                e.wait_ge(sem("E_conv"), ct + 1)
                e.activation(th[:, ct, :], conv[:, ct, :, :].rearrange("p b t -> p (b t)"), ACT.Tanh,
                             scale=0.5).then_inc(sem("E_th"), 1)
            for ct in range(2):
                e.wait_ge(sem("E_c"), ct + 1)
                e.activation(cT[:, ct, :], (O, D)[ct][:, 0:B * P], ACT.Identity, scale=0.5,
                             bias=part(scanw, SCAN, "bbc")[:, 2 + ct:3 + ct]).then_inc(sem("E_cs"), 1)
            for b in range(B):
                e.wait_ge(sem("F_gate"), 2 * b + 1)
                e.wait_ge(sem("F_ch"), 1)
                e.activation(thf[:, b, :], S[:, 2 * b, :], ACT.Tanh, scale=ch[:, b:b + 1]).then_inc(sem("F_th"), 1)
            for b in range(B):
                e.wait_ge(sem("F_hqt"), b + 1)
                e.activation(hqT[:, b, :, :].rearrange("p h t -> p (h t)"),
                             T[:, b, :].bitcast(BF16)[:, 0:HC * P], ACT.Copy).then_inc(sem("F_hqs"), 1)

        @block.vector
        def _(e):
            count = [0]

            def link(ins):
                count[0] += 1
                ins.then_inc(sem("dve_step"), 1)
                e.wait_ge(sem("dve_step"), count[0])

            def norm(n, between=None):
                for b in range(B):
                    last = e.bn_stats(stats[:, b, :], X[:, b, :])
                link(last)
                for b in range(B):
                    last = e.bn_aggr(mv[:, b, :], stats[:, b, :])
                link(last)
                e.tensor_scalar(veps[:, :], mv[:, :, 1], EPS, None, ALU.add).then_inc(sem("veps"), 1)
                if between:
                    between()
                e.wait_ge(sem("rstd"), n + 1)
                for b in range(B):
                    e.tensor_scalar(xn[:, b, :], X[:, b, :], mv[:, b, 0:1], rstd[:, b:b + 1], ALU.subtract,
                                    ALU.mult).then_inc(sem("xn"), 1)
                if n in (5,):
                    return
                e.wait_ge(sem("xn_t"), n + 1)
                e.tensor_copy(xnT[:, :], T[:, 0, 0:B * P]).then_inc(sem("xnT"), 1)

            def softmax(p, ns, scale_by=None):
                def shift(i):
                    g = i % G
                    k = g if ns == 1 else 2 * (g % 2)
                    sc = S[:, k:k + ns, :].rearrange("p s (j k) -> p s j k", j=J)
                    e.wait_ge(sem(p + "scores"), i + 1)
                    if ns == 1:
                        link(e.tensor_reduce(MX[:, i, :], sc[:, 0], AX.X, ALU.max))
                    else:
                        link(e.tensor_reduce(MX[:, i, :], sc.rearrange("p s j k -> p j s k"), AX.XY, ALU.max))
                    if i >= 4:
                        e.wait_ge(sem(p + "transposed"), (i - 3) * ns)
                    m = MX[:, i, :].unsqueeze(1).unsqueeze(3).to_broadcast([P, ns, J, P])
                    e.tensor_tensor(PR[:, i % 4, 0:ns * J, :].rearrange("p (s j) k -> p s j k", s=ns), sc, m,
                                    ALU.subtract).then_inc(sem(p + "shifted"), 1)

                def divide(b):
                    e.wait_ge(sem(p + "pv"), G * (b + 1))
                    link(e.reciprocal(rden[:, :], D[:, :]))
                    out = ON[:, b, :, :].rearrange("p g q -> p (g q)")
                    if scale_by is None:
                        e.tensor_tensor(out, O[:, :], rden[:, :], ALU.mult).then_inc(sem(p + "on"), 1)
                    else:
                        e.scalar_tensor_tensor(out, O[:, :], scale_by[:, b:b + 1], rden[:, :], ALU.mult,
                                               ALU.mult).then_inc(sem(p + "on"), 1)

                for i in range(B * G):
                    shift(i)
                    if i == G + 1:
                        divide(0)
                divide(1)

            def residual(p, half=False):
                for b in range(B):
                    e.wait_ge(sem(p + "out"), b + 1)
                    if half:
                        last = e.scalar_tensor_tensor(X[:, b, :], S[:, b, 0:P], 0.5, X[:, b, :], ALU.mult, ALU.add)
                    else:
                        last = e.tensor_tensor(X[:, b, :], X[:, b, :], S[:, b, 0:P], ALU.add)
                link(last)

            e.wait_ge(sem("x_in"), 16)

            def k_of_A():
                e.wait_ge(sem("const_in"), 16)
                e.wait_ge(sem("A_k"), 1)
                for b in range(B):
                    e.scalar_tensor_tensor(KB[:, b, :, :], S[:, 0, b * P:(b + 1) * P].unsqueeze(1).to_broadcast([P, J, P]),
                                           part(first, FIRST, "bk"), delta.unsqueeze(2).to_broadcast([P, J, P]),
                                           ALU.add, ALU.mult).then_inc(sem("A_kb"), 1)

            norm(0, k_of_A)

            def tile_list():
                e.wait_ge(sem("mask_in"), 16)
                link(e.tensor_scalar(keepm[:, :], mask[:, :], 0.0, None, ALU.not_equal))
                link(e.tensor_reduce(act32[:, :], keepm[:, :], AX.X, ALU.max))
                e.tensor_scalar(actv[:, :], part(const, CONST, "tile")[0:B * NT], act32[:, 0:1], None, ALU.mult).then_inc(sem("act"), 1)
                e.tensor_scalar(actb[:, :], part(const, CONST, "batch")[0:B * NT], act32[:, 0:1], None, ALU.mult).then_inc(sem("act"), 1)
                e.wait_ge(sem("act_t"), 1)
                e.tensor_copy(lstin[:, :, :].rearrange("p b j -> p (b j)"), T[0:1, 1, 0:B * NT])
                e.tensor_copy(cnti[:, :], T[0:1, 1, B * NT:B * NT + B])
                e.tensor_reduce(most[:, :], T[0:1, 1, B * NT:B * NT + B], AX.X, ALU.max)
                link(e.tensor_copy(cnt[:, :], T[:, 1, B * NT:B * NT + B]))
                for b in range(B):
                    link(e.max(lst[:, b, 0:8], lstin[:, b, :]))
                for b in range(B):
                    link(e.match_replace(lsttmp[:, b, :], lst[:, b, 0:8], lstin[:, b, :], 0.0))
                for b in range(B):
                    last = e.max(lst[:, b, 8:16], lsttmp[:, b, :])
                link(last)
                link(e.tensor_scalar(idf[:, :, :], lst[:, :, :], 1.0, 1.0, ALU.max, ALU.subtract))
                e.tensor_copy(ids[:, :, :], idf[:, :, :]).then_inc(sem("list_made"), 1)
                link(e.tensor_scalar(have[:, :, :], lst[:, :, 0:NS], 0.0, None, ALU.is_gt))
                link(e.tensor_scalar(anyk[:, :], cnt[:, :], 1.0, None, ALU.min))
                link(e.reciprocal(ranyk[:, :], anyk[:, :]))
                link(e.tensor_tensor(nanf[:, :], ranyk[:, :], anyk[:, :], ALU.mult))

            e.wait_ge(sem("A_q"), 1)
            e.tensor_scalar(QT[:, :], S[:, 2, 0:B * P], part(first, FIRST, "bq"), SCALE, ALU.add, ALU.mult)\
                .then_inc(sem("A_qt"), 1)
            tile_list()
            softmax("A_", 1)
            residual("A_")

            def keys_of_D():
                e.wait_ge(sem("pool_zero"), 9)
                for b in range(B):
                    for s in range(NS):
                        t = b * NS + s
                        e.wait_ge(sem("maskS_in"), 16 * B * NS)
                        link(e.tensor_scalar(keepS[:, t, :], maskS[:, t, :], 0.0, have[:, b, s:s + 1], ALU.not_equal,
                                             ALU.mult))
                        e.tensor_scalar(biasS[0:1, t, :], keepS[:, t, :], 1.0, -NEG, ALU.subtract, ALU.mult)\
                            .then_inc(sem("D_bias"), 1)
                e.wait_ge(sem("D_k"), 1)
                for t in range(B * NS):
                    e.tensor_tensor(KBx[:, t, :, :], O[:, t * P:(t + 1) * P].unsqueeze(1).to_broadcast([P, J, P]),
                                    delta.unsqueeze(2).to_broadcast([P, J, P]), ALU.mult).then_inc(sem("D_kb"), 1)

            norm(1, keys_of_D)
            cos = part(const, CONST, "cos").unsqueeze(1).to_broadcast([P, B, P])
            sin = part(const, CONST, "sin").unsqueeze(1).to_broadcast([P, B, P])

            def two(t):
                return t.rearrange("p (b t) -> p b t", b=B)

            e.wait_ge(sem("B_k"), 2)
            e.tensor_tensor(two(rope[:, 0, :]), two(S[:, 0, 0:B * P]), cos, ALU.mult)
            link(e.tensor_tensor(two(rope[:, 1, :]), two(S[:, 1, 0:B * P]), sin, ALU.mult))
            link(e.tensor_tensor(KT[:, 0:B * P], rope[:, 0, :], rope[:, 1, :], ALU.add))
            for b in range(B):
                e.tensor_tensor(KB[:, b, :, :], KT[:, b * P:(b + 1) * P].unsqueeze(1).to_broadcast([P, J, P]),
                                delta.unsqueeze(2).to_broadcast([P, J, P]), ALU.mult).then_inc(sem("B_kb"), 1)
            e.wait_ge(sem("B_q"), 2)
            e.scalar_tensor_tensor(two(rope[:, 2, :]), two(S[:, 2, 0:B * P]), SCALE, cos, ALU.mult, ALU.mult)
            link(e.scalar_tensor_tensor(two(rope[:, 3, :]), two(S[:, 3, 0:B * P]), SCALE, sin, ALU.mult, ALU.mult))
            e.tensor_tensor(QT[:, :], rope[:, 2, :], rope[:, 3, :], ALU.add).then_inc(sem("B_qt"), 1)
            softmax("B_", 1)
            residual("B_")

            def decay_vector():
                e.wait_ge(sem("decay_exp"), 1)
                link(e.tensor_scalar(avec[:, 0:2], avec[:, 0:2], 1.0, None, ALU.add))
                e.reciprocal(avec[:, 2:4], avec[:, 0:2]).then_inc(sem("avec"), 1)

            norm(2, decay_vector)
            e.wait_ge(sem("C_logits"), 1)
            L = S[:, 2, 0:B * E].rearrange("p (b e) -> p b e", b=B)
            link(e.tensor_reduce(lmax[:, :], L, AX.X, ALU.max))
            e.tensor_tensor(lg[:, :, :], L, lmax[:, :].unsqueeze(2).to_broadcast([P, B, E]), ALU.subtract)\
                .then_inc(sem("C_lg"), 1)
            e.wait_ge(sem("C_exp"), 1)
            link(e.tensor_reduce(lsum[:, :], lg[:, :, :], AX.X, ALU.add))
            link(e.reciprocal(lmax[:, :], lsum[:, :]))
            link(e.tensor_tensor(prob[:, :, :], lg[:, :, :], lmax[:, :].unsqueeze(2).to_broadcast([P, B, E]), ALU.mult))
            for b in range(B):
                last = e.max(top[:, b, :], prob[:, b, :])
            link(last)
            for b in range(B):
                last = e.max_index(topi[:, b, :], top[:, b, :], prob[:, b, :])
            link(last)
            link(e.tensor_copy(topf[:, :, :], topi[:, :, 0:2]))
            ex = part(const, CONST, "expert")
            for b in range(B):
                last = e.tensor_scalar(oh1[:, b, :], ex, topf[:, b, 0:1], None, ALU.is_equal)
            link(last)
            for b in range(B):
                last = e.scalar_tensor_tensor(oh[:, b, :], ex, topf[:, b, 1:2], oh1[:, b, :], ALU.is_equal, ALU.add)
            link(last)
            e.tensor_copy(ohb[:, :, :], oh[:, :, :]).then_inc(sem("C_oh"), 1)
            link(e.tensor_tensor(gates[:, :, :], oh[:, :, :], prob[:, :, :], ALU.mult))
            e.wait_ge(sem("C_cnt"), 1)
            link(e.tensor_tensor(eq[:, :, :], S[:, 3, 0:B * E].unsqueeze(2).to_broadcast([P, B * E, SLOTS]),
                                 part(const, CONST, "slot").unsqueeze(1).to_broadcast([P, B * E, SLOTS]), ALU.is_equal))
            for t, w, done in ((disp, oh, "C_disp"), (comb, gates, "C_comb")):
                e.tensor_tensor(t[:, :, :], eq[:, :, :],
                                w[:, :, :].rearrange("p b e -> p (b e)").unsqueeze(2).to_broadcast([P, B * E, SLOTS]),
                                ALU.mult).then_inc(sem(done), 1)
            b1 = part(moe, MOE, "b1")
            for i in range(4):
                e.wait_ge(sem("C_hp"), i + 1)
                e.tensor_tensor(hid[:, 2 * i:2 * i + 2, :, :].rearrange("p e h s -> p (e h) s"),
                                S[:, i, :].rearrange("p (q s) -> p q s", q=2 * HC),
                                b1[:, 2 * HC * i:2 * HC * (i + 1)].unsqueeze(2).to_broadcast([P, 2 * HC, B * SLOTS]),
                                ALU.add).then_inc(sem("C_hb"), 1)
            e.wait_ge(sem("C_y"), 1)
            e.tensor_tensor(ysb[:, :, :, :].rearrange("p b h c -> p b (h c)"), O[:, :].rearrange("p (b n) -> p b n", b=B),
                            part(moe, MOE, "b2").unsqueeze(1).to_broadcast([P, B, 2 * P]), ALU.add).then_inc(sem("C_ys"), 1)
            residual("C_")

            def weight_scales():
                e.wait_ge(sem("F_wsum"), 1)
                link(e.tensor_scalar(wmean[:, :], D[:, 0:3], 1.0 / (HC * P * P), EPS, ALU.mult, ALU.max))
                e.reciprocal(wscale[:, :], wmean[:, :]).then_inc(sem("wscale"), 1)

            norm(3, weight_scales)
            e.wait_ge(sem("D_q"), 1)
            e.tensor_scalar(QT[:, :], S[:, 2, 0:B * P], SCALE, None, ALU.mult).then_inc(sem("D_qt"), 1)

            def general(b):
                n = e.value_load(cnti[0:1, b:b + 1], min_val=0, max_val=NT)
                e.memset(gm[:, :], NEG).then_inc(sem(f"g_kvs{b}"), 1)
                e.memset(gV[:, :, DH:DH + 1], 1.0)
                e.memset(gacc[:, :, :], 0.0).then_inc(sem(f"g_acc{b}"), 1)
                e.drain()
                with e.Fori(0, NT) as i:
                    with e.If(n > i):
                        e.wait_ge(sem(f"gmask_in{b}"), i * 16 + 16)
                        e.tensor_scalar(gkeep[:, :], gmask[:, :], 0.0, None, ALU.not_equal)
                        e.drain()
                        e.tensor_scalar(gbias[0:1, :], gkeep[:, :], 1.0, -NEG, ALU.subtract, ALU.mult)
                        e.wait_ge(sem(f"g_kv{b}"), i + 1)
                        e.tensor_tensor(gKB[:, :, :], T[:, 0, 0:P].unsqueeze(1).to_broadcast([P, J, P]),
                                        delta.unsqueeze(2).to_broadcast([P, J, P]), ALU.mult)
                        e.tensor_copy(gV[:, :, 0:DH], T[:, 0, P:2 * P].rearrange("p (h d) -> p h d", d=DH))\
                            .then_inc(sem(f"g_kvs{b}"), 1)
                        e.wait_ge(sem(f"g_scores{b}"), i + 1)
                        sc = S[:, :, :].rearrange("p g (j k) -> p (g j) k", j=J)
                        e.tensor_reduce(gmt[:, :], sc, AX.X, ALU.max)
                        e.drain()
                        e.tensor_tensor(gmn[:, :], gmt[:, :], gm[:, :], ALU.max)
                        e.drain()
                        e.tensor_tensor(gal[:, :], gm[:, :], gmn[:, :], ALU.subtract)
                        e.drain()
                        e.tensor_copy(gm[:, :], gmn[:, :])
                        e.tensor_tensor(PR[:, 0:2, :, :].rearrange("p a j k -> p (a j) k"), sc,
                                        gmn[:, :].unsqueeze(2).to_broadcast([P, H, P]), ALU.subtract)\
                            .then_inc(sem(f"g_shift{b}"), 1)
                        for half in range(2):
                            e.wait_ge(sem(f"g_t{b}"), 2 * i + (half + 1))
                            e.tensor_copy(PT[:, half, :, :].rearrange("p j k -> p (j k)"),
                                          T[:, :, :].rearrange("p a n -> p (a n)")).then_inc(sem(f"g_ts{b}"), 1)
                        e.tensor_tensor(gsc[:, :, :], gacc[:, :, :], gal[:, :].unsqueeze(2).to_broadcast([P, H, DH + 1]),
                                        ALU.mult)
                        e.drain()
                        e.wait_ge(sem(f"g_pv{b}"), i + 1)
                        e.tensor_tensor(gacc[:, :, :], gsc[:, :, :],
                                        S[:, 0, 0:H * (DH + 1)].rearrange("p (h d) -> p h d", h=H), ALU.add)\
                            .then_inc(sem(f"g_acc{b}"), 1)
                        e.drain()
                e.tensor_copy(gpad[:, 0, :, 0:DH], gacc[:, :, 0:DH])
                e.tensor_copy(gpad[:, 1, :, :], gacc[:, :, DH:DH + 1].to_broadcast([P, H, 32]))\
                    .then_inc(sem(f"g_pad{b}"), 1)
                e.wait_ge(sem(f"g_back{b}"), 1)
                e.reciprocal(rden[:, :], D[:, :])
                e.drain()
                e.scalar_tensor_tensor(ON[:, b, :, :].rearrange("p g q -> p (g q)"), O[:, :], nanf[:, b:b + 1],
                                       rden[:, :], ALU.mult, ALU.mult).then_inc(sem(f"g_on{b}"), 1)

            softmax("D_", NS, nanf)
            with e.If(e.value_load(most[0:1, 0:1], min_val=0, max_val=NT) > NS):
                for b in range(B):
                    general(b)
            residual("D_")

            norm(4)
            cw, cb = part(scanw, SCAN, "cw"), part(scanw, SCAN, "cb")
            for ct in range(2):
                e.wait_ge(sem("E_up"), ct + 1)
                link(e.tensor_scalar(conv[:, ct, :, :], upad[:, ct, :, 3:P + 3], cw[:, 4 * ct + 3:4 * ct + 4],
                                     cb[:, ct:ct + 1], ALU.mult, ALU.add))
                for k in range(3):
                    ins = e.scalar_tensor_tensor(conv[:, ct, :, :], upad[:, ct, :, k:k + P],
                                                 cw[:, 4 * ct + k:4 * ct + k + 1], conv[:, ct, :, :], ALU.mult, ALU.add)
                    if k < 2:
                        link(ins)
                    else:
                        ins.then_inc(sem("E_conv"), 1)
            for ct in range(2):
                e.wait_ge(sem("E_th"), ct + 1)
                e.scalar_tensor_tensor(su[:, ct, :], th[:, ct, :], 1.0, conv[:, ct, :, :].rearrange("p b t -> p (b t)"),
                                       ALU.add, ALU.mult).then_inc(sem("E_su"), 1)
            e.wait_ge(sem("decay"), 4)
            for ct in range(2):
                e.wait_ge(sem("E_b"), ct + 1)
                link(e.tensor_scalar(bT[:, ct, :], T[:, ct, 0:B * P], 0.5, part(scanw, SCAN, "bbc")[:, ct:ct + 1],
                                     ALU.mult, ALU.add))
                link(e.tensor_tensor_scan(st[:, ct, :], decay[:, ct, :, :].rearrange("p b t -> p (b t)"), bT[:, ct, :],
                                          0.0, ALU.mult, ALU.add))
            e.wait_ge(sem("E_thg"), 2)
            e.wait_ge(sem("E_cs"), 2)
            link(e.scalar_tensor_tensor(thg[:, :, :], thg[:, :, :], 1.0, cT[:, :, :], ALU.add, ALU.mult))
            e.tensor_tensor(su[:, :, :], thg[:, :, :], st[:, :, :], ALU.mult).then_inc(sem("E_y"), 1)
            residual("E_", half=True)

            norm(5)
            e.wait_ge(sem("xn"), 12)

            def quantise(ins3, src, peak, scale, factor, tmp, out):
                link(e.tensor_scalar(peak, peak, EPS, None, ALU.max))
                link(e.reciprocal(scale, peak))
                e.tensor_scalar(factor, peak, 1.0 / 127.0, None, ALU.mult)
                link(e.tensor_scalar(scale, scale, 127.0, None, ALU.mult))
                for k, (t, s) in enumerate(zip(tmp, src)):
                    last = e.tensor_scalar(t, s, scale[:, k:k + 1], MAGIC, ALU.mult, ALU.add)
                link(last)
                for t in tmp:
                    last = e.tensor_scalar(t, t, MAGIC - 128.0, MAGIC + 127.0, ALU.max, ALU.min)
                link(last)
                for t, o in zip(tmp, out):
                    last = e.tensor_scalar(o, t, MAGIC, None, ALU.subtract)
                return last

            link(e.tensor_reduce(amax[:, :], xn[:, :, :], AX.X, ALU.max, apply_absolute_value=True))
            quantise(None, [xn[:, b, :] for b in range(B)], amax[:, :], sx[:, :], fx[:, :],
                     [qf[:, b, :] for b in range(B)], [xq[:, b, :] for b in range(B)]).then_inc(sem("F_xq"), 1)
            link(e.tensor_scalar(ch[:, :], fx[:, :], wmean[:, 0:1], 0.5, ALU.mult, ALU.mult))
            link(e.tensor_tensor(kk[:, :], ch[:, :], fx[:, :], ALU.mult))
            e.tensor_scalar(kk[:, :], kk[:, :], wmean[:, 1:2], None, ALU.mult).then_inc(sem("F_ch"), 1)
            e.wait_ge(sem("F_xqt"), 1)
            e.tensor_copy(xqT[:, :], T[:, 0, :].bitcast(BF16)[:, 0:B * P]).then_inc(sem("F_xqs"), 1)
            for b in range(B):
                e.wait_ge(sem("F_th"), b + 1)
                e.wait_ge(sem("F_ch"), 1)
                e.wait_ge(sem("F_gate"), 2 * b + 2)
                link(e.scalar_tensor_tensor(hm[:, b, :], thf[:, b, :], 1.0, S[:, 2 * b, :], ALU.add, ALU.mult))
                link(e.scalar_tensor_tensor(hm[:, b, :], hm[:, b, :], kk[:, b:b + 1], S[:, 2 * b + 1, :], ALU.mult,
                                            ALU.mult))
                link(e.tensor_reduce(hmax[:, b:b + 1], hm[:, b, :], AX.X, ALU.max, apply_absolute_value=True))
                quantise(None, [hm[:, b, :]], hmax[:, b:b + 1], sh[:, b:b + 1], kd[:, b:b + 1], [thf[:, b, :]],
                         [hq[:, b, :]]).then_inc(sem("F_hq"), 1)
            link(e.tensor_scalar(kd[:, :], kd[:, :], wmean[:, 2:3], None, ALU.mult))
            for b in range(B):
                e.wait_ge(sem("F_out"), b + 1)
                e.scalar_tensor_tensor(X[:, b, :], (O, D)[b][:, 0:P], kd[:, b:b + 1], X[:, b, :], ALU.mult, ALU.add)\
                    .then_inc(sem("x_out"), 1)

        @block.tensor
        def _(e):
            def mm(out, lhsT, rhs, start=True, stop=True):
                return e.matmul(out, lhsT, rhs, start=start, stop=stop, skip_group_check=True)

            def tile(t, b):
                return t[:, b * P:(b + 1) * P]

            def norm_t(n):
                for b in range(B):
                    e.wait_ge(sem("xn"), 2 * n + b + 1)
                    last = e.transpose(T[:, 0, b * P:(b + 1) * P], xn[:, b, :], ident)
                last.then_inc(sem("xn_t"), 1)
                e.wait_ge(sem("xnT"), n + 1)

            def softmax(p, ns, kb, v, bias):
                def scores(i):
                    b, g = divmod(i, G)
                    if ns == 1:
                        if i >= 4:
                            e.wait_ge(sem(p + "shifted"), i - 3)
                    elif i >= 2:
                        e.wait_ge(sem(p + "shifted"), i - 1)
                    for s in range(ns):
                        k = g if ns == 1 else 2 * (g % 2) + s
                        bias(S[:, k, :].rearrange("p (j k) -> p j k", j=J), b * ns + s)
                        last = mm(S[:, k, :], QT[32 * g:32 * g + 32, b * P:(b + 1) * P],
                                  kb[32 * g:32 * g + 32, b * ns + s, :, :].rearrange("p j k -> p (j k)"), start=False)
                    last.then_inc(sem(p + "scores"), 1)

                def turn(i):
                    e.wait_ge(sem(p + "exp"), i + 1)
                    for s in range(ns):
                        u = i * ns + s
                        if u >= 2:
                            e.wait_ge(sem(p + "pt"), u - 1)
                        for j in range(J):
                            last = e.transpose(T[:, u % 2, j * P:(j + 1) * P], PR[:, i % 4, s * J + j, :], ident)
                        last.then_inc(sem(p + "transposed"), 1)

                def pv(i):
                    b, g = divmod(i, G)
                    e.wait_ge(sem(p + "pt"), (i + 1) * ns)
                    if i == G:
                        e.wait_ge(sem(p + "on"), 1)
                    for s in range(ns):
                        for j in range(J):
                            e.matmul(O[32 * j:32 * j + 32, g * P:(g + 1) * P], v[:, b * ns + s, g * J + j, :],
                                     PT[:, i % 4, s * J + j, :], start=(s == 0), stop=(s == ns - 1),
                                     tile_position=(0, 32 * j), skip_group_check=True)
                    for s in range(ns):
                        for j in range(J):
                            last = e.matmul(D[32 * j:32 * j + 32, g * P:(g + 1) * P], ones[:, 0:32],
                                            PT[:, i % 4, s * J + j, :], start=(s == 0), stop=(s == ns - 1),
                                            tile_position=(0, 32 * j), skip_group_check=True)
                    last.then_inc(sem(p + "pv"), 1)

                ahead = 4 if ns == 1 else 2
                for i in range(ahead):
                    scores(i)
                for i in range(B * G):
                    turn(i)
                    if i + ahead < B * G:
                        scores(i + ahead)
                    if i:
                        pv(i - 1)
                pv(B * G - 1)

            def project(p, wo, brow):
                for b in range(B):
                    e.wait_ge(sem(p + "on"), b + 1)
                    for g in range(G):
                        last = mm(S[:, b, 0:P], ON[:, b, g, :], wo[:, g * P:(g + 1) * P], start=(g == 0),
                                  stop=(g == G - 1 and brow is None))
                    if brow is not None:
                        last = mm(S[:, b, 0:P], ones[0:1, :], brow, start=False)
                    last.then_inc(sem(p + "out"), 1)

            def causal(out, t):
                mm(out, identb, part(constb, CONSTB, "causal").unsqueeze(1).to_broadcast([P, J, P]), stop=False)

            def kept(out, t):
                mm(out, onesb[:, :], biasS[:, t, :].unsqueeze(1).to_broadcast([P, J, P]), stop=False)

            e.wait_ge(sem("first_in"), 16)
            fctx = part(first, FIRST, "ctx")
            mm(S[:, 0, 0:B * P], part(first, FIRST, "wk"), fctx).then_inc(sem("A_k"), 1)
            e.wait_ge(sem("pool_const"), 4)
            e.wait_ge(sem("rows_in"), 16)
            for b in range(B):
                mm(S[:, 1, b * P:(b + 1) * P], tile(fctx, b), part(first, FIRST, "wv"), stop=False)
                mm(S[:, 1, b * P:(b + 1) * P], ones[0:1, :], part(rows, ROWS, "bv"), start=False).then_inc(sem("A_v"), 1)
            e.wait_ge(sem("const_in"), 16)
            norm_t(0)
            mm(S[:, 2, 0:B * P], part(first, FIRST, "wq"), xnT[:, :]).then_inc(sem("A_q"), 1)
            e.wait_ge(sem("act"), 2)
            mm(T[0:1, 1, 0:B * NT], actv[:, :], ident[0:B * NT, 0:B * NT])
            mm(T[:, 1, B * NT:B * NT + B], ones[0:B * NT, :], actb[:, :]).then_inc(sem("act_t"), 1)
            e.wait_ge(sem("constb"), 1)
            e.wait_ge(sem("A_kb"), 2)
            e.wait_ge(sem("A_qt"), 1)
            e.wait_ge(sem("A_va"), 2)
            e.wait_ge(sem("list_made"), 1)
            softmax("A_", 1, KB, VA, causal)
            e.wait_ge(sem("woA_in"), 16)
            project("A_", woA[:, :, :].rearrange("p g c -> p (g c)"), part(rows, ROWS, "bo"))
            e.wait_ge(sem("cross_in"), 16)
            e.wait_ge(sem("ctxS_in"), 16 * B * NS)
            mm(O[:, :], part(cross, CROSS, "wk"), ctxS[:, :, :].rearrange("p s k -> p (s k)")).then_inc(sem("D_k"), 1)
            for t in range(B * NS):
                last = mm(D[:, t * P:(t + 1) * P], ctxS[:, t, :], part(cross, CROSS, "wv"))
            last.then_inc(sem("D_v"), 1)

            norm_t(1)
            e.wait_ge(sem("self_in"), 16)
            for k, w in enumerate(("wk", "wks")):
                mm(S[:, k, 0:B * P], part(selfw, SELF, w), xnT[:, :]).then_inc(sem("B_k"), 1)
            for k, w in enumerate(("wq", "wqs")):
                mm(S[:, 2 + k, 0:B * P], part(selfw, SELF, w), xnT[:, :]).then_inc(sem("B_q"), 1)
            e.wait_ge(sem("D_vx"), B * NS)
            for b in range(B):
                mm(D[:, b * P:(b + 1) * P], tile(xnT, b), part(selfw, SELF, "wv")).then_inc(sem("B_v"), 1)
            e.wait_ge(sem("B_kb"), 2)
            e.wait_ge(sem("B_qt"), 1)
            e.wait_ge(sem("B_vb"), 2)
            e.wait_ge(sem("D_kb"), B * NS)
            softmax("B_", 1, KB, VB, causal)
            project("B_", part(selfw, SELF, "wo"), None)

            norm_t(2)
            e.wait_ge(sem("moe_in"), 16)
            for b in range(B):
                mm(S[:, 2, b * E:(b + 1) * E], tile(xnT, b), part(moe, MOE, "wr"), stop=False)
                last = mm(S[:, 2, b * E:(b + 1) * E], ones[0:1, :], part(rows, ROWS, "br"), start=False)
            last.then_inc(sem("C_logits"), 1)
            e.wait_ge(sem("C_oh"), 1)
            mm(S[:, 3, 0:B * E], part(constb, CONSTB, "before"), ohb[:, :, :].rearrange("p b e -> p (b e)"))\
                .then_inc(sem("C_cnt"), 1)
            e.wait_ge(sem("C_disp"), 1)
            for b in range(B):
                mm(T[:, b, 0:E * SLOTS], xn[:, b, :], disp[:, b * E:(b + 1) * E, :].rearrange("p e s -> p (e s)"))\
                    .then_inc(sem("C_buf"), 1)
            e.wait_ge(sem("C_comb"), 1)
            for b in range(B):
                for h in range(2):
                    q = 2 * b + h
                    last = e.transpose(D[:, q * P:(q + 1) * P],
                                       comb[:, b * E + 4 * h:b * E + 4 * h + 4, :].rearrange("p e s -> p (e s)"), ident)
            last.then_inc(sem("C_ct"), 1)
            e.wait_ge(sem("C_bufs"), 2)
            for i in range(4):
                e.wait_ge(sem(f"w1_in{i}"), 16)
                for k in range(2 * HC):
                    ex, hc = 2 * i + k // HC, k % HC
                    last = mm(S[:, i, k * B * SLOTS:(k + 1) * B * SLOTS], w1[:, ex, hc * P:(hc + 1) * P],
                              buf[:, ex, :, :].rearrange("p b s -> p (b s)"))
                last.then_inc(sem("C_hp"), 1)
            for h in range(2):
                e.wait_ge(sem("C_h"), 2 * h + 2)
                e.wait_ge(sem(f"w2_in{h}"), 16)
                for b in range(B):
                    q = 2 * b + h
                    for hc in range(HC):
                        for j in range(4):
                            ex = 4 * h + j
                            last = e.matmul(O[32 * j:32 * j + 32, q * P:(q + 1) * P],
                                            hid[:, ex, hc, b * SLOTS:(b + 1) * SLOTS], w2[:, ex * HC + hc, :],
                                            start=(hc == 0), stop=(hc == HC - 1), tile_position=(0, 32 * j),
                                            skip_group_check=True)
            last.then_inc(sem("C_y"), 1)
            e.wait_ge(sem("wabs"), 3)
            e.wait_ge(sem("C_cts"), 1)
            mm(D[:, 0:3], ones[:, :], wabs[:, :]).then_inc(sem("F_wsum"), 1)
            e.wait_ge(sem("C_ys"), 1)
            for b in range(B):
                for h in range(2):
                    last = mm(S[:, b, 0:P], combT[:, b, h, :], ysb[:, b, h, :], start=(h == 0), stop=(h == 1))
                last.then_inc(sem("C_out"), 1)

            norm_t(3)
            mm(S[:, 2, 0:B * P], part(cross, CROSS, "wq"), xnT[:, :]).then_inc(sem("D_q"), 1)
            e.wait_ge(sem("D_qt"), 1)
            e.wait_ge(sem("D_bias"), B * NS)

            def general(b):
                n = e.value_load(cnti[0:1, b:b + 1], min_val=0, max_val=NT)
                with e.Fori(0, NT) as i:
                    with e.If(n > i):
                        e.wait_ge(sem(f"gctx_in{b}"), i * 16 + 16)
                        e.wait_ge(sem(f"g_acc{b}"), i + 1)
                        mm(T[:, 0, 0:P], part(cross, CROSS, "wk"), gctx[:, :])
                        mm(T[:, 0, P:2 * P], gctx[:, :], part(cross, CROSS, "wv")).then_inc(sem(f"g_kv{b}"), 1)
                        e.wait_ge(sem(f"g_kvs{b}"), i + 2)
                        for g in range(G):
                            mm(S[:, g, :].rearrange("p (j k) -> p j k", j=J), onesb[:, :],
                               gbias[:, :].unsqueeze(1).to_broadcast([P, J, P]), stop=False)
                            last = mm(S[:, g, :], QT[32 * g:32 * g + 32, b * P:(b + 1) * P],
                                      gKB[32 * g:32 * g + 32, :, :].rearrange("p j k -> p (j k)"), start=False)
                        last.then_inc(sem(f"g_scores{b}"), 1)
                        e.wait_ge(sem(f"g_exp{b}"), i + 1)
                        for half in range(2):
                            if half:
                                e.wait_ge(sem(f"g_ts{b}"), 2 * i + 1)
                            for k in range(8):
                                last = e.transpose(T[:, k // 4, (k % 4) * P:(k % 4 + 1) * P], PR[:, half, k, :], ident)
                            last.then_inc(sem(f"g_t{b}"), 1)
                        e.wait_ge(sem(f"g_ts{b}"), 2 * i + 2)
                        for h in range(H):
                            last = mm(S[:, 0, h * (DH + 1):(h + 1) * (DH + 1)], PT[:, h // 8, h % 8, :], gV[:, h, :])
                        last.then_inc(sem(f"g_pv{b}"), 1)
                e.wait_ge(sem(f"g_pad{b}"), 1)
                for k, bank in enumerate((O, D)):
                    for g in range(G):
                        last = e.transpose(bank[:, g * P:(g + 1) * P],
                                           gpad[:, k, g * J:(g + 1) * J, :].rearrange("p j c -> p (j c)"), ident)
                last.then_inc(sem(f"g_back{b}"), 1)
                e.wait_ge(sem(f"g_on{b}"), 1)

            softmax("D_", NS, KBx, VX, kept)
            with e.If(e.value_load(most[0:1, 0:1], min_val=0, max_val=NT) > NS):
                e.wait_ge(sem("D_on"), B)
                for b in range(B):
                    general(b)
            project("D_", part(cross, CROSS, "wo"), part(rows, ROWS, "bproj"))

            norm_t(4)
            win = part(scanw, SCAN, "win")
            for ct in range(4):
                mm(S[:, ct, 0:B * P], tile(win, ct), xnT[:, :]).then_inc(sem("E_u" if ct < 2 else "E_g"), 1)
            wbc = part(scanw, SCAN, "wbc")
            for ct in range(2):
                e.wait_ge(sem("E_su"), 2)
                for kt in range(2):
                    last = mm(T[:, ct, 0:B * P], wbc[:, kt * 512 + ct * P:kt * 512 + (ct + 1) * P], su[:, kt, :],
                              start=(kt == 0), stop=(kt == 1))
                last.then_inc(sem("E_b"), 1)
            for ct in range(2):
                for kt in range(2):
                    last = mm((O, D)[ct][:, 0:B * P], wbc[:, kt * 512 + (2 + ct) * P:kt * 512 + (3 + ct) * P], su[:, kt, :],
                              start=(kt == 0), stop=(kt == 1))
                last.then_inc(sem("E_c"), 1)
            e.wait_ge(sem("E_y"), 1)
            wout = part(scanw, SCAN, "wout")
            for b in range(B):
                for kt in range(2):
                    mm(S[:, b, 0:P], su[:, kt, b * P:(b + 1) * P], wout[:, kt * P:(kt + 1) * P], start=(kt == 0), stop=False)
                mm(S[:, b, 0:P], twos[0:1, :], part(rows, ROWS, "bout"), start=False).then_inc(sem("E_out"), 1)

            e.wait_ge(sem("F_xq"), 1)
            for b in range(B):
                last = e.transpose(T[:, 0, :].bitcast(BF16)[:, b * P:(b + 1) * P], xq[:, b, :], identb)
            last.then_inc(sem("F_xqt"), 1)
            e.wait_ge(sem("F_xqs"), 1)
            e.wait_ge(sem("w_round"), 9)
            for b in range(B):
                mm(S[:, 2 * b, :], tile(xqT, b), wq3[:, 0, :]).then_inc(sem("F_gate"), 1)
                mm(S[:, 2 * b + 1, :], tile(xqT, b), wq3[:, 1, :]).then_inc(sem("F_gate"), 1)
            for b in range(B):
                e.wait_ge(sem("F_hq"), b + 1)
                for hc in range(HC):
                    last = e.transpose(T[:, b, :].bitcast(BF16)[:, hc * P:(hc + 1) * P], hq[:, b, hc * P:(hc + 1) * P], identb)
                last.then_inc(sem("F_hqt"), 1)
                e.wait_ge(sem("F_hqs"), b + 1)
                for hc in range(HC):
                    last = mm((O, D)[b][:, 0:P], hqT[:, b, hc, :], wq3[:, 2, hc * P:(hc + 1) * P], start=(hc == 0), stop=(hc == HC - 1))
                last.then_inc(sem("F_out"), 1)


def constants():
    c = np.zeros((P, CONST_W), np.float32)

    def put(name, value):
        a, b = CONST[name]
        c[:, a:b] = value

    r = np.arange(P)
    put("ident", np.eye(P))
    put("causal", np.where(r[None, :] > r[:, None], NEG, 0.0))
    put("before", r[:, None] < r[None, :])
    inv = (np.float32(1.0) / np.float32(10000.0) ** (np.arange(0, DH, 2, dtype=np.float32) / np.float32(DH))).astype(np.float32)
    ang = (r.astype(np.float32)[None, :] * inv[(r % DH) % (DH // 2)][:, None]).astype(np.float32)
    put("cos", np.cos(ang))
    put("sin", np.where((r % DH < DH // 2)[:, None], -np.sin(ang), np.sin(ang)))
    put("delta", (r[:, None] // DH % J == np.arange(J)[None, :]))
    put("slot", np.where(np.arange(SLOTS) < CAP, np.arange(SLOTS), -1)[None, :])
    put("tile", (r % NT + 1)[:, None])
    put("batch", (r[:, None] // NT == np.arange(B)[None, :]))
    put("expert", np.arange(E)[None, :])
    return c


def layout(i):
    def pack(table, width, parts, n=P):
        out = np.zeros((n, width), np.float32)
        for name, v in parts.items():
            a, b = table[name]
            out[:, a:b] = v
        return out

    def heads(w):
        out = np.zeros((J, 32, G, P), np.float32)
        out[:, 0:DH] = w.reshape(G, J, DH, P).transpose(1, 2, 0, 3)
        return out.reshape(P, G * P)

    def tiles(w, n):
        return w.reshape(n, P, -1).transpose(1, 0, 2).reshape(P, -1)

    def cols(v, n):
        return v.reshape(n, P).T

    ctxT = np.ascontiguousarray(i["ctx_1024"].transpose(2, 0, 1))
    swap = (np.arange(P) // DH) * DH + (np.arange(P) + DH // 2) % DH
    a = {}
    a["x"] = i["x"]
    a["ctxT"] = ctxT
    a["mask"] = i["mask_BxS2_ik0"]
    a["first"] = pack(FIRST, FIRST_W, dict(
        wq=i["L0_xattn_Wq"].T, wk=i["L0_xattn_Wk"].T, wv=i["L0_xattn_Wv"].T, bq=i["L0_xattn_bq"][:, None],
        bk=i["L0_xattn_bk"][:, None], ctx=ctxT[:, :, 0:P].reshape(P, B * P)))
    a["const"] = constants()
    a["woA"] = heads(i["L0_xattn_Wo"].T).reshape(P, G, P)
    wqT, wkT = i["L0_attn_Wq"].T, i["L0_attn_Wk"].T
    a["selfw"] = pack(SELF, SELF_W, dict(wq=wqT, wqs=wqT[:, swap], wk=wkT, wks=wkT[:, swap], wv=i["L0_attn_Wv"].T,
                                         wo=heads(i["L0_attn_Wo"].T)))
    a["rows"] = pack(ROWS, ROWS_W, dict(bv=i["L0_xattn_bv"], bo=i["L0_xattn_bo"], br=i["L0_ffn_br"],
                                        bproj=i["L1_xattn_bproj"], bout=i["L1_attn_b_out"]), 1)
    b1 = i["L0_ffn_b1"].reshape(E, HC, P).transpose(2, 0, 1).reshape(P, E * HC)
    b2 = np.repeat(i["L0_ffn_b2"].reshape(2, 4, P).transpose(1, 0, 2), 32, axis=0).reshape(P, 2 * P)
    a["moe"] = pack(MOE, MOE_W, dict(wr=i["L0_ffn_Wr"], b1=b1, b2=b2))
    a["w1"] = i["L0_ffn_W1"].transpose(1, 0, 2)
    a["w2"] = i["L0_ffn_W2"].reshape(E * HC, P, P).transpose(1, 0, 2)
    a["cross"] = pack(CROSS, CROSS_W, dict(wq=i["L1_xattn_Wq"], wk=i["L1_xattn_Wkv"][:, 0:P],
                                           wv=i["L1_xattn_Wkv"][:, P:2 * P], wo=heads(i["L1_xattn_Wproj"])))
    a["scanw"] = pack(SCAN, SCAN_W, dict(
        win=i["L1_attn_W_in"], bin=cols(i["L1_attn_b_in"], 4), cw=tiles(i["L1_attn_conv_w"][:, 0, :], 2),
        cb=cols(i["L1_attn_conv_b"], 2), bbc=cols(i["L1_attn_b_bc"], 4), ld=cols(i["L1_attn_log_decay"], 2),
        wout=tiles(i["L1_attn_W_out"], 2), wbc=tiles(i["L1_attn_W_bc"], 2)))
    a["ffn"] = pack(FFN, FFN_W, dict(gate=i["L1_ffn_w_gate"].T, up=i["L1_ffn_w_up"].T,
                                     down=tiles(np.ascontiguousarray(i["L1_ffn_w_down"].T), 4)))
    return {k: np.ascontiguousarray(v) for k, v in a.items()}


def kernel(**inputs):
    import concourse.bacc as bacc
    from concourse.bass_utils import run_bass_kernel_spmd

    nc = bacc.Bacc("TRN2", target_bir_lowering=False, num_devices=1)
    arrays = {f"in_{k}": v for k, v in layout({k: np.asarray(v) for k, v in inputs.items()}).items()}
    d = {k[3:]: nc.dram_tensor(k, v.shape, mybir.dt.from_np(v.dtype), kind="ExternalInput").ap()
         for k, v in arrays.items()}
    d["out"] = nc.dram_tensor("out_0", (B, P, P), F32, kind="ExternalOutput").ap()
    program(nc, d)
    r = run_bass_kernel_spmd(nc, [arrays], core_ids=[0])
    return r.results[0]["out_0"]
```

```python
import concourse.bass as bass
from concourse import mybir
from contextlib import ExitStack
import numpy as np

ALU = mybir.AluOpType
ACT = mybir.ActivationFunctionType
AX = mybir.AxisListType
F32 = mybir.dt.float32
BF16 = mybir.dt.bfloat16
I32 = mybir.dt.int32
U32 = mybir.dt.uint32

P = 128
B = 2
H, DH = 16, 8
G = 4
J = H // G
CTX = 2048
NT = CTX // P
NS = 2
E, SLOTS, CAP = 8, 32, 20
HC = 4
EPS = 1e-5
SCALE = DH ** -0.5
NEG = -1e30
ZEROED = 13
MAGIC = 1.5 * 2 ** 23


def columns(**widths):
    at, out = 0, {}
    for name, w in widths.items():
        out[name] = (at, at + w)
        at += w
    return out, at


FIRST, FIRST_W = columns(wq=P, wk=P, wv=P, bq=1, bk=1, ctx=B * P)
CONST, CONST_W = columns(ident=P, causal=P, before=P, cos=P, sin=P, delta=J, slot=SLOTS, tile=1, batch=B, expert=E, group=G)
CONSTB, CONSTB_W = columns(ident=P, causal=P, before=P)
SELF, SELF_W = columns(wq=P, wqs=P, wk=P, wks=P, wv=P, wo=G * P)
ROWS, ROWS_W = columns(bv=P, bo=P, br=E, bproj=P, bout=P)
MOE, MOE_W = columns(wr=E, b1=E * HC, b2=2 * P)
CROSS, CROSS_W = columns(wq=P, wk=P, wv=P, wo=G * P)
SCAN, SCAN_W = columns(win=4 * P, bin=4, cw=8, cb=2, bbc=4, ld=2, wout=2 * P, wbc=8 * P)
FFN, FFN_W = columns(gate=4 * P, up=4 * P, down=4 * P)


def program(nc, d):
    with ExitStack() as ctx:
        def sb(name, shape, dt=F32):
            return ctx.enter_context(nc.sbuf_tensor(name, shape, dt))

        def ps(name, shape, dt=F32):
            return ctx.enter_context(nc.psum_tensor(name, shape, dt))

        made = {}

        def sem(name):
            if name not in made:
                made[name] = ctx.enter_context(nc.semaphore(name))
            return made[name]

        X = sb("X", [P, B, P])
        first = sb("first", [P, FIRST_W])
        const = sb("const", [P, CONST_W])
        constb = sb("constb", [P, CONSTB_W], BF16)
        selfw = sb("selfw", [P, SELF_W])
        woA = sb("woA", [P, G, P])
        rows = sb("rows", [1, ROWS_W])
        moe = sb("moe", [P, MOE_W])
        w1 = sb("w1", [P, E, HC * P])
        w2 = sb("w2", [P, E * HC, P])
        cross = sb("cross", [P, CROSS_W])
        scanw = sb("scanw", [P, SCAN_W])
        ffn = sb("ffn", [P, FFN_W])
        mask = sb("mask", [B * NT, P], I32)

        def part(t, table, name):
            a, b = table[name]
            return t[:, a:b]

        def tile(t, b):
            return t[:, b * P:(b + 1) * P]

        ident = part(const, CONST, "ident")
        identb = part(constb, CONSTB, "ident")
        delta = part(const, CONST, "delta")
        group = part(const, CONST, "group")

        ones = sb("ones", [P, P])
        twos = sb("twos", [1, P])
        onesb = sb("onesb", [P, P], BF16)
        neghalf = sb("neghalf", [P, B])

        stats = sb("stats", [P, B, 6])
        mv = sb("mv", [P, B, 2])
        veps = sb("veps", [P, B])
        rstd = sb("rstd", [P, B])
        xn = sb("xn", [P, B, P])
        xnT = sb("xnT", [P, B * P])

        QZ = sb("QZ", [P, B, G, P])
        KT = sb("KT", [P, P])
        QT = sb("QT", [P, P])
        rope = sb("rope", [P, 2, 2, P])
        KB = sb("KB", [P, B, J, P])
        KBx = sb("KBx", [P, B * NS, J, P])
        VA = sb("VA", [P, B, H, 32])
        VB = sb("VB", [P, B, H, 32])
        VX = sb("VX", [P, B * NS, H, 32])
        MX = sb("MX", [P, B * G, J])
        PR = sb("PR", [P, 4, NS * J, P])
        PT = sb("PT", [P, 4, NS * J, P])
        OQ = sb("OQ", [P, G * P])
        OD = sb("OD", [P, H, 32])
        rden = sb("rden", [P, H])
        ON = sb("ON", [P, B, G, P])

        keepm = sb("keepm", [B * NT, P])
        act32 = sb("act32", [B * NT, 1])
        actv = sb("actv", [B * NT, 1])
        actb = sb("actb", [B * NT, B])
        lst = sb("lst", [1, B, NT])
        lstin = sb("lstin", [1, B, NT])
        lsttmp = sb("lsttmp", [1, B, NT])
        idf = sb("idf", [1, B, NT])
        ids = sb("ids", [1, B, NT], I32)
        have = sb("have", [1, B, NS])
        cnti = sb("cnti", [1, B], I32)
        most = sb("most", [1, 1], I32)
        cnt = sb("cnt", [P, B])
        anyk = sb("anyk", [P, B])
        ranyk = sb("ranyk", [P, B])
        nanf = sb("nanf", [P, B])
        ctxS = sb("ctxS", [P, B * NS, P])
        maskS = sb("maskS", [1, B * NS, P], I32)
        keepS = sb("keepS", [1, B * NS, P])
        biasS = sb("biasS", [P, B * NS, P], BF16)

        gctx = sb("gctx", [P, P])
        gmask = sb("gmask", [1, P], I32)
        gkeep = sb("gkeep", [1, P])
        gbias = sb("gbias", [P, P], BF16)
        gKB = sb("gKB", [P, J, P])
        gV = sb("gV", [P, H, DH + 1])
        gm = sb("gm", [P, H])
        gmt = sb("gmt", [P, H])
        gmn = sb("gmn", [P, H])
        gal = sb("gal", [P, H])
        gacc = sb("gacc", [P, H, DH + 1])
        gsc = sb("gsc", [P, H, DH + 1])
        gpad = sb("gpad", [P, H, 32])
        grd = sb("grd", [P, H])

        lg = sb("lg", [P, B, E])
        lmax = sb("lmax", [P, B])
        lsum = sb("lsum", [P, B])
        prob = sb("prob", [P, B, E])
        top = sb("top", [P, B, 8])
        topi = sb("topi", [P, B, 8], U32)
        topf = sb("topf", [P, B, 2])
        oh1 = sb("oh1", [P, B, E])
        oh = sb("oh", [P, B, E])
        ohb = sb("ohb", [P, B, E], BF16)
        gates = sb("gates", [P, B, E])
        eq = sb("eq", [P, B * E, SLOTS])
        disp = sb("disp", [P, B * E, SLOTS])
        comb = sb("comb", [P, B * E, SLOTS])
        combT = sb("combT", [P, B, 2, P])
        buf = sb("buf", [P, E, B, SLOTS])
        hid = PR[:, 0:2, :, :].rearrange("p a j k -> p (a j k)").rearrange("p (e h s) -> p e h s", e=E, h=HC)
        ysb = sb("ysb", [P, B, 2, P])

        upad = sb("upad", [P, 2, B, P + 3])
        conv = sb("conv", [P, 2, B, P])
        th = sb("th", [P, 2, B * P])
        su = sb("su", [P, 2, B * P])
        thg = sb("thg", [P, 2, B * P])
        bT = sb("bT", [P, 2, B * P])
        cT = sb("cT", [P, 2, B * P])
        st = sb("st", [P, 2, B * P])
        decay = sb("decay", [P, 2, B, P])
        avec = sb("avec", [P, 4])
        bgh = sb("bgh", [P, 2])

        wabs = sb("wabs", [P, 3])
        wjunk = sb("wjunk", [P, HC * P])
        wmean = sb("wmean", [P, 3])
        wscale = sb("wscale", [P, 3])
        wtmp = sb("wtmp", [P, HC * P])
        wq3 = sb("wq3", [P, 3, HC * P], BF16)
        amax = sb("amax", [P, B])
        sx = sb("sx", [P, B])
        fx = sb("fx", [P, B])
        ch = sb("ch", [P, B])
        kk = sb("kk", [P, B])
        kd = sb("kd", [P, B])
        qf = sb("qf", [P, B, P])
        xq = sb("xq", [P, B, P], BF16)
        xqT = sb("xqT", [P, B * P], BF16)
        thf = PT[:, 0, :, :].rearrange("p j k -> p (j k)").rearrange("p (b n) -> p b n", b=B)
        hm = PT[:, 1, :, :].rearrange("p j k -> p (j k)").rearrange("p (b n) -> p b n", b=B)
        hq = sb("hq", [P, B, HC * P], BF16)
        hqT = sb("hqT", [P, B, HC, P], BF16)
        hmax = sb("hmax", [P, B])
        sh = sb("sh", [P, B])

        S = ps("S", [P, 4, 512])
        T = ps("T", [P, 2, 512])
        O = ps("O", [P, 512])
        D = ps("D", [P, 512])

        block = ctx.enter_context(nc.Block())

        @block.sync
        def _(e):
            e.dma_start(X[:, :, :], d["x"].rearrange("b t c -> t b c")).then_inc(sem("x_in"), 16)
            e.dma_start(first[:, :], d["first"]).then_inc(sem("first_in"), 16)
            e.dma_start(mask[:, :], d["mask"].rearrange("b (j k) -> (b j) k", k=P)).then_inc(sem("mask_in"), 16)
            e.dma_start(rows[:, :], d["rows"]).then_inc(sem("rows_in"), 16)
            e.dma_start(woA[:, :, :], d["woA"]).then_inc(sem("woA_in"), 16)
            e.dma_start(selfw[:, :], d["selfw"]).then_inc(sem("self_in"), 16)
            e.dma_start(cross[:, :], d["cross"]).then_inc(sem("cross_in"), 16)
            e.wait_ge(sem("list_made"), 1)
            for b in range(B):
                for s in range(NS):
                    t = e.value_load(ids[0:1, b, s:s + 1], min_val=0, max_val=NT - 1)
                    e.dma_start(ctxS[:, b * NS + s, :],
                                d["ctxT"][:, b, bass.ds(t * P, P)]).then_inc(sem("ctxS_in"), 16)
                    e.dma_start(maskS[:, b * NS + s, :],
                                d["mask"][b:b + 1, bass.ds(t * P, P)]).then_inc(sem("maskS_in"), 16)
            e.dma_start(moe[:, :], d["moe"]).then_inc(sem("moe_in"), 16)
            for i in range(4):
                e.dma_start(w1[:, 2 * i:2 * i + 2, :], d["w1"][:, 2 * i:2 * i + 2, :]).then_inc(sem(f"w1_in{i}"), 16)
            for i in range(2):
                e.dma_start(w2[:, 16 * i:16 * i + 16, :],
                            d["w2"][:, 16 * i:16 * i + 16, :]).then_inc(sem(f"w2_in{i}"), 16)
            e.dma_start(scanw[:, :], d["scanw"]).then_inc(sem("scan_in"), 16)
            e.dma_start(ffn[:, :], d["ffn"]).then_inc(sem("ffn_in"), 16)
            with e.If(e.value_load(most[0:1, 0:1], min_val=0, max_val=NT) > NS):
                for b in range(B):
                    n = e.value_load(cnti[0:1, b:b + 1], min_val=0, max_val=NT)
                    with e.Fori(0, NT) as i:
                        with e.If(n > i):
                            t = e.value_load(ids[0:1, b, bass.ds(i, 1)], min_val=0, max_val=NT - 1)
                            e.wait_ge(sem(f"g_kvs{b}"), i + 1)
                            e.dma_start(gctx[:, :], d["ctxT"][:, b, bass.ds(t * P, P)]).then_inc(sem(f"gctx_in{b}"), 16)
                            e.dma_start(gmask[:, :], d["mask"][b:b + 1, bass.ds(t * P, P)]).then_inc(sem(f"gmask_in{b}"), 16)
            for b in range(B):
                e.wait_ge(sem("x_out"), b + 1)
                e.dma_start(d["out"][b], X[:, b, :]).then_inc(sem("stored"), 16)
            e.wait_ge(sem("stored"), 32)

        @block.gpsimd
        def _(e):
            e.memset(neghalf[:, :], -0.5).then_inc(sem("pool_const"), 1)
            e.memset(ones[:, :], 1.0).then_inc(sem("pool_const"), 1)
            e.memset(twos[:, :], 2.0).then_inc(sem("pool_const"), 1)
            e.memset(onesb[:, :], 1.0).then_inc(sem("pool_const"), 1)
            for t in (VA, VB, VX, upad, decay, gpad, OD, gV, biasS, gbias):
                n = len(t.shape)
                e.memset(t[tuple([slice(None)] * n)], 0.0).then_inc(sem("pool_zero"), 1)
            e.wait_ge(sem("pool_zero"), 3)
            for t in (VA, VB, VX):
                e.memset(t[:, :, :, DH:DH + 1], 1.0).then_inc(sem("pool_zero"), 1)

            def power(n):
                for b in range(B):
                    e.wait_ge(sem("veps"), B * n + b + 1)
                    e.tensor_tensor(rstd[:, b:b + 1], veps[:, b:b + 1], neghalf[:, 0:1], ALU.pow).then_inc(sem("rstd"), 1)

            e.wait_ge(sem("pool_const"), 4)
            power(0)
            power(1)
            power(2)
            e.wait_ge(sem("scan_in"), 16)
            e.tensor_scalar(bgh[:, :], part(scanw, SCAN, "bin")[:, 2:4], 0.5, None, ALU.mult).then_inc(sem("bgh"), 1)
            e.wait_ge(sem("avec"), 1)
            e.wait_ge(sem("pool_zero"), 5)
            for ct in range(2):
                for b in range(B):
                    e.tensor_copy(decay[:, ct, b, 1:P],
                                  avec[:, 2 + ct:3 + ct].to_broadcast([P, P - 1])).then_inc(sem("decay"), 1)
            power(3)
            e.wait_ge(sem("wscale"), 1)
            for m in range(3):
                w = ffn[:, m * HC * P:(m + 1) * HC * P]
                if m:
                    e.wait_ge(sem("w_round"), 3 * m)
                e.tensor_scalar(wtmp[:, :], w, wscale[:, m:m + 1], MAGIC, ALU.mult, ALU.add).then_inc(sem("w_round"), 1)
                e.wait_ge(sem("w_round"), 3 * m + 1)
                e.tensor_scalar(wtmp[:, :], wtmp[:, :], MAGIC, 1.0, ALU.subtract, ALU.min).then_inc(sem("w_round"), 1)
                e.wait_ge(sem("w_round"), 3 * m + 2)
                e.tensor_scalar(wq3[:, m, :], wtmp[:, :], -1.0, None, ALU.max).then_inc(sem("w_round"), 1)
            power(4)
            power(5)

        @block.scalar
        def _(e):
            e.dma_start(const[:, :], d["const"]).then_inc(sem("const_in"), 16)
            e.wait_ge(sem("const_in"), 16)
            e.activation(constb[:, :], const[:, 0:CONSTB_W], ACT.Copy).then_inc(sem("constb"), 1)

            def softmax(p, ns):
                def exps(i):
                    e.wait_ge(sem(p + "shifted"), i + 1)
                    t = PR[:, i % 4, 0:ns * J, :]
                    e.activation(t, t, ACT.Exp).then_inc(sem(p + "exp"), 1)

                def evac(i):
                    for s in range(ns):
                        u = i * ns + s
                        e.wait_ge(sem(p + "transposed"), u + 1)
                        if i >= 4:
                            e.wait_ge(sem(p + "pv"), i - 3)
                        e.activation(PT[:, i % 4, s * J:(s + 1) * J, :], T[:, u % 2, :].rearrange("p (j k) -> p j k", j=J),
                                     ACT.Copy).then_inc(sem(p + "pt"), 1)

                exps(0)
                for i in range(1, B * G):
                    exps(i)
                    evac(i - 1)
                evac(B * G - 1)

            def xn_transposed(n, b):
                e.wait_ge(sem("xn_t"), B * n + b + 1)
                e.activation(tile(xnT, b), T[:, b, 0:P], ACT.Copy).then_inc(sem("xnT"), 1)

            e.wait_ge(sem("pool_zero"), ZEROED)
            for b in range(B):
                e.wait_ge(sem("A_v"), B)
                e.activation(VA[:, b, :, 0:DH], S[:, 1, b * P:(b + 1) * P].rearrange("p (h d) -> p h d", d=DH),
                             ACT.Copy).then_inc(sem("A_va"), 1)
            for b in range(B):
                xn_transposed(0, b)
            softmax("A_", 1)
            for b in range(B):
                xn_transposed(1, b)
                e.wait_ge(sem("B_v"), b + 1)
                e.activation(VB[:, b, :, 0:DH], T[:, b, P:2 * P].rearrange("p (h d) -> p h d", d=DH),
                             ACT.Copy).then_inc(sem("B_va"), 1)
            softmax("B_", 1)
            for b in range(B):
                xn_transposed(2, b)
            e.wait_ge(sem("C_lg"), 1)
            e.activation(lg[:, :, :], lg[:, :, :], ACT.Exp).then_inc(sem("C_exp"), 1)
            e.wait_ge(sem("D_v"), 1)
            for s in range(B * NS):
                e.activation(VX[:, s, :, 0:DH], D[:, s * P:(s + 1) * P].rearrange("p (h d) -> p h d", d=DH),
                             ACT.Copy).then_inc(sem("D_va"), 1)
            e.wait_ge(sem("scan_in"), 16)
            e.activation(avec[:, 0:2], part(scanw, SCAN, "ld"), ACT.Exp).then_inc(sem("decay_exp"), 1)
            for b in range(B):
                e.wait_ge(sem("C_buf"), b + 1)
                e.activation(buf[:, :, b, :], T[:, b, 0:E * SLOTS].rearrange("p (e s) -> p e s", e=E),
                             ACT.Copy).then_inc(sem("C_bufs"), 1)
            e.wait_ge(sem("C_ct"), 1)
            e.activation(combT[:, :, :, :].rearrange("p b h t -> p (b h t)"), D[:, :], ACT.Copy).then_inc(sem("C_cts"), 1)
            e.wait_ge(sem("ffn_in"), 16)
            for m in range(3):
                if m:
                    e.wait_ge(sem("wabs"), m)
                e.activation(wjunk[:, :], ffn[:, m * HC * P:(m + 1) * HC * P], ACT.Abs,
                             accum_out=wabs[:, m:m + 1]).then_inc(sem("wabs"), 1)
            for i in range(4):
                e.wait_ge(sem("C_hb"), i + 1)
                t = hid[:, 2 * i:2 * i + 2, :, :]
                e.activation(t, t, ACT.Relu).then_inc(sem("C_h"), 1)
            for b in range(B):
                xn_transposed(3, b)
            softmax("D_", NS)
            with e.If(e.value_load(most[0:1, 0:1], min_val=0, max_val=NT) > NS):
                for b in range(B):
                    n = e.value_load(cnti[0:1, b:b + 1], min_val=0, max_val=NT)
                    with e.Fori(0, NT) as i:
                        with e.If(n > i):
                            e.wait_ge(sem(f"g_shift{b}"), i + 1)
                            e.activation(gal[:, :], gal[:, :], ACT.Exp)
                            t = PR[:, 0:2, :, :].rearrange("p a j k -> p (a j k)")
                            e.activation(t, t, ACT.Exp).then_inc(sem(f"g_exp{b}"), 1)
            for b in range(B):
                xn_transposed(4, b)
            for ct in range(2):
                e.wait_ge(sem("E_u"), ct + 1)
                e.activation(upad[:, ct, :, 3:P + 3], S[:, ct, 0:B * P].rearrange("p (b t) -> p b t", b=B),
                             ACT.Identity, bias=part(scanw, SCAN, "bin")[:, ct:ct + 1]).then_inc(sem("E_up"), 1)
            e.wait_ge(sem("bgh"), 1)
            for ct in range(2):
                e.wait_ge(sem("E_g"), ct + 1)
                e.activation(thg[:, ct, :], S[:, 2 + ct, 0:B * P], ACT.Tanh, scale=0.5,
                             bias=bgh[:, ct:ct + 1]).then_inc(sem("E_thg"), 1)
            for ct in range(2):
                e.wait_ge(sem("E_conv"), ct + 1)
                e.activation(th[:, ct, :], conv[:, ct, :, :].rearrange("p b t -> p (b t)"), ACT.Tanh,
                             scale=0.5).then_inc(sem("E_th"), 1)
            for ct in range(2):
                e.wait_ge(sem("E_c"), ct + 1)
                e.activation(cT[:, ct, :], (O, D)[ct][:, 0:B * P], ACT.Identity, scale=0.5,
                             bias=part(scanw, SCAN, "bbc")[:, 2 + ct:3 + ct]).then_inc(sem("E_cs"), 1)
            for b in range(B):
                e.wait_ge(sem("F_gate"), 2 * b + 1)
                e.wait_ge(sem("F_ch"), 1)
                e.activation(thf[:, b, :], S[:, 2 * b, :], ACT.Tanh, scale=ch[:, b:b + 1]).then_inc(sem("F_th"), 1)
            for b in range(B):
                e.wait_ge(sem("F_hqt"), b + 1)
                e.activation(hqT[:, b, :, :].rearrange("p h t -> p (h t)"),
                             T[:, b, :].bitcast(BF16)[:, 0:HC * P], ACT.Copy).then_inc(sem("F_hqs"), 1)

        @block.vector
        def _(e):
            count = [0]

            def link(ins):
                count[0] += 1
                ins.then_inc(sem("dve_step"), 1)
                e.wait_ge(sem("dve_step"), count[0])

            def residual(p, b, half=False):
                e.wait_ge(sem(p + "out"), b + 1)
                if half:
                    link(e.scalar_tensor_tensor(X[:, b, :], S[:, b, 0:P], 0.5, X[:, b, :], ALU.mult, ALU.add))
                else:
                    link(e.tensor_tensor(X[:, b, :], X[:, b, :], S[:, b, 0:P], ALU.add))

            def moments(b):
                link(e.bn_stats(stats[:, b, :], X[:, b, :]))
                link(e.bn_aggr(mv[:, b, :], stats[:, b, :]))
                e.tensor_scalar(veps[:, b:b + 1], mv[:, b, 1:2], EPS, None, ALU.add).then_inc(sem("veps"), 1)

            def normalise(n, b):
                e.wait_ge(sem("rstd"), B * n + b + 1)
                e.tensor_scalar(xn[:, b, :], X[:, b, :], mv[:, b, 0:1], rstd[:, b:b + 1], ALU.subtract,
                                ALU.mult).then_inc(sem("xn"), 1)

            def softmax(p, ns, scale_by=None, between=(), early=None):
                def shift(i):
                    g = i % G
                    k = g if ns == 1 else 2 * (g % 2)
                    sc = S[:, k:k + ns, :].rearrange("p s (j k) -> p s j k", j=J)
                    e.wait_ge(sem(p + "scores"), i + 1)
                    if ns == 1:
                        link(e.tensor_reduce(MX[:, i, :], sc[:, 0], AX.X, ALU.max))
                    else:
                        link(e.tensor_reduce(MX[:, i, :], sc.rearrange("p s j k -> p j s k"), AX.XY, ALU.max))
                    if i >= 4:
                        e.wait_ge(sem(p + "transposed"), (i - 3) * ns)
                    m = MX[:, i, :].unsqueeze(1).unsqueeze(3).to_broadcast([P, ns, J, P])
                    e.tensor_tensor(PR[:, i % 4, 0:ns * J, :].rearrange("p (s j) k -> p s j k", s=ns), sc, m,
                                    ALU.subtract).then_inc(sem(p + "shifted"), 1)

                def divide(b, bank, g0, g1, n):
                    w = (g1 - g0) * P
                    e.wait_ge(sem(p + "pv"), n)
                    q = OQ[:, 0:w].rearrange("p (c d) -> p c d", d=32)
                    h = (g1 - g0) * J
                    link(e.transpose(OQ[:, 0:w], bank[:, 0:w]))
                    link(e.reciprocal(rden[:, 0:h], q[:, :, DH]))
                    r = rden[:, 0:h].unsqueeze(2).to_broadcast([P, h, DH])
                    if scale_by is None:
                        link(e.tensor_tensor(OD[:, 0:h, 0:DH], q[:, :, 0:DH], r, ALU.mult))
                    else:
                        link(e.scalar_tensor_tensor(OD[:, 0:h, 0:DH], q[:, :, 0:DH], scale_by[:, b:b + 1], r, ALU.mult,
                                                    ALU.mult))
                    e.transpose(ON[:, b, g0:g1, :].rearrange("p g q -> p (g q)"),
                                OD[:, 0:h, :].rearrange("p h d -> p (h d)")).then_inc(sem(p + "on"), 1)

                for i in range(B * G):
                    shift(i)
                    if i == 1:
                        for work in between:
                            work()
                    if i == G + 1:
                        divide(0, O, 0, G, G)
                divide(1, D, 0, G - 1, 2 * G - 1)
                if early:
                    early()
                divide(1, O, G - 1, G, 2 * G)

            def first_batch(p, half=False):
                residual(p, 0, half)
                moments(0)

            def second_batch(p, n, half=False, meanwhile=None):
                normalise(n, 0)
                residual(p, 1, half)
                moments(1)
                if meanwhile:
                    meanwhile()
                normalise(n, 1)

            e.wait_ge(sem("x_in"), 16)

            def k_of_A():
                e.wait_ge(sem("const_in"), 16)
                e.wait_ge(sem("A_k"), 1)
                for b in range(B):
                    e.scalar_tensor_tensor(KB[:, b, :, :], S[:, 0, b * P:(b + 1) * P].unsqueeze(1).to_broadcast([P, J, P]),
                                           part(first, FIRST, "bk"), delta.unsqueeze(2).to_broadcast([P, J, P]),
                                           ALU.add, ALU.mult).then_inc(sem("A_kb"), 1)

            for b in range(B):
                moments(b)
            for b in range(B):
                normalise(0, b)
            k_of_A()

            def tile_list():
                e.wait_ge(sem("mask_in"), 16)
                link(e.tensor_scalar(keepm[:, :], mask[:, :], 0.0, None, ALU.not_equal))
                link(e.tensor_reduce(act32[:, :], keepm[:, :], AX.X, ALU.max))
                e.tensor_scalar(actv[:, :], part(const, CONST, "tile")[0:B * NT], act32[:, 0:1], None, ALU.mult).then_inc(sem("act"), 1)
                e.tensor_scalar(actb[:, :], part(const, CONST, "batch")[0:B * NT], act32[:, 0:1], None, ALU.mult).then_inc(sem("act"), 1)
                e.wait_ge(sem("act_t"), 1)
                e.tensor_copy(lstin[:, :, :].rearrange("p b j -> p (b j)"), D[0:1, 0:B * NT])
                e.tensor_copy(cnti[:, :], D[0:1, B * NT:B * NT + B])
                e.tensor_reduce(most[:, :], D[0:1, B * NT:B * NT + B], AX.X, ALU.max)
                link(e.tensor_copy(cnt[:, :], D[:, B * NT:B * NT + B]))
                for b in range(B):
                    link(e.max(lst[:, b, 0:8], lstin[:, b, :]))
                for b in range(B):
                    link(e.match_replace(lsttmp[:, b, :], lst[:, b, 0:8], lstin[:, b, :], 0.0))
                for b in range(B):
                    last = e.max(lst[:, b, 8:16], lsttmp[:, b, :])
                link(last)
                link(e.tensor_scalar(idf[:, :, :], lst[:, :, :], 1.0, 1.0, ALU.max, ALU.subtract))
                e.tensor_copy(ids[:, :, :], idf[:, :, :]).then_inc(sem("list_made"), 1)
                link(e.tensor_scalar(have[:, :, :], lst[:, :, 0:NS], 0.0, None, ALU.is_gt))
                link(e.tensor_scalar(anyk[:, :], cnt[:, :], 1.0, None, ALU.min))
                link(e.reciprocal(ranyk[:, :], anyk[:, :]))
                link(e.tensor_tensor(nanf[:, :], ranyk[:, :], anyk[:, :], ALU.mult))

            def spread(out, b, source, bias=None):
                q = source.unsqueeze(1).to_broadcast([P, G, P])
                m = group.unsqueeze(2).to_broadcast([P, G, P])
                if bias is None:
                    return e.tensor_tensor(out[:, b, :, :], q, m, ALU.mult)
                return e.scalar_tensor_tensor(out[:, b, :, :], q, bias, m, ALU.add, ALU.mult)

            for b in range(B):
                e.wait_ge(sem("A_q"), b + 1)
                spread(QZ, b, T[:, b, P:2 * P], part(first, FIRST, "bq")).then_inc(sem("A_qt"), 1)
            softmax("A_", 1, between=[tile_list], early=lambda: first_batch("A_"))
            second_batch("A_", 1)

            cs = const[:, CONST["cos"][0]:CONST["sin"][1]].rearrange("p (k t) -> p k t", k=2)

            def rotate(b):
                banks = (S[:, 0, :], S[:, 2, :]) if b == 0 else (O, D)
                for k, (bank, name, out) in enumerate(zip(banks, ("B_k", "B_q"), (KT, QT))):
                    e.wait_ge(sem(name), b + 1)
                    link(e.tensor_tensor(rope[:, k, :, :], bank[:, 0:2 * P].rearrange("p (k t) -> p k t", k=2), cs,
                                         ALU.mult))
                    link(e.tensor_tensor(out[:, :], rope[:, k, 0, :], rope[:, k, 1, :], ALU.add))
                    if k == 0:
                        e.tensor_tensor(KB[:, b, :, :], KT[:, :].unsqueeze(1).to_broadcast([P, J, P]),
                                        delta.unsqueeze(2).to_broadcast([P, J, P]), ALU.mult).then_inc(sem("B_kb"), 1)
                    else:
                        spread(QZ, b, QT[:, :]).then_inc(sem("B_qt"), 1)

            rotate(0)
            softmax("B_", 1, between=[lambda: rotate(1)], early=lambda: first_batch("B_"))

            def decay_vector():
                e.wait_ge(sem("decay_exp"), 1)
                link(e.tensor_scalar(avec[:, 0:2], avec[:, 0:2], 1.0, None, ALU.add))
                e.reciprocal(avec[:, 2:4], avec[:, 0:2]).then_inc(sem("avec"), 1)

            def keys_of_D():
                for b in range(B):
                    for s in range(NS):
                        t = b * NS + s
                        e.wait_ge(sem("maskS_in"), 16 * B * NS)
                        link(e.tensor_scalar(keepS[:, t, :], maskS[:, t, :], 0.0, have[:, b, s:s + 1], ALU.not_equal,
                                             ALU.mult))
                        e.tensor_scalar(biasS[0:1, t, :], keepS[:, t, :], 1.0, -NEG, ALU.subtract, ALU.mult)\
                            .then_inc(sem("D_bias"), 1)
                e.wait_ge(sem("D_k"), 1)
                for t in range(B * NS):
                    e.tensor_tensor(KBx[:, t, :, :], O[:, t * P:(t + 1) * P].unsqueeze(1).to_broadcast([P, J, P]),
                                    delta.unsqueeze(2).to_broadcast([P, J, P]), ALU.mult).then_inc(sem("D_kb"), 1)

            second_batch("B_", 2)
            e.wait_ge(sem("C_logits"), 1)
            L = S[:, 2, 0:B * E].rearrange("p (b e) -> p b e", b=B)
            link(e.tensor_reduce(lmax[:, :], L, AX.X, ALU.max))
            e.tensor_tensor(lg[:, :, :], L, lmax[:, :].unsqueeze(2).to_broadcast([P, B, E]), ALU.subtract)\
                .then_inc(sem("C_lg"), 1)
            e.wait_ge(sem("C_exp"), 1)
            link(e.tensor_reduce(lsum[:, :], lg[:, :, :], AX.X, ALU.add))
            link(e.reciprocal(lmax[:, :], lsum[:, :]))
            link(e.tensor_tensor(prob[:, :, :], lg[:, :, :], lmax[:, :].unsqueeze(2).to_broadcast([P, B, E]), ALU.mult))
            for b in range(B):
                last = e.max(top[:, b, :], prob[:, b, :])
            link(last)
            for b in range(B):
                last = e.max_index(topi[:, b, :], top[:, b, :], prob[:, b, :])
            link(last)
            link(e.tensor_copy(topf[:, :, :], topi[:, :, 0:2]))
            ex = part(const, CONST, "expert")
            for b in range(B):
                last = e.tensor_scalar(oh1[:, b, :], ex, topf[:, b, 0:1], None, ALU.is_equal)
            link(last)
            for b in range(B):
                last = e.scalar_tensor_tensor(oh[:, b, :], ex, topf[:, b, 1:2], oh1[:, b, :], ALU.is_equal, ALU.add)
            link(last)
            e.tensor_copy(ohb[:, :, :], oh[:, :, :]).then_inc(sem("C_oh"), 1)
            link(e.tensor_tensor(gates[:, :, :], oh[:, :, :], prob[:, :, :], ALU.mult))
            e.wait_ge(sem("C_cnt"), 1)
            link(e.tensor_tensor(eq[:, :, :], S[:, 3, 0:B * E].unsqueeze(2).to_broadcast([P, B * E, SLOTS]),
                                 part(const, CONST, "slot").unsqueeze(1).to_broadcast([P, B * E, SLOTS]), ALU.is_equal))
            for t, w, done in ((disp, oh, "C_disp"), (comb, gates, "C_comb")):
                e.tensor_tensor(t[:, :, :], eq[:, :, :],
                                w[:, :, :].rearrange("p b e -> p (b e)").unsqueeze(2).to_broadcast([P, B * E, SLOTS]),
                                ALU.mult).then_inc(sem(done), 1)
            keys_of_D()
            decay_vector()
            b1 = part(moe, MOE, "b1")
            for i in range(4):
                e.wait_ge(sem("C_hp"), i + 1)
                e.tensor_tensor(hid[:, 2 * i:2 * i + 2, :, :].rearrange("p e h s -> p (e h) s"),
                                S[:, i, :].rearrange("p (q s) -> p q s", q=2 * HC),
                                b1[:, 2 * HC * i:2 * HC * (i + 1)].unsqueeze(2).to_broadcast([P, 2 * HC, B * SLOTS]),
                                ALU.add).then_inc(sem("C_hb"), 1)
            e.wait_ge(sem("C_y"), 1)
            e.tensor_tensor(ysb[:, :, :, :].rearrange("p b h c -> p b (h c)"), O[:, :].rearrange("p (b n) -> p b n", b=B),
                            part(moe, MOE, "b2").unsqueeze(1).to_broadcast([P, B, 2 * P]), ALU.add).then_inc(sem("C_ys"), 1)
            first_batch("C_")

            def weight_scales():
                e.wait_ge(sem("F_wsum"), 1)
                link(e.tensor_scalar(wmean[:, :], D[:, 0:3], 1.0 / (HC * P * P), EPS, ALU.mult, ALU.max))
                e.reciprocal(wscale[:, :], wmean[:, :]).then_inc(sem("wscale"), 1)

            second_batch("C_", 3, meanwhile=weight_scales)
            for b in range(B):
                e.wait_ge(sem("D_q"), b + 1)
                spread(QZ, b, T[:, b, P:2 * P]).then_inc(sem("D_qt"), 1)

            def general(b):
                n = e.value_load(cnti[0:1, b:b + 1], min_val=0, max_val=NT)
                e.memset(gm[:, :], NEG).then_inc(sem(f"g_kvs{b}"), 1)
                e.memset(gV[:, :, DH:DH + 1], 1.0)
                e.memset(gacc[:, :, :], 0.0).then_inc(sem(f"g_acc{b}"), 1)
                e.drain()
                with e.Fori(0, NT) as i:
                    with e.If(n > i):
                        e.wait_ge(sem(f"gmask_in{b}"), i * 16 + 16)
                        e.tensor_scalar(gkeep[:, :], gmask[:, :], 0.0, None, ALU.not_equal)
                        e.drain()
                        e.tensor_scalar(gbias[0:1, :], gkeep[:, :], 1.0, -NEG, ALU.subtract, ALU.mult)
                        e.wait_ge(sem(f"g_kv{b}"), i + 1)
                        e.tensor_tensor(gKB[:, :, :], T[:, 0, 0:P].unsqueeze(1).to_broadcast([P, J, P]),
                                        delta.unsqueeze(2).to_broadcast([P, J, P]), ALU.mult)
                        e.tensor_copy(gV[:, :, 0:DH], T[:, 0, P:2 * P].rearrange("p (h d) -> p h d", d=DH))\
                            .then_inc(sem(f"g_kvs{b}"), 1)
                        e.wait_ge(sem(f"g_scores{b}"), i + 1)
                        sc = S[:, :, :].rearrange("p g (j k) -> p (g j) k", j=J)
                        e.tensor_reduce(gmt[:, :], sc, AX.X, ALU.max)
                        e.drain()
                        e.tensor_tensor(gmn[:, :], gmt[:, :], gm[:, :], ALU.max)
                        e.drain()
                        e.tensor_tensor(gal[:, :], gm[:, :], gmn[:, :], ALU.subtract)
                        e.drain()
                        e.tensor_copy(gm[:, :], gmn[:, :])
                        e.tensor_tensor(PR[:, 0:2, :, :].rearrange("p a j k -> p (a j) k"), sc,
                                        gmn[:, :].unsqueeze(2).to_broadcast([P, H, P]), ALU.subtract)\
                            .then_inc(sem(f"g_shift{b}"), 1)
                        for half in range(2):
                            e.wait_ge(sem(f"g_t{b}"), 2 * i + (half + 1))
                            e.tensor_copy(PT[:, half, :, :].rearrange("p j k -> p (j k)"),
                                          T[:, :, :].rearrange("p a n -> p (a n)")).then_inc(sem(f"g_ts{b}"), 1)
                        e.tensor_tensor(gsc[:, :, :], gacc[:, :, :], gal[:, :].unsqueeze(2).to_broadcast([P, H, DH + 1]),
                                        ALU.mult)
                        e.drain()
                        e.wait_ge(sem(f"g_pv{b}"), i + 1)
                        e.tensor_tensor(gacc[:, :, :], gsc[:, :, :],
                                        S[:, 0, 0:H * (DH + 1)].rearrange("p (h d) -> p h d", h=H), ALU.add)\
                            .then_inc(sem(f"g_acc{b}"), 1)
                        e.drain()
                e.reciprocal(grd[:, :], gacc[:, :, DH])
                e.drain()
                e.scalar_tensor_tensor(gpad[:, :, 0:DH], gacc[:, :, 0:DH], nanf[:, b:b + 1],
                                       grd[:, :].unsqueeze(2).to_broadcast([P, H, DH]), ALU.mult, ALU.mult)\
                    .then_inc(sem(f"g_pad{b}"), 1)
                e.wait_ge(sem(f"g_back{b}"), 1)
                e.tensor_copy(ON[:, b, :, :].rearrange("p g q -> p (g q)"), O[:, :]).then_inc(sem(f"g_on{b}"), 1)

            softmax("D_", NS, nanf)
            with e.If(e.value_load(most[0:1, 0:1], min_val=0, max_val=NT) > NS):
                for b in range(B):
                    general(b)
            first_batch("D_")
            second_batch("D_", 4)

            cw, cb = part(scanw, SCAN, "cw"), part(scanw, SCAN, "cb")
            for ct in range(2):
                e.wait_ge(sem("E_up"), ct + 1)
                link(e.tensor_scalar(conv[:, ct, :, :], upad[:, ct, :, 3:P + 3], cw[:, 4 * ct + 3:4 * ct + 4],
                                     cb[:, ct:ct + 1], ALU.mult, ALU.add))
                for k in range(3):
                    ins = e.scalar_tensor_tensor(conv[:, ct, :, :], upad[:, ct, :, k:k + P],
                                                 cw[:, 4 * ct + k:4 * ct + k + 1], conv[:, ct, :, :], ALU.mult, ALU.add)
                    if k < 2:
                        link(ins)
                    else:
                        ins.then_inc(sem("E_conv"), 1)
            for ct in range(2):
                e.wait_ge(sem("E_th"), ct + 1)
                e.scalar_tensor_tensor(su[:, ct, :], th[:, ct, :], 1.0, conv[:, ct, :, :].rearrange("p b t -> p (b t)"),
                                       ALU.add, ALU.mult).then_inc(sem("E_su"), 1)
            e.wait_ge(sem("decay"), 4)
            for ct in range(2):
                e.wait_ge(sem("E_b"), ct + 1)
                link(e.tensor_scalar(bT[:, ct, :], T[:, ct, 0:B * P], 0.5, part(scanw, SCAN, "bbc")[:, ct:ct + 1],
                                     ALU.mult, ALU.add))
                link(e.tensor_tensor_scan(st[:, ct, :], decay[:, ct, :, :].rearrange("p b t -> p (b t)"), bT[:, ct, :],
                                          0.0, ALU.mult, ALU.add))
            e.wait_ge(sem("E_thg"), 2)
            e.wait_ge(sem("E_cs"), 2)
            link(e.scalar_tensor_tensor(thg[:, :, :], thg[:, :, :], 1.0, cT[:, :, :], ALU.add, ALU.mult))
            e.tensor_tensor(su[:, :, :], thg[:, :, :], st[:, :, :], ALU.mult).then_inc(sem("E_y"), 1)
            first_batch("E_", half=True)
            second_batch("E_", 5, half=True)

            e.wait_ge(sem("xn"), 12)

            def quantise(ins3, src, peak, scale, factor, tmp, out):
                link(e.tensor_scalar(peak, peak, EPS, None, ALU.max))
                link(e.reciprocal(scale, peak))
                e.tensor_scalar(factor, peak, 1.0 / 127.0, None, ALU.mult)
                link(e.tensor_scalar(scale, scale, 127.0, None, ALU.mult))
                for k, (t, s) in enumerate(zip(tmp, src)):
                    last = e.tensor_scalar(t, s, scale[:, k:k + 1], MAGIC, ALU.mult, ALU.add)
                link(last)
                for t in tmp:
                    last = e.tensor_scalar(t, t, MAGIC - 128.0, MAGIC + 127.0, ALU.max, ALU.min)
                link(last)
                for t, o in zip(tmp, out):
                    last = e.tensor_scalar(o, t, MAGIC, None, ALU.subtract)
                return last

            link(e.tensor_reduce(amax[:, :], xn[:, :, :], AX.X, ALU.max, apply_absolute_value=True))
            quantise(None, [xn[:, b, :] for b in range(B)], amax[:, :], sx[:, :], fx[:, :],
                     [qf[:, b, :] for b in range(B)], [xq[:, b, :] for b in range(B)]).then_inc(sem("F_xq"), 1)
            link(e.tensor_scalar(ch[:, :], fx[:, :], wmean[:, 0:1], 0.5, ALU.mult, ALU.mult))
            link(e.tensor_tensor(kk[:, :], ch[:, :], fx[:, :], ALU.mult))
            e.tensor_scalar(kk[:, :], kk[:, :], wmean[:, 1:2], None, ALU.mult).then_inc(sem("F_ch"), 1)
            e.wait_ge(sem("F_xqt"), 1)
            e.tensor_copy(xqT[:, :], T[:, 0, :].bitcast(BF16)[:, 0:B * P]).then_inc(sem("F_xqs"), 1)
            for b in range(B):
                e.wait_ge(sem("F_th"), b + 1)
                e.wait_ge(sem("F_ch"), 1)
                e.wait_ge(sem("F_gate"), 2 * b + 2)
                link(e.scalar_tensor_tensor(hm[:, b, :], thf[:, b, :], 1.0, S[:, 2 * b, :], ALU.add, ALU.mult))
                link(e.scalar_tensor_tensor(hm[:, b, :], hm[:, b, :], kk[:, b:b + 1], S[:, 2 * b + 1, :], ALU.mult,
                                            ALU.mult))
                link(e.tensor_reduce(hmax[:, b:b + 1], hm[:, b, :], AX.X, ALU.max, apply_absolute_value=True))
                quantise(None, [hm[:, b, :]], hmax[:, b:b + 1], sh[:, b:b + 1], kd[:, b:b + 1], [thf[:, b, :]],
                         [hq[:, b, :]]).then_inc(sem("F_hq"), 1)
            link(e.tensor_scalar(kd[:, :], kd[:, :], wmean[:, 2:3], None, ALU.mult))
            for b in range(B):
                e.wait_ge(sem("F_out"), b + 1)
                e.scalar_tensor_tensor(X[:, b, :], (O, D)[b][:, 0:P], kd[:, b:b + 1], X[:, b, :], ALU.mult, ALU.add)\
                    .then_inc(sem("x_out"), 1)

        @block.tensor
        def _(e):
            def mm(out, lhsT, rhs, start=True, stop=True):
                return e.matmul(out, lhsT, rhs, start=start, stop=stop, skip_group_check=True)

            def norm_t(n, b):
                e.wait_ge(sem("xn"), B * n + b + 1)
                e.transpose(T[:, b, 0:P], xn[:, b, :], ident).then_inc(sem("xn_t"), 1)

            def softmax(p, ns, kb, v, bias, between=None, early=None):
                def scores(i):
                    b, g = divmod(i, G)
                    if g == 0:
                        e.wait_ge(sem(p + "kb"), (b + 1) * ns)
                        e.wait_ge(sem(p + "qt"), b + 1)
                    if ns == 1:
                        if i >= 4:
                            e.wait_ge(sem(p + "shifted"), i - 3)
                    elif i >= 2:
                        e.wait_ge(sem(p + "shifted"), i - 1)
                    for s in range(ns):
                        k = g if ns == 1 else 2 * (g % 2) + s
                        bias(S[:, k, :].rearrange("p (j k) -> p j k", j=J), b * ns + s)
                        last = mm(S[:, k, :], QZ[:, b, g, :], kb[:, b * ns + s, :, :].rearrange("p j k -> p (j k)"),
                                  start=False)
                    last.then_inc(sem(p + "scores"), 1)

                def turn(i):
                    e.wait_ge(sem(p + "exp"), i + 1)
                    if i == 0:
                        e.wait_ge(sem(p + "qt"), B)
                        e.wait_ge(sem(p + "va"), B * ns)
                    for s in range(ns):
                        u = i * ns + s
                        if u >= 2:
                            e.wait_ge(sem(p + "pt"), u - 1)
                        for j in range(J):
                            last = e.transpose(T[:, u % 2, j * P:(j + 1) * P], PR[:, i % 4, s * J + j, :], ident)
                        last.then_inc(sem(p + "transposed"), 1)

                def pv(i):
                    b, g = divmod(i, G)
                    e.wait_ge(sem(p + "pt"), (i + 1) * ns)
                    bank, c = (O, g) if b == 0 else (D, g)
                    if i == G and between:
                        e.wait_ge(sem("list_made"), 1)
                    if i == B * G - 1:
                        e.wait_ge(sem(p + "on"), 1)
                        bank, c = O, 0
                    for s in range(ns):
                        for j in range(J):
                            last = e.matmul(bank[32 * j:32 * j + 32, c * P:(c + 1) * P], v[:, b * ns + s, g * J + j, :],
                                            PT[:, i % 4, s * J + j, :], start=(s == 0), stop=(s == ns - 1),
                                            tile_position=(0, 32 * j), skip_group_check=True)
                    last.then_inc(sem(p + "pv"), 1)

                ahead = 4 if ns == 1 else 2
                for i in range(ahead):
                    scores(i)
                for i in range(B * G):
                    turn(i)
                    if i + ahead < B * G:
                        scores(i + ahead)
                    if i == 1 and between:
                        between()
                    if i:
                        pv(i - 1)
                if early:
                    early()
                pv(B * G - 1)

            def project(p, b, wo, brow):
                if brow is not None:
                    mm(S[:, b, 0:P], ones[0:1, :], brow, stop=False)
                for g in range(G):
                    e.wait_ge(sem(p + "on"), b + 1 if g < G - 1 or b == 0 else 3)
                    last = mm(S[:, b, 0:P], ON[:, b, g, :], wo[:, g * P:(g + 1) * P],
                              start=(g == 0 and brow is None), stop=(g == G - 1))
                last.then_inc(sem(p + "out"), 1)

            def causal(out, t):
                mm(out, identb, part(constb, CONSTB, "causal").unsqueeze(1).to_broadcast([P, J, P]), stop=False)

            def kept(out, t):
                mm(out, onesb[:, :], biasS[:, t, :].unsqueeze(1).to_broadcast([P, J, P]), stop=False)

            e.wait_ge(sem("first_in"), 16)
            fctx = part(first, FIRST, "ctx")
            mm(S[:, 0, 0:B * P], part(first, FIRST, "wk"), fctx).then_inc(sem("A_k"), 1)
            e.wait_ge(sem("pool_const"), 4)
            e.wait_ge(sem("rows_in"), 16)
            for b in range(B):
                mm(S[:, 1, b * P:(b + 1) * P], tile(fctx, b), part(first, FIRST, "wv"), stop=False)
                mm(S[:, 1, b * P:(b + 1) * P], ones[0:1, :], part(rows, ROWS, "bv"), start=False).then_inc(sem("A_v"), 1)
            e.wait_ge(sem("const_in"), 16)
            for b in range(B):
                norm_t(0, b)
            for b in range(B):
                e.wait_ge(sem("xnT"), b + 1)
                mm(T[:, b, P:2 * P], part(first, FIRST, "wq"), tile(xnT, b)).then_inc(sem("A_q"), 1)
            e.wait_ge(sem("constb"), 1)

            def active_tiles():
                e.wait_ge(sem("act"), 2)
                mm(D[0:1, 0:B * NT], actv[:, :], ident[0:B * NT, 0:B * NT])
                mm(D[:, B * NT:B * NT + B], ones[0:B * NT, :], actb[:, :]).then_inc(sem("act_t"), 1)

            def project_A(b):
                e.wait_ge(sem("woA_in"), 16)
                project("A_", b, woA[:, :, :].rearrange("p g c -> p (g c)"), part(rows, ROWS, "bo"))

            e.wait_ge(sem("A_va"), B)
            softmax("A_", 1, KB, VA, causal, between=active_tiles, early=lambda: project_A(0))
            project_A(1)
            e.wait_ge(sem("self_in"), 16)
            for b in range(B):
                norm_t(1, b)
                e.wait_ge(sem("xnT"), B + b + 1)
                banks = (S[:, 0, :], S[:, 2, :]) if b == 0 else (O, D)
                for bank, names, done in zip(banks, (("wk", "wks"), ("wq", "wqs")), ("B_k", "B_q")):
                    for k, w in enumerate(names):
                        last = mm(bank[:, k * P:(k + 1) * P], part(selfw, SELF, w), tile(xnT, b))
                    last.then_inc(sem(done), 1)
                mm(T[:, b, P:2 * P], tile(xnT, b), part(selfw, SELF, "wv")).then_inc(sem("B_v"), 1)

            def project_B(b):
                project("B_", b, part(selfw, SELF, "wo"), None)

            softmax("B_", 1, KB, VB, causal, early=lambda: project_B(0))
            project_B(1)

            e.wait_ge(sem("moe_in"), 16)
            for b in range(B):
                norm_t(2, b)
                e.wait_ge(sem("xnT"), 2 * B + b + 1)
                mm(S[:, 2, b * E:(b + 1) * E], tile(xnT, b), part(moe, MOE, "wr"), stop=False)
                last = mm(S[:, 2, b * E:(b + 1) * E], ones[0:1, :], part(rows, ROWS, "br"), start=False)
            last.then_inc(sem("C_logits"), 1)
            e.wait_ge(sem("cross_in"), 16)
            e.wait_ge(sem("ctxS_in"), 16 * B * NS)
            mm(O[:, :], part(cross, CROSS, "wk"), ctxS[:, :, :].rearrange("p s k -> p (s k)")).then_inc(sem("D_k"), 1)
            for t in range(B * NS):
                last = mm(D[:, t * P:(t + 1) * P], ctxS[:, t, :], part(cross, CROSS, "wv"))
            last.then_inc(sem("D_v"), 1)
            e.wait_ge(sem("C_oh"), 1)
            mm(S[:, 3, 0:B * E], part(constb, CONSTB, "before"), ohb[:, :, :].rearrange("p b e -> p (b e)"))\
                .then_inc(sem("C_cnt"), 1)
            e.wait_ge(sem("C_disp"), 1)
            for b in range(B):
                mm(T[:, b, 0:E * SLOTS], xn[:, b, :], disp[:, b * E:(b + 1) * E, :].rearrange("p e s -> p (e s)"))\
                    .then_inc(sem("C_buf"), 1)
            e.wait_ge(sem("C_comb"), 1)
            e.wait_ge(sem("D_va"), B * NS)
            for b in range(B):
                for h in range(2):
                    q = 2 * b + h
                    last = e.transpose(D[:, q * P:(q + 1) * P],
                                       comb[:, b * E + 4 * h:b * E + 4 * h + 4, :].rearrange("p e s -> p (e s)"), ident)
            last.then_inc(sem("C_ct"), 1)
            e.wait_ge(sem("C_bufs"), 2)
            for i in range(4):
                e.wait_ge(sem(f"w1_in{i}"), 16)
                for k in range(2 * HC):
                    ex, hc = 2 * i + k // HC, k % HC
                    last = mm(S[:, i, k * B * SLOTS:(k + 1) * B * SLOTS], w1[:, ex, hc * P:(hc + 1) * P],
                              buf[:, ex, :, :].rearrange("p b s -> p (b s)"))
                last.then_inc(sem("C_hp"), 1)
            e.wait_ge(sem("D_kb"), B * NS)
            for h in range(2):
                e.wait_ge(sem("C_h"), 2 * h + 2)
                e.wait_ge(sem(f"w2_in{h}"), 16)
                for b in range(B):
                    q = 2 * b + h
                    for hc in range(HC):
                        for j in range(4):
                            ex = 4 * h + j
                            last = e.matmul(O[32 * j:32 * j + 32, q * P:(q + 1) * P],
                                            hid[:, ex, hc, b * SLOTS:(b + 1) * SLOTS], w2[:, ex * HC + hc, :],
                                            start=(hc == 0), stop=(hc == HC - 1), tile_position=(0, 32 * j),
                                            skip_group_check=True)
            last.then_inc(sem("C_y"), 1)
            e.wait_ge(sem("wabs"), 3)
            e.wait_ge(sem("C_cts"), 1)
            mm(D[:, 0:3], ones[:, :], wabs[:, :]).then_inc(sem("F_wsum"), 1)
            e.wait_ge(sem("C_ys"), 1)
            for b in range(B):
                for h in range(2):
                    last = mm(S[:, b, 0:P], combT[:, b, h, :], ysb[:, b, h, :], start=(h == 0), stop=(h == 1))
                last.then_inc(sem("C_out"), 1)

            for b in range(B):
                norm_t(3, b)
            for b in range(B):
                e.wait_ge(sem("xnT"), 3 * B + b + 1)
                mm(T[:, b, P:2 * P], part(cross, CROSS, "wq"), tile(xnT, b)).then_inc(sem("D_q"), 1)
            e.wait_ge(sem("D_bias"), B * NS)

            def general(b):
                n = e.value_load(cnti[0:1, b:b + 1], min_val=0, max_val=NT)
                with e.Fori(0, NT) as i:
                    with e.If(n > i):
                        e.wait_ge(sem(f"gctx_in{b}"), i * 16 + 16)
                        e.wait_ge(sem(f"g_acc{b}"), i + 1)
                        mm(T[:, 0, 0:P], part(cross, CROSS, "wk"), gctx[:, :])
                        mm(T[:, 0, P:2 * P], gctx[:, :], part(cross, CROSS, "wv")).then_inc(sem(f"g_kv{b}"), 1)
                        e.wait_ge(sem(f"g_kvs{b}"), i + 2)
                        for g in range(G):
                            mm(S[:, g, :].rearrange("p (j k) -> p j k", j=J), onesb[:, :],
                               gbias[:, :].unsqueeze(1).to_broadcast([P, J, P]), stop=False)
                            last = mm(S[:, g, :], QZ[:, b, g, :],
                                      gKB[:, :, :].rearrange("p j k -> p (j k)"), start=False)
                        last.then_inc(sem(f"g_scores{b}"), 1)
                        e.wait_ge(sem(f"g_exp{b}"), i + 1)
                        for half in range(2):
                            if half:
                                e.wait_ge(sem(f"g_ts{b}"), 2 * i + 1)
                            for k in range(8):
                                last = e.transpose(T[:, k // 4, (k % 4) * P:(k % 4 + 1) * P], PR[:, half, k, :], ident)
                            last.then_inc(sem(f"g_t{b}"), 1)
                        e.wait_ge(sem(f"g_ts{b}"), 2 * i + 2)
                        for h in range(H):
                            last = mm(S[:, 0, h * (DH + 1):(h + 1) * (DH + 1)], PT[:, h // 8, h % 8, :], gV[:, h, :])
                        last.then_inc(sem(f"g_pv{b}"), 1)
                e.wait_ge(sem(f"g_pad{b}"), 1)
                for g in range(G):
                    last = e.transpose(O[:, g * P:(g + 1) * P],
                                       gpad[:, g * J:(g + 1) * J, :].rearrange("p j c -> p (j c)"), ident)
                last.then_inc(sem(f"g_back{b}"), 1)
                e.wait_ge(sem(f"g_on{b}"), 1)

            softmax("D_", NS, KBx, VX, kept)
            with e.If(e.value_load(most[0:1, 0:1], min_val=0, max_val=NT) > NS):
                e.wait_ge(sem("D_on"), 3)
                for b in range(B):
                    general(b)
            for b in range(B):
                project("D_", b, part(cross, CROSS, "wo"), part(rows, ROWS, "bproj"))

            for b in range(B):
                norm_t(4, b)
            e.wait_ge(sem("xnT"), 5 * B)
            win = part(scanw, SCAN, "win")
            for ct in range(4):
                mm(S[:, ct, 0:B * P], tile(win, ct), xnT[:, :]).then_inc(sem("E_u" if ct < 2 else "E_g"), 1)
            wbc = part(scanw, SCAN, "wbc")
            for ct in range(2):
                e.wait_ge(sem("E_su"), 2)
                for kt in range(2):
                    last = mm(T[:, ct, 0:B * P], wbc[:, kt * 512 + ct * P:kt * 512 + (ct + 1) * P], su[:, kt, :],
                              start=(kt == 0), stop=(kt == 1))
                last.then_inc(sem("E_b"), 1)
            for ct in range(2):
                for kt in range(2):
                    last = mm((O, D)[ct][:, 0:B * P], wbc[:, kt * 512 + (2 + ct) * P:kt * 512 + (3 + ct) * P], su[:, kt, :],
                              start=(kt == 0), stop=(kt == 1))
                last.then_inc(sem("E_c"), 1)
            e.wait_ge(sem("E_y"), 1)
            wout = part(scanw, SCAN, "wout")
            for b in range(B):
                for kt in range(2):
                    mm(S[:, b, 0:P], su[:, kt, b * P:(b + 1) * P], wout[:, kt * P:(kt + 1) * P], start=(kt == 0), stop=False)
                mm(S[:, b, 0:P], twos[0:1, :], part(rows, ROWS, "bout"), start=False).then_inc(sem("E_out"), 1)

            e.wait_ge(sem("F_xq"), 1)
            for b in range(B):
                last = e.transpose(T[:, 0, :].bitcast(BF16)[:, b * P:(b + 1) * P], xq[:, b, :], identb)
            last.then_inc(sem("F_xqt"), 1)
            e.wait_ge(sem("F_xqs"), 1)
            e.wait_ge(sem("w_round"), 9)
            for b in range(B):
                mm(S[:, 2 * b, :], tile(xqT, b), wq3[:, 0, :]).then_inc(sem("F_gate"), 1)
                mm(S[:, 2 * b + 1, :], tile(xqT, b), wq3[:, 1, :]).then_inc(sem("F_gate"), 1)
            for b in range(B):
                e.wait_ge(sem("F_hq"), b + 1)
                for hc in range(HC):
                    last = e.transpose(T[:, b, :].bitcast(BF16)[:, hc * P:(hc + 1) * P], hq[:, b, hc * P:(hc + 1) * P], identb)
                last.then_inc(sem("F_hqt"), 1)
                e.wait_ge(sem("F_hqs"), b + 1)
                for hc in range(HC):
                    last = mm((O, D)[b][:, 0:P], hqT[:, b, hc, :], wq3[:, 2, hc * P:(hc + 1) * P], start=(hc == 0), stop=(hc == HC - 1))
                last.then_inc(sem("F_out"), 1)


def constants():
    c = np.zeros((P, CONST_W), np.float32)

    def put(name, value):
        a, b = CONST[name]
        c[:, a:b] = value

    r = np.arange(P)
    put("ident", np.eye(P))
    put("causal", np.where(r[None, :] > r[:, None], NEG, 0.0))
    put("before", r[:, None] < r[None, :])
    inv = (np.float32(1.0) / np.float32(10000.0) ** (np.arange(0, DH, 2, dtype=np.float32) / np.float32(DH))).astype(np.float32)
    ang = (r.astype(np.float32)[None, :] * inv[(r % DH) % (DH // 2)][:, None]).astype(np.float32)
    put("cos", np.cos(ang))
    put("sin", np.where((r % DH < DH // 2)[:, None], -np.sin(ang), np.sin(ang)))
    put("delta", (r[:, None] // DH % J == np.arange(J)[None, :]))
    put("group", SCALE * (r[:, None] // 32 == np.arange(G)[None, :]))
    put("slot", np.where(np.arange(SLOTS) < CAP, np.arange(SLOTS), -1)[None, :])
    put("tile", (r % NT + 1)[:, None])
    put("batch", (r[:, None] // NT == np.arange(B)[None, :]))
    put("expert", np.arange(E)[None, :])
    return c


def layout(i):
    def pack(table, width, parts, n=P):
        out = np.zeros((n, width), np.float32)
        for name, v in parts.items():
            a, b = table[name]
            out[:, a:b] = v
        return out

    def heads(w):
        out = np.zeros((J, 32, G, P), np.float32)
        out[:, 0:DH] = w.reshape(G, J, DH, P).transpose(1, 2, 0, 3)
        return out.reshape(P, G * P)

    def tiles(w, n):
        return w.reshape(n, P, -1).transpose(1, 0, 2).reshape(P, -1)

    def cols(v, n):
        return v.reshape(n, P).T

    ctxT = np.ascontiguousarray(i["ctx_1024"].transpose(2, 0, 1))
    swap = (np.arange(P) // DH) * DH + (np.arange(P) + DH // 2) % DH
    a = {}
    a["x"] = i["x"]
    a["ctxT"] = ctxT
    a["mask"] = i["mask_BxS2_ik0"]
    a["first"] = pack(FIRST, FIRST_W, dict(
        wq=i["L0_xattn_Wq"].T, wk=i["L0_xattn_Wk"].T, wv=i["L0_xattn_Wv"].T, bq=i["L0_xattn_bq"][:, None],
        bk=i["L0_xattn_bk"][:, None], ctx=ctxT[:, :, 0:P].reshape(P, B * P)))
    a["const"] = constants()
    a["woA"] = heads(i["L0_xattn_Wo"].T).reshape(P, G, P)
    wqT, wkT = i["L0_attn_Wq"].T, i["L0_attn_Wk"].T
    a["selfw"] = pack(SELF, SELF_W, dict(wq=wqT, wqs=wqT[:, swap], wk=wkT, wks=wkT[:, swap], wv=i["L0_attn_Wv"].T,
                                         wo=heads(i["L0_attn_Wo"].T)))
    a["rows"] = pack(ROWS, ROWS_W, dict(bv=i["L0_xattn_bv"], bo=i["L0_xattn_bo"], br=i["L0_ffn_br"],
                                        bproj=i["L1_xattn_bproj"], bout=i["L1_attn_b_out"]), 1)
    b1 = i["L0_ffn_b1"].reshape(E, HC, P).transpose(2, 0, 1).reshape(P, E * HC)
    b2 = np.repeat(i["L0_ffn_b2"].reshape(2, 4, P).transpose(1, 0, 2), 32, axis=0).reshape(P, 2 * P)
    a["moe"] = pack(MOE, MOE_W, dict(wr=i["L0_ffn_Wr"], b1=b1, b2=b2))
    a["w1"] = i["L0_ffn_W1"].transpose(1, 0, 2)
    a["w2"] = i["L0_ffn_W2"].reshape(E * HC, P, P).transpose(1, 0, 2)
    a["cross"] = pack(CROSS, CROSS_W, dict(wq=i["L1_xattn_Wq"], wk=i["L1_xattn_Wkv"][:, 0:P],
                                           wv=i["L1_xattn_Wkv"][:, P:2 * P], wo=heads(i["L1_xattn_Wproj"])))
    a["scanw"] = pack(SCAN, SCAN_W, dict(
        win=i["L1_attn_W_in"], bin=cols(i["L1_attn_b_in"], 4), cw=tiles(i["L1_attn_conv_w"][:, 0, :], 2),
        cb=cols(i["L1_attn_conv_b"], 2), bbc=cols(i["L1_attn_b_bc"], 4), ld=cols(i["L1_attn_log_decay"], 2),
        wout=tiles(i["L1_attn_W_out"], 2), wbc=tiles(i["L1_attn_W_bc"], 2)))
    a["ffn"] = pack(FFN, FFN_W, dict(gate=i["L1_ffn_w_gate"].T, up=i["L1_ffn_w_up"].T,
                                     down=tiles(np.ascontiguousarray(i["L1_ffn_w_down"].T), 4)))
    return {k: np.ascontiguousarray(v) for k, v in a.items()}


def kernel(**inputs):
    import concourse.bacc as bacc
    from concourse.bass_utils import run_bass_kernel_spmd

    nc = bacc.Bacc("TRN2", target_bir_lowering=False, num_devices=1)
    arrays = {f"in_{k}": v for k, v in layout({k: np.asarray(v) for k, v in inputs.items()}).items()}
    d = {k[3:]: nc.dram_tensor(k, v.shape, mybir.dt.from_np(v.dtype), kind="ExternalInput").ap()
         for k, v in arrays.items()}
    d["out"] = nc.dram_tensor("out_0", (B, P, P), F32, kind="ExternalOutput").ap()
    program(nc, d)
    r = run_bass_kernel_spmd(nc, [arrays], core_ids=[0])
    return r.results[0]["out_0"]
```

```python
import concourse.bass as bass
from concourse import mybir
from contextlib import ExitStack
import numpy as np

ALU = mybir.AluOpType
ACT = mybir.ActivationFunctionType
AX = mybir.AxisListType
F32 = mybir.dt.float32
BF16 = mybir.dt.bfloat16
I32 = mybir.dt.int32
U32 = mybir.dt.uint32

P = 128
B = 2
H, DH = 16, 8
G = 4
J = H // G
CTX = 2048
NT = CTX // P
NS = 2
E, SLOTS, CAP = 8, 32, 20
HC = 4
EPS = 1e-5
SCALE = DH ** -0.5
NEG = -1e30
WARM = dict(start=17, A_q=4, A_norm=2, B_norm=5, C_norm=9, D_norm=8, E_conv=4, E_gate=2, E_norm=12, last_turn=5)
ZEROED = 9
MAGIC = 1.5 * 2 ** 23


def columns(**widths):
    at, out = 0, {}
    for name, w in widths.items():
        out[name] = (at, at + w)
        at += w
    return out, at


FIRST, FIRST_W = columns(wq=P, wk=P, wv=P, bq=1, bk=1, ctx=B * P)
CONST, CONST_W = columns(ident=P, causal=P, before=P, cos=P, sin=P, delta=J, slot=SLOTS, tile=1, batch=B, expert=E, group=G)
CONSTB, CONSTB_W = columns(ident=P, causal=P, before=P)
SELF, SELF_W = columns(wq=P, wqs=P, wk=P, wks=P, wv=P, wo=G * P)
ROWS, ROWS_W = columns(bv=P, bo=P, br=E, bproj=P, bout=P, cb=P)
MOE, MOE_W = columns(wr=E, b1=E * HC, b2=2 * P)
CROSS, CROSS_W = columns(wq=P, wk=P, wv=P, wo=G * P)
SCAN, SCAN_W = columns(win=4 * P, bin=4, cw=8, cb=2, bbc=4, ld=2, wout=2 * P, wbc=8 * P)
FFN, FFN_W = columns(gate=4 * P, up=4 * P, down=4 * P)


def program(nc, d):
    with ExitStack() as ctx:
        def sb(name, shape, dt=F32):
            return ctx.enter_context(nc.sbuf_tensor(name, shape, dt))

        def ps(name, shape, dt=F32):
            return ctx.enter_context(nc.psum_tensor(name, shape, dt))

        made = {}

        def sem(name):
            if name not in made:
                made[name] = ctx.enter_context(nc.semaphore(name))
            return made[name]

        X = sb("X", [P, B, P])
        first = sb("first", [P, FIRST_W])
        const = sb("const", [P, CONST_W])
        constb = sb("constb", [P, CONSTB_W], BF16)
        selfw = sb("selfw", [P, SELF_W])
        woA = sb("woA", [P, G, P])
        rows = sb("rows", [1, ROWS_W])
        moe = sb("moe", [P, MOE_W])
        w1 = sb("w1", [P, E, HC * P])
        w2 = sb("w2", [P, E * HC, P])
        cross = sb("cross", [P, CROSS_W])
        scanw = sb("scanw", [P, SCAN_W])
        ffn = sb("ffn", [P, FFN_W])
        mask = sb("mask", [B * NT, P], I32)

        def part(t, table, name):
            a, b = table[name]
            return t[:, a:b]

        def tile(t, b):
            return t[:, b * P:(b + 1) * P]

        ident = part(const, CONST, "ident")
        identb = part(constb, CONSTB, "ident")
        delta = part(const, CONST, "delta")
        group = part(const, CONST, "group")

        ones = sb("ones", [P, P])
        fours = sb("fours", [1, P])
        onesb = sb("onesb", [P, P], BF16)
        neghalf = sb("neghalf", [P, B])

        stats = sb("stats", [P, B, 6])
        mv = sb("mv", [P, B, 2])
        veps = sb("veps", [P, B])
        rstd = sb("rstd", [P, B])
        xn = sb("xn", [P, B, P])
        xnT = sb("xnT", [P, B * P])

        QZ = sb("QZ", [P, B, G, P])
        KT = sb("KT", [P, P])
        QT = sb("QT", [P, B, P])
        bqs = sb("bqs", [P, G])
        rope = sb("rope", [P, 2, 2, P])
        KB = sb("KB", [P, B, J, P])
        KBx = sb("KBx", [P, B * NS, J, P])
        VA = sb("VA", [P, B, H, 32])
        VB = sb("VB", [P, B, H, 32])
        VX = sb("VX", [P, B * NS, H, 32])
        MX = sb("MX", [P, B * G, J])
        PR = sb("PR", [P, 4, NS * J, P])
        PT = sb("PT", [P, 4, NS * J, P])
        SUM = sb("SUM", [P, B * G, J])
        RSUM = sb("RSUM", [P, B * G, J])
        ON = sb("ON", [P, B, G, P])

        keepm = sb("keepm", [B * NT, P])
        act32 = sb("act32", [B * NT, 1])
        actv = sb("actv", [B * NT, 1])
        actb = sb("actb", [B * NT, B])
        lst = sb("lst", [1, B, NT])
        lstin = sb("lstin", [1, B, NT])
        lsttmp = sb("lsttmp", [1, B, NT])
        idf = sb("idf", [1, B, NT])
        ids = sb("ids", [1, B, NT], I32)
        have = sb("have", [1, B, NS])
        cnti = sb("cnti", [1, B], I32)
        most = sb("most", [1, 1], I32)
        cnt = sb("cnt", [P, B])
        anyk = sb("anyk", [P, B])
        ranyk = sb("ranyk", [P, B])
        nanf = sb("nanf", [P, B])
        ctxS = sb("ctxS", [P, B * NS, P])
        maskS = sb("maskS", [1, B * NS, P], I32)
        keepS = sb("keepS", [1, B * NS, P])
        biasS = sb("biasS", [P, B * NS, P], BF16)

        gctx = sb("gctx", [P, P])
        gmask = sb("gmask", [1, P], I32)
        gkeep = sb("gkeep", [1, P])
        gbias = sb("gbias", [P, P], BF16)
        gKB = sb("gKB", [P, J, P])
        gV = sb("gV", [P, H, DH + 1])
        gm = sb("gm", [P, H])
        gmt = sb("gmt", [P, H])
        gmn = sb("gmn", [P, H])
        gal = sb("gal", [P, H])
        gacc = sb("gacc", [P, H, DH + 1])
        gsc = sb("gsc", [P, H, DH + 1])
        gpad = sb("gpad", [P, H, 32])
        grd = sb("grd", [P, H])

        lg = sb("lg", [P, B, E])
        lmax = sb("lmax", [P, B])
        lsum = sb("lsum", [P, B])
        prob = sb("prob", [P, B, E])
        top = sb("top", [P, B, 8])
        topi = sb("topi", [P, B, 8], U32)
        topf = sb("topf", [P, B, 2])
        oh1 = sb("oh1", [P, B, E])
        oh = sb("oh", [P, B, E])
        ohb = sb("ohb", [P, B, E], BF16)
        gates = sb("gates", [P, B, E])
        far = sb("far", [P, B, E])
        place = sb("place", [P, B, E])
        disp = sb("disp", [P, B * E, SLOTS])
        comb = sb("comb", [P, B * E, SLOTS])
        combT = sb("combT", [P, B, 2, P])
        buf = sb("buf", [P, E, B, SLOTS])
        hid = PR[:, 0:2, :, :].rearrange("p a j k -> p (a j k)").rearrange("p (e h s) -> p e h s", e=E, h=HC)
        ysb = sb("ysb", [P, B, 2, P])

        upad = sb("upad", [P, 2, B, P + 3])
        conv = sb("conv", [P, B, P])
        th = sb("th", [P, 2, B * P])
        su = sb("su", [P, 2, B * P])
        gated = sb("gated", [P, 2, B * P])
        thg = sb("thg", [P, 2, B * P])
        bT = sb("bT", [P, 2, B * P])
        st = sb("st", [P, 2, B * P])
        decay = sb("decay", [P, 2, B, P])
        avec = sb("avec", [P, 4])
        taps = sb("taps", [P, 4, P])
        bbc2 = sb("bbc2", [P, 2])
        bgh = sb("bgh", [P, 2])

        wabs = sb("wabs", [P, 3])
        wjunk = sb("wjunk", [P, HC * P])
        wmean = sb("wmean", [P, 3])
        wscale = sb("wscale", [P, 3])
        wtmp = sb("wtmp", [P, HC * P])
        wq3 = sb("wq3", [P, 3, HC * P], BF16)
        amax = sb("amax", [P, B])
        sx = sb("sx", [P, B])
        fx = sb("fx", [P, B])
        ch = sb("ch", [P, B])
        kk = sb("kk", [P, B])
        kd = sb("kd", [P, B])
        qf = sb("qf", [P, B, P])
        xq = sb("xq", [P, B, P], BF16)
        xqT = sb("xqT", [P, B * P], BF16)
        thf = PT[:, 0, :, :].rearrange("p j k -> p (j k)").rearrange("p (b n) -> p b n", b=B)
        hm = PT[:, 1, :, :].rearrange("p j k -> p (j k)").rearrange("p (b n) -> p b n", b=B)
        hq = sb("hq", [P, B, HC * P], BF16)
        hqT = sb("hqT", [P, B, HC, P], BF16)
        hmax = sb("hmax", [P, B])
        sh = sb("sh", [P, B])

        S = ps("S", [P, 4, 512])
        T = ps("T", [P, 2, 512])
        O = ps("O", [P, 512])
        D = ps("D", [P, 512])

        block = ctx.enter_context(nc.Block())

        @block.sync
        def _(e):
            e.dma_start(X[:, :, :], d["x"].rearrange("b t c -> t b c")).then_inc(sem("x_in"), 16)
            e.dma_start(first[:, :], d["first"]).then_inc(sem("first_in"), 16)
            e.dma_start(mask[:, :], d["mask"].rearrange("b (j k) -> (b j) k", k=P)).then_inc(sem("mask_in"), 16)
            e.dma_start(rows[:, :], d["rows"]).then_inc(sem("rows_in"), 16)
            e.dma_start(woA[:, :, :], d["woA"]).then_inc(sem("attn_in"), 16)
            e.dma_start(selfw[:, :], d["selfw"]).then_inc(sem("attn_in"), 16)
            e.dma_start(cross[:, :], d["cross"]).then_inc(sem("attn_in"), 16)
            e.dma_start(moe[:, :], d["moe"]).then_inc(sem("moe_in"), 16)
            for i in range(4):
                e.dma_start(w1[:, 2 * i:2 * i + 2, :], d["w1"][:, 2 * i:2 * i + 2, :]).then_inc(sem(f"w1_in{i}"), 16)
            for i in range(2):
                e.dma_start(w2[:, 16 * i:16 * i + 16, :],
                            d["w2"][:, 16 * i:16 * i + 16, :]).then_inc(sem("w2_in"), 16)
            e.dma_start(scanw[:, :], d["scanw"]).then_inc(sem("late_in"), 16)
            e.dma_start(ffn[:, :], d["ffn"]).then_inc(sem("late_in"), 16)
            e.wait_ge(sem("list_made"), 1)
            for b in range(B):
                for s in range(NS):
                    t = e.value_load(ids[0:1, b, s:s + 1], min_val=0, max_val=NT - 1)
                    e.dma_start(ctxS[:, b * NS + s, :],
                                d["ctxT"][:, b, bass.ds(t * P, P)]).then_inc(sem("ctxS_in"), 16)
                    e.dma_start(maskS[:, b * NS + s, :],
                                d["mask"][b:b + 1, bass.ds(t * P, P)]).then_inc(sem("maskS_in"), 16)
            with e.If(e.value_load(most[0:1, 0:1], min_val=0, max_val=NT) > NS):
                for b in range(B):
                    n = e.value_load(cnti[0:1, b:b + 1], min_val=0, max_val=NT)
                    with e.Fori(0, NT) as i:
                        with e.If(n > i):
                            t = e.value_load(ids[0:1, b, bass.ds(i, 1)], min_val=0, max_val=NT - 1)
                            e.wait_ge(sem(f"g_kvs{b}"), i + 1)
                            e.dma_start(gctx[:, :], d["ctxT"][:, b, bass.ds(t * P, P)]).then_inc(sem(f"gctx_in{b}"), 16)
                            e.dma_start(gmask[:, :], d["mask"][b:b + 1, bass.ds(t * P, P)]).then_inc(sem(f"gmask_in{b}"), 16)
            for b in range(B):
                e.wait_ge(sem("x_out"), b + 1)
                e.dma_start(d["out"][b], X[:, b, :]).then_inc(sem("stored"), 16)
            e.wait_ge(sem("stored"), 32)

        @block.gpsimd
        def _(e):
            e.memset(neghalf[:, :], -0.5).then_inc(sem("pool_const"), 1)
            e.memset(ones[:, :], 1.0).then_inc(sem("pool_const"), 1)
            e.memset(fours[:, :], 4.0).then_inc(sem("pool_const"), 1)
            e.memset(onesb[:, :], 1.0).then_inc(sem("pool_const"), 1)
            for t in (VA, VB, VX, upad, decay, gpad, gV, biasS, gbias):
                n = len(t.shape)
                e.memset(t[tuple([slice(None)] * n)], 0.0).then_inc(sem("pool_zero"), 1)

            def power_both(n):
                e.wait_ge(sem("veps"), B * (n + 1))
                e.tensor_tensor(rstd[:, :], veps[:, :], neghalf[:, :], ALU.pow).then_inc(sem("rstd"), B)

            def power(n):
                for b in range(B):
                    e.wait_ge(sem("veps"), B * n + b + 1)
                    e.tensor_tensor(rstd[:, b:b + 1], veps[:, b:b + 1], neghalf[:, 0:1], ALU.pow).then_inc(sem("rstd"), 1)

            e.wait_ge(sem("pool_const"), 4)
            def softmax(p):
                for i in range(B * G):
                    e.wait_ge(sem(p + "rsum"), i + 1)
                    t = PR[:, i % 4, 0:J, :]
                    e.tensor_tensor(t, t, RSUM[:, i, :].unsqueeze(2).to_broadcast([P, J, P]), ALU.mult)\
                        .then_inc(sem(p + "prob"), 1)

            power(0)
            softmax("A_")
            power(1)
            softmax("B_")
            power(2)
            e.wait_ge(sem("late_in"), 32)
            e.tensor_scalar(bgh[:, :], part(scanw, SCAN, "bin")[:, 2:4], 0.5, None, ALU.mult).then_inc(sem("scan_const"), 1)
            e.tensor_scalar(bbc2[:, :], part(scanw, SCAN, "bbc")[:, 2:4], 2.0, None, ALU.mult).then_inc(sem("scan_const"), 1)
            for k in range(4):
                e.tensor_scalar(taps[:, k, :], ident, part(scanw, SCAN, "cw")[:, 4 + k:5 + k], None, ALU.mult)\
                    .then_inc(sem("scan_const"), 1)
            e.wait_ge(sem("wscale"), 1)
            for m in range(3):
                w = ffn[:, m * HC * P:(m + 1) * HC * P]
                if m:
                    e.wait_ge(sem("w_round"), 3 * m)
                e.tensor_scalar(wtmp[:, :], w, wscale[:, m:m + 1], MAGIC, ALU.mult, ALU.add).then_inc(sem("w_round"), 1)
                e.wait_ge(sem("w_round"), 3 * m + 1)
                e.tensor_scalar(wtmp[:, :], wtmp[:, :], MAGIC, 1.0, ALU.subtract, ALU.min).then_inc(sem("w_round"), 1)
                e.wait_ge(sem("w_round"), 3 * m + 2)
                e.tensor_scalar(wq3[:, m, :], wtmp[:, :], -1.0, None, ALU.max).then_inc(sem("w_round"), 1)
            e.wait_ge(sem("avec"), 1)
            e.wait_ge(sem("pool_zero"), 5)
            for ct in range(2):
                for b in range(B):
                    e.tensor_copy(decay[:, ct, b, 1:P],
                                  avec[:, 2 + ct:3 + ct].to_broadcast([P, P - 1])).then_inc(sem("decay"), 1)
            power(3)
            softmax("D_")
            power_both(4)
            power_both(5)

        @block.scalar
        def _(e):
            e.dma_start(const[:, :], d["const"]).then_inc(sem("const_in"), 16)
            e.wait_ge(sem("const_in"), 16)
            e.activation(constb[:, :], const[:, 0:CONSTB_W], ACT.Copy).then_inc(sem("constb"), 1)

            def queries(p, b, source, bias=None):
                for g in range(G):
                    last = e.activation(QZ[:, b, g, :], source, ACT.Identity, scale=group[:, g:g + 1],
                                        bias=0.0 if bias is None else bias[:, g:g + 1])
                last.then_inc(sem(p + "qt"), 1)

            def softmax(p, ns):
                def exps(i):
                    e.wait_ge(sem(p + "shifted"), i + 1)
                    for j in range(J):
                        t = PR[:, i % 4, 0:ns * J, :].rearrange("p (s j) k -> p j s k", s=ns)[:, j]
                        last = e.activation(t, t, ACT.Exp, accum_out=SUM[:, i, j:j + 1])
                    last.then_inc(sem(p + "exp"), 1)

                def evac(i):
                    for s in range(ns):
                        u = i * ns + s
                        e.wait_ge(sem(p + "transposed"), u + 1)
                        if i >= 4:
                            e.wait_ge(sem(p + "pv"), i - 3)
                        e.activation(PT[:, i % 4, s * J:(s + 1) * J, :], T[:, u % 2, :].rearrange("p (j k) -> p j k", j=J),
                                     ACT.Copy).then_inc(sem(p + "pt"), 1)

                for i in range(B * G):
                    if i > 1 and ns > 1:
                        evac(i - 2)
                    exps(i)
                    if i > 1 and ns == 1:
                        evac(i - 2)
                evac(B * G - 2)
                evac(B * G - 1)

            def xn_transposed(n, b):
                e.wait_ge(sem("xn_t"), B * n + b + 1)
                e.activation(tile(xnT, b), T[:, b, 0:P], ACT.Copy).then_inc(sem("xnT"), 1)

            e.wait_ge(sem("pool_zero"), ZEROED)
            for b in range(B):
                e.wait_ge(sem("A_v"), B)
                e.activation(VA[:, b, :, 0:DH], S[:, 1, b * P:(b + 1) * P].rearrange("p (h d) -> p h d", d=DH),
                             ACT.Copy).then_inc(sem("A_va"), 1)
            for b in range(B):
                xn_transposed(0, b)
            e.wait_ge(sem("bqs"), 1)
            for b in range(B):
                e.wait_ge(sem("A_q"), b + 1)
                queries("A_", b, T[:, b, P:2 * P], bqs)
            softmax("A_", 1)
            for b in range(B):
                xn_transposed(1, b)
                e.wait_ge(sem("B_v"), b + 1)
                e.activation(VB[:, b, :, 0:DH], T[:, b, P:2 * P].rearrange("p (h d) -> p h d", d=DH),
                             ACT.Copy).then_inc(sem("B_va"), 1)

            def queries_B(b):
                e.wait_ge(sem("B_qr"), b + 1)
                queries("B_", b, QT[:, b, :])

            queries_B(0)
            queries_B(1)
            softmax("B_", 1)
            e.wait_ge(sem("late_in"), 32)
            for m in range(3):
                if m:
                    e.wait_ge(sem("wabs"), m)
                e.activation(wjunk[:, :], ffn[:, m * HC * P:(m + 1) * HC * P], ACT.Abs,
                             accum_out=wabs[:, m:m + 1]).then_inc(sem("wabs"), 1)
            for b in range(B):
                xn_transposed(2, b)
            e.wait_ge(sem("C_lg"), 1)
            e.activation(lg[:, :, :], lg[:, :, :], ACT.Exp).then_inc(sem("C_exp"), 1)
            e.wait_ge(sem("D_v"), 1)
            for s in range(B * NS):
                e.activation(VX[:, s, :, 0:DH], D[:, s * P:(s + 1) * P].rearrange("p (h d) -> p h d", d=DH),
                             ACT.Copy).then_inc(sem("D_va"), 1)
            e.wait_ge(sem("late_in"), 32)
            e.activation(avec[:, 0:2], part(scanw, SCAN, "ld"), ACT.Exp).then_inc(sem("decay_exp"), 1)
            for b in range(B):
                e.wait_ge(sem("C_buf"), b + 1)
                e.activation(buf[:, :, b, :], T[:, b, 0:E * SLOTS].rearrange("p (e s) -> p e s", e=E),
                             ACT.Copy).then_inc(sem("C_bufs"), 1)
            e.wait_ge(sem("C_ct"), 1)
            e.activation(combT[:, :, :, :].rearrange("p b h t -> p (b h t)"), D[:, :], ACT.Copy).then_inc(sem("C_cts"), 1)
            for i in range(4):
                e.wait_ge(sem("C_hb"), i + 1)
                t = hid[:, 2 * i:2 * i + 2, :, :]
                e.activation(t, t, ACT.Relu).then_inc(sem("C_h"), 1)
            for b in range(B):
                xn_transposed(3, b)
            for b in range(B):
                e.wait_ge(sem("D_q"), b + 1)
                queries("D_", b, T[:, b, P:2 * P])
            softmax("D_", NS)
            with e.If(e.value_load(most[0:1, 0:1], min_val=0, max_val=NT) > NS):
                for b in range(B):
                    n = e.value_load(cnti[0:1, b:b + 1], min_val=0, max_val=NT)
                    with e.Fori(0, NT) as i:
                        with e.If(n > i):
                            e.wait_ge(sem(f"g_shift{b}"), i + 1)
                            e.activation(gal[:, :], gal[:, :], ACT.Exp)
                            t = PR[:, 0:2, :, :].rearrange("p a j k -> p (a j k)")
                            e.activation(t, t, ACT.Exp).then_inc(sem(f"g_exp{b}"), 1)
            for b in range(B):
                xn_transposed(4, b)
            for k, ct in enumerate((1, 0)):
                e.wait_ge(sem("E_u"), k + 1)
                e.activation(upad[:, ct, :, 3:P + 3], S[:, ct, 0:B * P].rearrange("p (b t) -> p b t", b=B),
                             ACT.Identity, bias=part(scanw, SCAN, "bin")[:, ct:ct + 1]).then_inc(sem("E_up"), 1)
            e.wait_ge(sem("scan_const"), 1)
            for ct in range(2):
                e.wait_ge(sem("E_g"), ct + 1)
                e.activation(thg[:, ct, :], S[:, 2 + ct, 0:B * P], ACT.Tanh, scale=0.5,
                             bias=bgh[:, ct:ct + 1]).then_inc(sem("E_thg"), 1)
            e.wait_ge(sem("E_convp"), 1)
            e.activation(th[:, 1, :], T[:, 0, 0:B * P], ACT.Tanh, scale=0.5).then_inc(sem("E_th"), 1)
            e.wait_ge(sem("E_conv"), 1)
            e.activation(th[:, 0, :], conv[:, :, :].rearrange("p b t -> p (b t)"), ACT.Tanh,
                         scale=0.5).then_inc(sem("E_th"), 1)
            for b in range(B):
                e.wait_ge(sem("F_gate"), 2 * b + 1)
                e.wait_ge(sem("F_ch"), 1)
                e.activation(thf[:, b, :], S[:, 2 * b, :], ACT.Tanh, scale=ch[:, b:b + 1]).then_inc(sem("F_th"), 1)
            e.wait_ge(sem("F_hqt"), 1)
            e.activation(hqT[:, 0, :, :].rearrange("p h t -> p (h t)"),
                         T[:, 0, :].bitcast(BF16)[:, 0:HC * P], ACT.Copy).then_inc(sem("F_hqs"), 1)

        @block.vector
        def _(e):
            count = [0]

            def link(ins):
                count[0] += 1
                ins.then_inc(sem("dve_step"), 1)
                e.wait_ge(sem("dve_step"), count[0])

            def step(ins):
                count[0] += 1
                ins.then_inc(sem("dve_step"), 1)
                return count[0]

            def residual(p, b):
                e.wait_ge(sem(p + "out"), b + 1)
                link(e.tensor_tensor(X[:, b, :], X[:, b, :], S[:, b, 0:P], ALU.add))

            def moments(b):
                link(e.bn_stats(stats[:, b, :], X[:, b, :]))
                link(e.bn_aggr(mv[:, b, :], stats[:, b, :]))
                e.tensor_scalar(veps[:, b:b + 1], mv[:, b, 1:2], EPS, None, ALU.add).then_inc(sem("veps"), 1)

            def normalise(n, b):
                e.wait_ge(sem("rstd"), B * n + b + 1)
                e.tensor_scalar(xn[:, b, :], X[:, b, :], mv[:, b, 0:1], rstd[:, b:b + 1], ALU.subtract,
                                ALU.mult).then_inc(sem("xn"), 1)

            def softmax(p, ns, scale_by=None, early=None):
                def shift(i):
                    g = i % G
                    k = g if ns == 1 else 2 * (g % 2)
                    sc = S[:, k:k + ns, :].rearrange("p s (j k) -> p s j k", j=J)
                    e.wait_ge(sem(p + "scores"), i + 1)
                    if ns == 1:
                        link(e.tensor_reduce(MX[:, i, :], sc[:, 0], AX.X, ALU.max))
                    else:
                        link(e.tensor_reduce(MX[:, i, :], sc.rearrange("p s j k -> p j s k"), AX.XY, ALU.max))
                    if i >= 4:
                        e.wait_ge(sem(p + "transposed"), (i - 3) * ns)
                    m = MX[:, i, :].unsqueeze(1).unsqueeze(3).to_broadcast([P, ns, J, P])
                    e.tensor_tensor(PR[:, i % 4, 0:ns * J, :].rearrange("p (s j) k -> p s j k", s=ns), sc, m,
                                    ALU.subtract).then_inc(sem(p + "shifted"), 1)

                def heads_out(b, bank, g0, g1, n):
                    e.wait_ge(sem(p + "pv"), n)
                    out = ON[:, b, g0:g1, :].rearrange("p g q -> p (g q)")
                    o = bank[:, 0:(g1 - g0) * P]
                    if scale_by is None:
                        e.tensor_copy(out, o).then_inc(sem(p + "on"), 1)
                    else:
                        e.tensor_scalar(out, o, scale_by[:, b:b + 1], None, ALU.mult).then_inc(sem(p + "on"), 1)

                def reciprocals(i):
                    e.wait_ge(sem(p + "exp"), i + 1)
                    e.reciprocal(RSUM[:, i, :], SUM[:, i, :]).then_inc(sem(p + "rsum"), 1)
                    if ns > 1:
                        e.wait_ge(sem(p + "rsum"), i + 1)
                        t = PR[:, i % 4, J:NS * J, :]
                        e.tensor_tensor(t, t, RSUM[:, i, :].unsqueeze(2).to_broadcast([P, J, P]), ALU.mult)\
                            .then_inc(sem(p + "prob2"), 1)

                for i in range(B * G):
                    shift(i)
                    if i:
                        reciprocals(i - 1)
                heads_out(0, O, 0, G, G)
                reciprocals(B * G - 1)
                if early:
                    early()
                heads_out(1, D, 0, G - 1, 2 * G - 1)
                heads_out(1, O, G - 1, G, 2 * G)

            def first_batch(p):
                residual(p, 0)
                moments(0)

            def both_batches(p, n, factor=None):
                e.wait_ge(sem(p + "out"), B)
                if factor is None:
                    link(e.tensor_tensor(X[:, :, :], X[:, :, :], S[:, 0:B, 0:P], ALU.add))
                else:
                    link(e.scalar_tensor_tensor(X[:, :, :], S[:, 0:B, 0:P], factor, X[:, :, :], ALU.mult, ALU.add))
                for b in range(B):
                    last = e.bn_stats(stats[:, b, :], X[:, b, :])
                link(last)
                for b in range(B):
                    last = e.bn_aggr(mv[:, b, :], stats[:, b, :])
                link(last)
                e.tensor_scalar(veps[:, :], mv[:, :, 1], EPS, None, ALU.add).then_inc(sem("veps"), B)
                for b in range(B):
                    normalise(n, b)

            def second_batch(p, n, meanwhile=None):
                normalise(n, 0)
                residual(p, 1)
                moments(1)
                if meanwhile:
                    meanwhile()
                normalise(n, 1)

            e.wait_ge(sem("x_in"), 16)

            e.wait_ge(sem("const_in"), 16)
            e.wait_ge(sem("first_in"), 16)
            e.tensor_scalar(bqs[:, :], group, part(first, FIRST, "bq"), None, ALU.mult).then_inc(sem("bqs"), 1)

            def k_of_A():
                e.wait_ge(sem("const_in"), 16)
                e.wait_ge(sem("A_k"), 1)
                for b in range(B):
                    e.scalar_tensor_tensor(KB[:, b, :, :], O[:, b * P:(b + 1) * P].unsqueeze(1).to_broadcast([P, J, P]),
                                           part(first, FIRST, "bk"), delta.unsqueeze(2).to_broadcast([P, J, P]),
                                           ALU.add, ALU.mult).then_inc(sem("A_kb"), 1)

            def kept_tiles():
                e.wait_ge(sem("mask_in"), 16)
                link(e.tensor_scalar(keepm[:, :], mask[:, :], 0.0, None, ALU.not_equal))
                link(e.tensor_reduce(act32[:, :], keepm[:, :], AX.X, ALU.max))
                e.tensor_scalar(actv[:, :], part(const, CONST, "tile")[0:B * NT], act32[:, 0:1], None, ALU.mult).then_inc(sem("act"), 1)
                e.tensor_scalar(actb[:, :], part(const, CONST, "batch")[0:B * NT], act32[:, 0:1], None, ALU.mult).then_inc(sem("act"), 1)
            def tile_list():
                e.wait_ge(sem("act_t"), 1)
                e.tensor_copy(lstin[:, :, :].rearrange("p b j -> p (b j)"), D[0:1, 0:B * NT])
                e.tensor_copy(cnti[:, :], D[0:1, B * NT:B * NT + B])
                e.tensor_reduce(most[:, :], D[0:1, B * NT:B * NT + B], AX.X, ALU.max)
                link(e.tensor_copy(cnt[:, :], D[:, B * NT:B * NT + B]))
                for b in range(B):
                    link(e.max(lst[:, b, 0:8], lstin[:, b, :]))
                for b in range(B):
                    link(e.match_replace(lsttmp[:, b, :], lst[:, b, 0:8], lstin[:, b, :], 0.0))
                for b in range(B):
                    last = e.max(lst[:, b, 8:16], lsttmp[:, b, :])
                link(last)
                link(e.tensor_scalar(idf[:, :, :], lst[:, :, :], 1.0, 1.0, ALU.max, ALU.subtract))
                e.tensor_copy(ids[:, :, :], idf[:, :, :]).then_inc(sem("list_made"), 1)
                link(e.tensor_scalar(have[:, :, :], lst[:, :, 0:NS], 0.0, None, ALU.is_gt))
                link(e.tensor_scalar(anyk[:, :], cnt[:, :], 1.0, None, ALU.min))
                link(e.reciprocal(ranyk[:, :], anyk[:, :]))
                link(e.tensor_tensor(nanf[:, :], ranyk[:, :], anyk[:, :], ALU.mult))

            for b in range(B):
                moments(b)
            kept_tiles()
            for b in range(B):
                normalise(0, b)
            k_of_A()

            tile_list()
            softmax("A_", 1, early=lambda: first_batch("A_"))
            second_batch("A_", 1)

            cs = const[:, CONST["cos"][0]:CONST["sin"][1]].rearrange("p (k t) -> p k t", k=2)

            def rotate(b):
                banks = (S[:, 0, :], S[:, 2, :]) if b == 0 else (O, D)
                for k, (bank, name, out) in enumerate(zip(banks, ("B_k", "B_q"), (KT[:, :], QT[:, b, :]))):
                    e.wait_ge(sem(name), b + 1)
                    link(e.tensor_tensor(rope[:, k, :, :], bank[:, 0:2 * P].rearrange("p (k t) -> p k t", k=2), cs,
                                         ALU.mult))
                    last = e.tensor_tensor(out, rope[:, k, 0, :], rope[:, k, 1, :], ALU.add)
                    if k == 0:
                        link(last)
                        e.tensor_tensor(KB[:, b, :, :], KT[:, :].unsqueeze(1).to_broadcast([P, J, P]),
                                        delta.unsqueeze(2).to_broadcast([P, J, P]), ALU.mult).then_inc(sem("B_kb"), 1)
                    else:
                        last.then_inc(sem("B_qr"), 1)

            rotate(0)
            rotate(1)
            softmax("B_", 1, early=lambda: first_batch("B_"))

            def decay_vector():
                e.wait_ge(sem("decay_exp"), 1)
                link(e.tensor_scalar(avec[:, 0:2], avec[:, 0:2], 1.0, None, ALU.add))
                e.reciprocal(avec[:, 2:4], avec[:, 0:2]).then_inc(sem("avec"), 1)

            def keys_of_D():
                for b in range(B):
                    for s in range(NS):
                        t = b * NS + s
                        e.wait_ge(sem("maskS_in"), 16 * B * NS)
                        link(e.tensor_scalar(keepS[:, t, :], maskS[:, t, :], 0.0, have[:, b, s:s + 1], ALU.not_equal,
                                             ALU.mult))
                        e.tensor_scalar(biasS[0:1, t, :], keepS[:, t, :], 1.0, -NEG, ALU.subtract, ALU.mult)\
                            .then_inc(sem("D_bias"), 1)
                e.wait_ge(sem("D_k"), 1)
                for t in range(B * NS):
                    e.tensor_tensor(KBx[:, t, :, :], O[:, t * P:(t + 1) * P].unsqueeze(1).to_broadcast([P, J, P]),
                                    delta.unsqueeze(2).to_broadcast([P, J, P]), ALU.mult).then_inc(sem("D_kb"), 1)

            def weight_scales():
                e.wait_ge(sem("F_wsum"), 1)
                link(e.tensor_scalar(wmean[:, :], O[:, 0:3], 1.0 / (HC * P * P), EPS, ALU.mult, ALU.max))
                e.reciprocal(wscale[:, :], wmean[:, :]).then_inc(sem("wscale"), 1)

            second_batch("B_", 2, meanwhile=weight_scales)
            e.wait_ge(sem("C_logits"), 1)
            L = S[:, 2, 0:B * E].rearrange("p (b e) -> p b e", b=B)
            link(e.tensor_reduce(lmax[:, :], L, AX.X, ALU.max))
            e.tensor_tensor(lg[:, :, :], L, lmax[:, :].unsqueeze(2).to_broadcast([P, B, E]), ALU.subtract)\
                .then_inc(sem("C_lg"), 1)
            e.wait_ge(sem("C_exp"), 1)
            for b in range(B):
                last = e.max(top[:, b, :], lg[:, b, :])
            link(last)
            for b in range(B):
                last = e.max_index(topi[:, b, :], top[:, b, :], lg[:, b, :])
            link(last)
            e.tensor_copy(topf[:, :, :], topi[:, :, 0:2])
            link(e.tensor_reduce(lsum[:, :], lg[:, :, :], AX.X, ALU.add))
            ex = part(const, CONST, "expert")
            for b in range(B):
                e.tensor_scalar(oh1[:, b, :], ex, topf[:, b, 0:1], None, ALU.is_equal)
            link(e.reciprocal(lmax[:, :], lsum[:, :]))
            for b in range(B):
                e.scalar_tensor_tensor(ohb[:, b, :], ex, topf[:, b, 1:2], oh1[:, b, :], ALU.is_equal, ALU.add)\
                    .then_inc(sem("C_oh"), 1)
            e.tensor_tensor(prob[:, :, :], lg[:, :, :], lmax[:, :].unsqueeze(2).to_broadcast([P, B, E]), ALU.mult)
            for b in range(B):
                last = e.scalar_tensor_tensor(oh[:, b, :], ex, topf[:, b, 1:2], oh1[:, b, :], ALU.is_equal, ALU.add)
            link(last)
            e.tensor_scalar(far[:, :, :], oh[:, :, :], 1.0, -2.0 * P, ALU.subtract, ALU.mult)
            link(e.tensor_tensor(gates[:, :, :], oh[:, :, :], prob[:, :, :], ALU.mult))
            e.wait_ge(sem("C_cnt"), 1)
            link(e.tensor_tensor(place[:, :, :], S[:, 3, 0:B * E].rearrange("p (b e) -> p b e", b=B), far[:, :, :], ALU.add))

            def over_slots(t, b):
                return t[:, b, :].unsqueeze(2).to_broadcast([P, E, SLOTS])

            for b in range(B):
                e.tensor_tensor(disp[:, b * E:(b + 1) * E, :], over_slots(place, b),
                                part(const, CONST, "slot").unsqueeze(1).to_broadcast([P, E, SLOTS]), ALU.is_equal)\
                    .then_inc(sem("C_disp"), 1)
            e.wait_ge(sem("C_disp"), B)
            for b in range(B):
                e.tensor_tensor(comb[:, b * E:(b + 1) * E, :], disp[:, b * E:(b + 1) * E, :], over_slots(gates, b), ALU.mult)\
                    .then_inc(sem("C_comb"), 1)
            keys_of_D()
            decay_vector()
            b1 = part(moe, MOE, "b1")
            for i in range(4):
                e.wait_ge(sem("C_hp"), i + 1)
                e.tensor_tensor(hid[:, 2 * i:2 * i + 2, :, :].rearrange("p e h s -> p (e h) s"),
                                S[:, i, :].rearrange("p (q s) -> p q s", q=2 * HC),
                                b1[:, 2 * HC * i:2 * HC * (i + 1)].unsqueeze(2).to_broadcast([P, 2 * HC, B * SLOTS]),
                                ALU.add).then_inc(sem("C_hb"), 1)
            for b in range(B):
                e.wait_ge(sem("C_y"), b + 1)
                e.tensor_tensor(ysb[:, b, :, :].rearrange("p h c -> p (h c)"), (O, D)[b][:, 0:2 * P],
                                part(moe, MOE, "b2"), ALU.add).then_inc(sem("C_ys"), 1)
            first_batch("C_")

            second_batch("C_", 3)

            def general(b):
                n = e.value_load(cnti[0:1, b:b + 1], min_val=0, max_val=NT)
                e.memset(gm[:, :], NEG).then_inc(sem(f"g_kvs{b}"), 1)
                e.memset(gV[:, :, DH:DH + 1], 1.0)
                e.memset(gacc[:, :, :], 0.0).then_inc(sem(f"g_acc{b}"), 1)
                e.drain()
                with e.Fori(0, NT) as i:
                    with e.If(n > i):
                        e.wait_ge(sem(f"gmask_in{b}"), i * 16 + 16)
                        e.tensor_scalar(gkeep[:, :], gmask[:, :], 0.0, None, ALU.not_equal)
                        e.drain()
                        e.tensor_scalar(gbias[0:1, :], gkeep[:, :], 1.0, -NEG, ALU.subtract, ALU.mult)
                        e.wait_ge(sem(f"g_kv{b}"), i + 1)
                        e.tensor_tensor(gKB[:, :, :], T[:, 0, 0:P].unsqueeze(1).to_broadcast([P, J, P]),
                                        delta.unsqueeze(2).to_broadcast([P, J, P]), ALU.mult)
                        e.tensor_copy(gV[:, :, 0:DH], T[:, 0, P:2 * P].rearrange("p (h d) -> p h d", d=DH))\
                            .then_inc(sem(f"g_kvs{b}"), 1)
                        e.wait_ge(sem(f"g_scores{b}"), i + 1)
                        sc = S[:, :, :].rearrange("p g (j k) -> p (g j) k", j=J)
                        e.tensor_reduce(gmt[:, :], sc, AX.X, ALU.max)
                        e.drain()
                        e.tensor_tensor(gmn[:, :], gmt[:, :], gm[:, :], ALU.max)
                        e.drain()
                        e.tensor_tensor(gal[:, :], gm[:, :], gmn[:, :], ALU.subtract)
                        e.drain()
                        e.tensor_copy(gm[:, :], gmn[:, :])
                        e.tensor_tensor(PR[:, 0:2, :, :].rearrange("p a j k -> p (a j) k"), sc,
                                        gmn[:, :].unsqueeze(2).to_broadcast([P, H, P]), ALU.subtract)\
                            .then_inc(sem(f"g_shift{b}"), 1)
                        for half in range(2):
                            e.wait_ge(sem(f"g_t{b}"), 2 * i + (half + 1))
                            e.tensor_copy(PT[:, half, :, :].rearrange("p j k -> p (j k)"),
                                          T[:, :, :].rearrange("p a n -> p (a n)")).then_inc(sem(f"g_ts{b}"), 1)
                        e.tensor_tensor(gsc[:, :, :], gacc[:, :, :], gal[:, :].unsqueeze(2).to_broadcast([P, H, DH + 1]),
                                        ALU.mult)
                        e.drain()
                        e.wait_ge(sem(f"g_pv{b}"), i + 1)
                        e.tensor_tensor(gacc[:, :, :], gsc[:, :, :],
                                        S[:, 0, 0:H * (DH + 1)].rearrange("p (h d) -> p h d", h=H), ALU.add)\
                            .then_inc(sem(f"g_acc{b}"), 1)
                        e.drain()
                e.reciprocal(grd[:, :], gacc[:, :, DH])
                e.drain()
                e.scalar_tensor_tensor(gpad[:, :, 0:DH], gacc[:, :, 0:DH], nanf[:, b:b + 1],
                                       grd[:, :].unsqueeze(2).to_broadcast([P, H, DH]), ALU.mult, ALU.mult)\
                    .then_inc(sem(f"g_pad{b}"), 1)
                e.wait_ge(sem(f"g_back{b}"), 1)
                e.tensor_copy(ON[:, b, :, :].rearrange("p g q -> p (g q)"), O[:, :]).then_inc(sem(f"g_on{b}"), 1)

            softmax("D_", NS, nanf)
            with e.If(e.value_load(most[0:1, 0:1], min_val=0, max_val=NT) > NS):
                for b in range(B):
                    general(b)
            both_batches("D_", 4)

            cw, cb = part(scanw, SCAN, "cw"), part(scanw, SCAN, "cb")
            e.wait_ge(sem("E_up"), 2)
            link(e.tensor_scalar(conv[:, :, :], upad[:, 0, :, 3:P + 3], cw[:, 3:4], cb[:, 0:1], ALU.mult, ALU.add))
            for k in range(3):
                ins = e.scalar_tensor_tensor(conv[:, :, :], upad[:, 0, :, k:k + P], cw[:, k:k + 1], conv[:, :, :],
                                             ALU.mult, ALU.add)
                if k < 2:
                    link(ins)
                else:
                    ins.then_inc(sem("E_conv"), 1)
            convs = (T[:, 0, 0:B * P], conv[:, :, :].rearrange("p b t -> p (b t)"))
            for k, ct in enumerate((1, 0)):
                e.wait_ge(sem("E_th"), k + 1)
                e.scalar_tensor_tensor(su[:, ct, :], th[:, ct, :], 1.0, convs[k], ALU.add, ALU.mult).then_inc(sem("E_su"), 1)
            e.wait_ge(sem("decay"), 4)
            e.wait_ge(sem("E_thg"), 2)
            e.wait_ge(sem("scan_const"), 2)
            bbc = part(scanw, SCAN, "bbc")

            def b_of(ct):
                e.wait_ge(sem("E_b"), ct + 1)
                return step(e.tensor_scalar(bT[:, ct, :], T[:, ct, 0:B * P], 0.5, bbc[:, ct:ct + 1], ALU.mult, ALU.add))

            def scan(ct, ready):
                e.wait_ge(sem("dve_step"), ready)
                return step(e.tensor_tensor_scan(st[:, ct, :], decay[:, ct, :, :].rearrange("p b t -> p (b t)"),
                                                 bT[:, ct, :], 0.0, ALU.mult, ALU.add))

            def gate(ct, ready):
                e.wait_ge(sem("dve_step"), ready)
                return step(e.scalar_tensor_tensor(thg[:, ct, :], thg[:, ct, :], 1.0, st[:, ct, :], ALU.add, ALU.mult))

            def output(ct, ready):
                e.wait_ge(sem("dve_step"), ready)
                e.wait_ge(sem("E_c"), ct + 1)
                e.scalar_tensor_tensor(gated[:, ct, :], (O, D)[ct][:, 0:B * P], bbc2[:, ct:ct + 1], thg[:, ct, :], ALU.add,
                                       ALU.mult).then_inc(sem("E_y"), 1)

            scanned0 = scan(0, b_of(0))
            b_ready1 = b_of(1)
            gated0 = gate(0, scanned0)
            scanned1 = scan(1, b_ready1)
            output(0, gated0)
            output(1, gate(1, scanned1))
            both_batches("E_", 5, 0.25)

            e.wait_ge(sem("xn"), 12)

            def quantise(src, peak, factor, scale, tmp, out, done):
                link(e.tensor_scalar(factor, peak, EPS, 1.0 / 127.0, ALU.max, ALU.mult))
                link(e.reciprocal(scale, factor))
                rounded = [step(e.tensor_scalar(tmp[:, b, :], src[:, b, :], scale[:, b:b + 1], MAGIC, ALU.mult, ALU.add))
                           for b in range(B)]
                for b in range(B):
                    e.wait_ge(sem("dve_step"), rounded[b])
                    e.tensor_scalar(out[:, b, :], tmp[:, b, :], MAGIC, 127.0, ALU.subtract, ALU.min).then_inc(sem(done), 1)

            link(e.tensor_reduce(amax[:, :], xn[:, :, :], AX.X, ALU.max, apply_absolute_value=True))
            quantise(xn, amax[:, :], fx[:, :], sx[:, :], qf, xq, "F_xq")
            halved = step(e.tensor_scalar(ch[:, :], fx[:, :], wmean[:, 0:1], 0.5, ALU.mult, ALU.mult))
            e.wait_ge(sem("F_xqt"), 1)
            e.tensor_copy(xqT[:, :], T[:, 0, :].bitcast(BF16)[:, 0:B * P]).then_inc(sem("F_xqs"), 1)
            e.wait_ge(sem("dve_step"), halved)
            link(e.tensor_tensor(kk[:, :], ch[:, :], fx[:, :], ALU.mult))
            e.tensor_scalar(kk[:, :], kk[:, :], wmean[:, 1:2], None, ALU.mult).then_inc(sem("F_ch"), 1)
            silu = []
            for b in range(B):
                e.wait_ge(sem("F_th"), b + 1)
                silu.append(step(e.scalar_tensor_tensor(hm[:, b, :], thf[:, b, :], 1.0, S[:, 2 * b, :], ALU.add,
                                                        ALU.mult)))
            e.wait_ge(sem("F_ch"), 1)
            product = []
            for b in range(B):
                e.wait_ge(sem("F_gate"), 2 * b + 2)
                e.wait_ge(sem("dve_step"), silu[b])
                product.append(step(e.scalar_tensor_tensor(hm[:, b, :], hm[:, b, :], kk[:, b:b + 1],
                                                           S[:, 2 * b + 1, :], ALU.mult, ALU.mult)))
            for b in range(B):
                e.wait_ge(sem("dve_step"), product[b])
                last = e.tensor_reduce(hmax[:, b:b + 1], hm[:, b, :], AX.X, ALU.max, apply_absolute_value=True)
            link(last)
            quantise(hm, hmax[:, :], kd[:, :], sh[:, :], thf, hq, "F_hq")
            scaled = step(e.tensor_scalar(kd[:, :], kd[:, :], wmean[:, 2:3], None, ALU.mult))
            e.wait_ge(sem("F_hqt"), 2)
            e.tensor_copy(hqT[:, 1, :, :].rearrange("p h t -> p (h t)"),
                          T[:, 1, :].bitcast(BF16)[:, 0:HC * P]).then_inc(sem("F_xqs"), 1)
            e.wait_ge(sem("dve_step"), scaled)
            for b in range(B):
                e.wait_ge(sem("F_out"), b + 1)
                e.scalar_tensor_tensor(X[:, b, :], (O, D)[b][:, 0:P], kd[:, b:b + 1], X[:, b, :], ALU.mult, ALU.add)\
                    .then_inc(sem("x_out"), 1)

        @block.tensor
        def _(e):
            def mm(out, lhsT, rhs, start=True, stop=True):
                return e.matmul(out, lhsT, rhs, start=start, stop=stop, skip_group_check=True)

            def norm_t(n, b):
                e.wait_ge(sem("xn"), B * n + b + 1)
                e.transpose(T[:, b, 0:P], xn[:, b, :], ident).then_inc(sem("xn_t"), 1)

            def keep_warm(where, bank=S[:, 3, :]):
                for _ in range(WARM[where]):
                    mm(bank.rearrange("p (j k) -> p j k", j=J), onesb[:, :],
                       onesb[:, :].unsqueeze(1).to_broadcast([P, J, P]))

            def softmax(p, ns, kb, v, bias, early=None):
                def scores(i):
                    b, g = divmod(i, G)
                    if g == 0:
                        e.wait_ge(sem(p + "kb"), (b + 1) * ns)
                        e.wait_ge(sem(p + "qt"), b + 1)
                    if ns == 1:
                        if i >= 4:
                            e.wait_ge(sem(p + "shifted"), i - 3)
                    elif i >= 2:
                        e.wait_ge(sem(p + "shifted"), i - 1)
                    for s in range(ns):
                        k = g if ns == 1 else 2 * (g % 2) + s
                        bias(S[:, k, :].rearrange("p (j k) -> p j k", j=J), b * ns + s)
                        last = mm(S[:, k, :], QZ[:, b, g, :], kb[:, b * ns + s, :, :].rearrange("p j k -> p (j k)"),
                                  start=False)
                    last.then_inc(sem(p + "scores"), 1)

                def turn(i):
                    e.wait_ge(sem(p + "prob"), i + 1)
                    if i == 0:
                        if p != "B_":
                            e.wait_ge(sem(p + "qt"), B)
                        e.wait_ge(sem(p + "va"), B * ns)
                    for s in range(ns):
                        u = i * ns + s
                        if s:
                            e.wait_ge(sem(p + "prob2"), i + 1)
                        if u >= 2:
                            e.wait_ge(sem(p + "pt"), u - 1)
                        for j in range(J):
                            last = e.transpose(T[:, u % 2, j * P:(j + 1) * P], PR[:, i % 4, s * J + j, :], ident)
                        last.then_inc(sem(p + "transposed"), 1)

                def pv(i):
                    b, g = divmod(i, G)
                    e.wait_ge(sem(p + "pt"), (i + 1) * ns)
                    bank, c = (O, g) if b == 0 else (D, g)
                    if i == 0:
                        e.wait_ge(sem(p + "kb"), B * ns)
                        e.wait_ge(sem(p + "qt"), B)
                    if i == B * G - 1:
                        e.wait_ge(sem(p + "on"), 1)
                        bank, c = O, 0
                    for s in range(ns):
                        for j in range(J):
                            last = e.matmul(bank[32 * j:32 * j + 32, c * P:(c + 1) * P], v[:, b * ns + s, g * J + j, :],
                                            PT[:, i % 4, s * J + j, :], start=(s == 0), stop=(s == ns - 1),
                                            tile_position=(0, 32 * j), skip_group_check=True)
                    last.then_inc(sem(p + "pv"), 1)

                ahead = 4 if ns == 1 else 2
                for i in range(ahead):
                    scores(i)
                for i in range(B * G):
                    if ns > 1 and i + ahead < B * G:
                        scores(i + ahead)
                    if i == B * G - 1 and early:
                        early()
                    turn(i)
                    if ns == 1 and i + ahead < B * G:
                        scores(i + ahead)
                    if i:
                        pv(i - 1)
                keep_warm("last_turn")
                pv(B * G - 1)

            def project(p, b, wo, brow):
                if brow is not None:
                    mm(S[:, b, 0:P], ones[0:1, :], brow, stop=False)
                for g in range(G):
                    e.wait_ge(sem(p + "on"), b + 1 if g < G - 1 or b == 0 else 3)
                    last = mm(S[:, b, 0:P], ON[:, b, g, :], wo[:, g * P:(g + 1) * P],
                              start=(g == 0 and brow is None), stop=(g == G - 1))
                last.then_inc(sem(p + "out"), 1)

            def causal(out, t):
                mm(out, identb, part(constb, CONSTB, "causal").unsqueeze(1).to_broadcast([P, J, P]), stop=False)

            def kept(out, t):
                mm(out, onesb[:, :], biasS[:, t, :].unsqueeze(1).to_broadcast([P, J, P]), stop=False)

            e.wait_ge(sem("pool_const"), 4)
            keep_warm("start")
            e.wait_ge(sem("first_in"), 16)
            fctx = part(first, FIRST, "ctx")
            mm(O[:, 0:B * P], part(first, FIRST, "wk"), fctx).then_inc(sem("A_k"), 1)
            e.wait_ge(sem("rows_in"), 16)
            for b in range(B):
                mm(S[:, 1, b * P:(b + 1) * P], tile(fctx, b), part(first, FIRST, "wv"), stop=False)
                mm(S[:, 1, b * P:(b + 1) * P], ones[0:1, :], part(rows, ROWS, "bv"), start=False).then_inc(sem("A_v"), 1)
            e.wait_ge(sem("const_in"), 16)
            for b in range(B):
                norm_t(0, b)
            keep_warm("A_q", D)
            for b in range(B):
                e.wait_ge(sem("xnT"), b + 1)
                mm(T[:, b, P:2 * P], part(first, FIRST, "wq"), tile(xnT, b)).then_inc(sem("A_q"), 1)
            e.wait_ge(sem("constb"), 1)

            e.wait_ge(sem("act"), 2)
            mm(D[0:1, 0:B * NT], actv[:, :], ident[0:B * NT, 0:B * NT])
            mm(D[:, B * NT:B * NT + B], ones[0:B * NT, :], actb[:, :]).then_inc(sem("act_t"), 1)

            def project_A(b):
                e.wait_ge(sem("attn_in"), 48)
                project("A_", b, woA[:, :, :].rearrange("p g c -> p (g c)"), part(rows, ROWS, "bo"))

            e.wait_ge(sem("A_va"), B)
            softmax("A_", 1, KB, VA, causal, early=lambda: project_A(0))
            project_A(1)
            keep_warm("A_norm")
            e.wait_ge(sem("attn_in"), 48)
            for b in range(B):
                norm_t(1, b)
                e.wait_ge(sem("xnT"), B + b + 1)
                banks = (S[:, 0, :], S[:, 2, :]) if b == 0 else (O, D)
                for bank, names, done in zip(banks, (("wk", "wks"), ("wq", "wqs")), ("B_k", "B_q")):
                    for k, w in enumerate(names):
                        last = mm(bank[:, k * P:(k + 1) * P], part(selfw, SELF, w), tile(xnT, b))
                    last.then_inc(sem(done), 1)
                mm(T[:, b, P:2 * P], tile(xnT, b), part(selfw, SELF, "wv")).then_inc(sem("B_v"), 1)

            def project_B(b):
                project("B_", b, part(selfw, SELF, "wo"), None)

            softmax("B_", 1, KB, VB, causal, early=lambda: project_B(0))
            project_B(1)
            e.wait_ge(sem("wabs"), 3)
            mm(O[:, 0:3], ones[:, :], wabs[:, :]).then_inc(sem("F_wsum"), 1)
            keep_warm("B_norm")

            e.wait_ge(sem("moe_in"), 16)
            for b in range(B):
                norm_t(2, b)
                e.wait_ge(sem("xnT"), 2 * B + b + 1)
                mm(S[:, 2, b * E:(b + 1) * E], tile(xnT, b), part(moe, MOE, "wr"), stop=False)
                last = mm(S[:, 2, b * E:(b + 1) * E], ones[0:1, :], part(rows, ROWS, "br"), start=False)
            last.then_inc(sem("C_logits"), 1)
            e.wait_ge(sem("attn_in"), 48)
            e.wait_ge(sem("ctxS_in"), 16 * B * NS)
            mm(O[:, :], part(cross, CROSS, "wk"), ctxS[:, :, :].rearrange("p s k -> p (s k)")).then_inc(sem("D_k"), 1)
            for t in range(B * NS):
                last = mm(D[:, t * P:(t + 1) * P], ctxS[:, t, :], part(cross, CROSS, "wv"))
            last.then_inc(sem("D_v"), 1)
            e.wait_ge(sem("C_oh"), B)
            mm(S[:, 3, 0:B * E], part(constb, CONSTB, "before"), ohb[:, :, :].rearrange("p b e -> p (b e)"))\
                .then_inc(sem("C_cnt"), 1)
            for b in range(B):
                e.wait_ge(sem("C_disp"), b + 1)
                mm(T[:, b, 0:E * SLOTS], xn[:, b, :], disp[:, b * E:(b + 1) * E, :].rearrange("p e s -> p (e s)"))\
                    .then_inc(sem("C_buf"), 1)
            e.wait_ge(sem("C_comb"), B)
            e.wait_ge(sem("D_va"), B * NS)
            for b in range(B):
                for h in range(2):
                    q = 2 * b + h
                    last = e.transpose(D[:, q * P:(q + 1) * P],
                                       comb[:, b * E + 4 * h:b * E + 4 * h + 4, :].rearrange("p e s -> p (e s)"), ident)
            last.then_inc(sem("C_ct"), 1)
            e.wait_ge(sem("C_bufs"), 2)
            for i in range(4):
                e.wait_ge(sem(f"w1_in{i}"), 16)
                for k in range(2 * HC):
                    ex, hc = 2 * i + k // HC, k % HC
                    last = mm(S[:, i, k * B * SLOTS:(k + 1) * B * SLOTS], w1[:, ex, hc * P:(hc + 1) * P],
                              buf[:, ex, :, :].rearrange("p b s -> p (b s)"))
                last.then_inc(sem("C_hp"), 1)
            e.wait_ge(sem("D_kb"), B * NS)
            e.wait_ge(sem("C_cts"), 1)
            for b in range(B):
                for h in range(2):
                    if b == 0:
                        e.wait_ge(sem("C_h"), 2 * h + 2)
                        e.wait_ge(sem("w2_in"), 32)
                    for hc in range(HC):
                        for j in range(4):
                            ex = 4 * h + j
                            last = e.matmul((O, D)[b][32 * j:32 * j + 32, h * P:(h + 1) * P],
                                            hid[:, ex, hc, b * SLOTS:(b + 1) * SLOTS], w2[:, ex * HC + hc, :],
                                            start=(hc == 0), stop=(hc == HC - 1), tile_position=(0, 32 * j),
                                            skip_group_check=True)
                last.then_inc(sem("C_y"), 1)
            for b in range(B):
                e.wait_ge(sem("C_ys"), b + 1)
                for h in range(2):
                    last = mm(S[:, b, 0:P], combT[:, b, h, :], ysb[:, b, h, :], start=(h == 0), stop=(h == 1))
                last.then_inc(sem("C_out"), 1)
            keep_warm("C_norm")

            for b in range(B):
                norm_t(3, b)
            for b in range(B):
                e.wait_ge(sem("xnT"), 3 * B + b + 1)
                mm(T[:, b, P:2 * P], part(cross, CROSS, "wq"), tile(xnT, b)).then_inc(sem("D_q"), 1)
            e.wait_ge(sem("D_bias"), B * NS)

            def general(b):
                n = e.value_load(cnti[0:1, b:b + 1], min_val=0, max_val=NT)
                with e.Fori(0, NT) as i:
                    with e.If(n > i):
                        e.wait_ge(sem(f"gctx_in{b}"), i * 16 + 16)
                        e.wait_ge(sem(f"g_acc{b}"), i + 1)
                        mm(T[:, 0, 0:P], part(cross, CROSS, "wk"), gctx[:, :])
                        mm(T[:, 0, P:2 * P], gctx[:, :], part(cross, CROSS, "wv")).then_inc(sem(f"g_kv{b}"), 1)
                        e.wait_ge(sem(f"g_kvs{b}"), i + 2)
                        for g in range(G):
                            mm(S[:, g, :].rearrange("p (j k) -> p j k", j=J), onesb[:, :],
                               gbias[:, :].unsqueeze(1).to_broadcast([P, J, P]), stop=False)
                            last = mm(S[:, g, :], QZ[:, b, g, :],
                                      gKB[:, :, :].rearrange("p j k -> p (j k)"), start=False)
                        last.then_inc(sem(f"g_scores{b}"), 1)
                        e.wait_ge(sem(f"g_exp{b}"), i + 1)
                        for half in range(2):
                            if half:
                                e.wait_ge(sem(f"g_ts{b}"), 2 * i + 1)
                            for k in range(8):
                                last = e.transpose(T[:, k // 4, (k % 4) * P:(k % 4 + 1) * P], PR[:, half, k, :], ident)
                            last.then_inc(sem(f"g_t{b}"), 1)
                        e.wait_ge(sem(f"g_ts{b}"), 2 * i + 2)
                        for h in range(H):
                            last = mm(S[:, 0, h * (DH + 1):(h + 1) * (DH + 1)], PT[:, h // 8, h % 8, :], gV[:, h, :])
                        last.then_inc(sem(f"g_pv{b}"), 1)
                e.wait_ge(sem(f"g_pad{b}"), 1)
                for g in range(G):
                    last = e.transpose(O[:, g * P:(g + 1) * P],
                                       gpad[:, g * J:(g + 1) * J, :].rearrange("p j c -> p (j c)"), ident)
                last.then_inc(sem(f"g_back{b}"), 1)
                e.wait_ge(sem(f"g_on{b}"), 1)

            softmax("D_", NS, KBx, VX, kept)
            with e.If(e.value_load(most[0:1, 0:1], min_val=0, max_val=NT) > NS):
                e.wait_ge(sem("D_on"), 3)
                for b in range(B):
                    general(b)
            for b in range(B):
                project("D_", b, part(cross, CROSS, "wo"), part(rows, ROWS, "bproj"))
            keep_warm("D_norm")

            for b in range(B):
                norm_t(4, b)
            e.wait_ge(sem("xnT"), 5 * B)
            win = part(scanw, SCAN, "win")
            for ct in (1, 0, 2, 3):
                mm(S[:, ct, 0:B * P], tile(win, ct), xnT[:, :]).then_inc(sem("E_u" if ct < 2 else "E_g"), 1)
            e.wait_ge(sem("scan_const"), 6)
            for b in range(B):
                mm(T[:, 0, b * P:(b + 1) * P], part(rows, ROWS, "cb"), ones[0:1, :], start=(b == 0), stop=False)
            e.wait_ge(sem("E_up"), 1)
            for k in range(4):
                last = mm(T[:, 0, 0:B * P].rearrange("p (b t) -> p b t", b=B), taps[:, k, :], upad[:, 1, :, k:k + P],
                          start=False, stop=(k == 3))
            last.then_inc(sem("E_convp"), 1)
            keep_warm("E_conv", D)
            wbc = part(scanw, SCAN, "wbc")
            for ct in range(2):
                e.wait_ge(sem("E_su"), 2)
                for kt in range(2):
                    last = mm(T[:, ct, 0:B * P], wbc[:, kt * 512 + ct * P:kt * 512 + (ct + 1) * P], su[:, kt, :],
                              start=(kt == 0), stop=(kt == 1))
                last.then_inc(sem("E_b"), 1)
            for ct in range(2):
                for kt in range(2):
                    last = mm((O, D)[ct][:, 0:B * P], wbc[:, kt * 512 + (2 + ct) * P:kt * 512 + (3 + ct) * P], su[:, kt, :],
                              start=(kt == 0), stop=(kt == 1))
                last.then_inc(sem("E_c"), 1)
            keep_warm("E_gate", S[:, 1, :])
            wout = part(scanw, SCAN, "wout")
            for b in range(B):
                mm(S[:, b, 0:P], fours[0:1, :], part(rows, ROWS, "bout"), stop=False)
            for kt in range(2):
                e.wait_ge(sem("E_y"), kt + 1)
                for b in range(B):
                    last = mm(S[:, b, 0:P], gated[:, kt, b * P:(b + 1) * P], wout[:, kt * P:(kt + 1) * P], start=False,
                              stop=(kt == 1))
                    if kt:
                        last.then_inc(sem("E_out"), 1)

            keep_warm("E_norm")
            for b in range(B):
                e.wait_ge(sem("F_xq"), b + 1)
                last = e.transpose(T[:, 0, :].bitcast(BF16)[:, b * P:(b + 1) * P], xq[:, b, :], identb)
            last.then_inc(sem("F_xqt"), 1)
            e.wait_ge(sem("F_xqs"), 1)
            e.wait_ge(sem("w_round"), 9)
            for b in range(B):
                mm(S[:, 2 * b, :], tile(xqT, b), wq3[:, 0, :]).then_inc(sem("F_gate"), 1)
                mm(S[:, 2 * b + 1, :], tile(xqT, b), wq3[:, 1, :]).then_inc(sem("F_gate"), 1)
            for b in range(B):
                e.wait_ge(sem("F_hq"), b + 1)
                for hc in range(HC):
                    last = e.transpose(T[:, b, :].bitcast(BF16)[:, hc * P:(hc + 1) * P], hq[:, b, hc * P:(hc + 1) * P], identb)
                last.then_inc(sem("F_hqt"), 1)
            for b in range(B):
                e.wait_ge(sem("F_hqs") if b == 0 else sem("F_xqs"), b + 1)
                for hc in range(HC):
                    last = mm((O, D)[b][:, 0:P], hqT[:, b, hc, :], wq3[:, 2, hc * P:(hc + 1) * P], start=(hc == 0), stop=(hc == HC - 1))
                last.then_inc(sem("F_out"), 1)


def constants():
    c = np.zeros((P, CONST_W), np.float32)

    def put(name, value):
        a, b = CONST[name]
        c[:, a:b] = value

    r = np.arange(P)
    put("ident", np.eye(P))
    put("causal", np.where(r[None, :] > r[:, None], NEG, 0.0))
    put("before", r[:, None] < r[None, :])
    inv = (np.float32(1.0) / np.float32(10000.0) ** (np.arange(0, DH, 2, dtype=np.float32) / np.float32(DH))).astype(np.float32)
    ang = (r.astype(np.float32)[None, :] * inv[(r % DH) % (DH // 2)][:, None]).astype(np.float32)
    put("cos", np.cos(ang))
    put("sin", np.where((r % DH < DH // 2)[:, None], -np.sin(ang), np.sin(ang)))
    put("delta", (r[:, None] // DH % J == np.arange(J)[None, :]))
    put("group", SCALE * (r[:, None] // 32 == np.arange(G)[None, :]))
    put("slot", np.where(np.arange(SLOTS) < CAP, np.arange(SLOTS), -1)[None, :])
    put("tile", (r % NT + 1)[:, None])
    put("batch", (r[:, None] // NT == np.arange(B)[None, :]))
    put("expert", np.arange(E)[None, :])
    return c


def layout(i):
    def pack(table, width, parts, n=P):
        out = np.zeros((n, width), np.float32)
        for name, v in parts.items():
            a, b = table[name]
            out[:, a:b] = v
        return out

    def heads(w):
        out = np.zeros((J, 32, G, P), np.float32)
        out[:, 0:DH] = w.reshape(G, J, DH, P).transpose(1, 2, 0, 3)
        return out.reshape(P, G * P)

    def tiles(w, n):
        return w.reshape(n, P, -1).transpose(1, 0, 2).reshape(P, -1)

    def cols(v, n):
        return v.reshape(n, P).T

    ctxT = np.ascontiguousarray(i["ctx_1024"].transpose(2, 0, 1))
    swap = (np.arange(P) // DH) * DH + (np.arange(P) + DH // 2) % DH
    a = {}
    a["x"] = i["x"]
    a["ctxT"] = ctxT
    a["mask"] = i["mask_BxS2_ik0"]
    a["first"] = pack(FIRST, FIRST_W, dict(
        wq=i["L0_xattn_Wq"].T, wk=i["L0_xattn_Wk"].T, wv=i["L0_xattn_Wv"].T, bq=i["L0_xattn_bq"][:, None],
        bk=i["L0_xattn_bk"][:, None], ctx=ctxT[:, :, 0:P].reshape(P, B * P)))
    a["const"] = constants()
    a["woA"] = heads(i["L0_xattn_Wo"].T).reshape(P, G, P)
    wqT, wkT = i["L0_attn_Wq"].T, i["L0_attn_Wk"].T
    a["selfw"] = pack(SELF, SELF_W, dict(wq=wqT, wqs=wqT[:, swap], wk=wkT, wks=wkT[:, swap], wv=i["L0_attn_Wv"].T,
                                         wo=heads(i["L0_attn_Wo"].T)))
    a["rows"] = pack(ROWS, ROWS_W, dict(bv=i["L0_xattn_bv"], bo=i["L0_xattn_bo"], br=i["L0_ffn_br"],
                                        bproj=i["L1_xattn_bproj"], bout=i["L1_attn_b_out"],
                                        cb=i["L1_attn_conv_b"][P:2 * P]), 1)
    b1 = i["L0_ffn_b1"].reshape(E, HC, P).transpose(2, 0, 1).reshape(P, E * HC)
    b2 = np.repeat(i["L0_ffn_b2"].reshape(2, 4, P).transpose(1, 0, 2), 32, axis=0).reshape(P, 2 * P)
    a["moe"] = pack(MOE, MOE_W, dict(wr=i["L0_ffn_Wr"], b1=b1, b2=b2))
    a["w1"] = i["L0_ffn_W1"].transpose(1, 0, 2)
    a["w2"] = i["L0_ffn_W2"].reshape(E * HC, P, P).transpose(1, 0, 2)
    a["cross"] = pack(CROSS, CROSS_W, dict(wq=i["L1_xattn_Wq"], wk=i["L1_xattn_Wkv"][:, 0:P],
                                           wv=i["L1_xattn_Wkv"][:, P:2 * P], wo=heads(i["L1_xattn_Wproj"])))
    a["scanw"] = pack(SCAN, SCAN_W, dict(
        win=i["L1_attn_W_in"], bin=cols(i["L1_attn_b_in"], 4), cw=tiles(i["L1_attn_conv_w"][:, 0, :], 2),
        cb=cols(i["L1_attn_conv_b"], 2), bbc=cols(i["L1_attn_b_bc"], 4), ld=cols(i["L1_attn_log_decay"], 2),
        wout=tiles(i["L1_attn_W_out"], 2), wbc=tiles(i["L1_attn_W_bc"], 2)))
    a["ffn"] = pack(FFN, FFN_W, dict(gate=i["L1_ffn_w_gate"].T, up=i["L1_ffn_w_up"].T,
                                     down=tiles(np.ascontiguousarray(i["L1_ffn_w_down"].T), 4)))
    return {k: np.ascontiguousarray(v) for k, v in a.items()}


def kernel(**inputs):
    import concourse.bacc as bacc
    from concourse.bass_utils import run_bass_kernel_spmd

    nc = bacc.Bacc("TRN2", target_bir_lowering=False, num_devices=1)
    arrays = {f"in_{k}": v for k, v in layout({k: np.asarray(v) for k, v in inputs.items()}).items()}
    d = {k[3:]: nc.dram_tensor(k, v.shape, mybir.dt.from_np(v.dtype), kind="ExternalInput").ap()
         for k, v in arrays.items()}
    d["out"] = nc.dram_tensor("out_0", (B, P, P), F32, kind="ExternalOutput").ap()
    program(nc, d)
    r = run_bass_kernel_spmd(nc, [arrays], core_ids=[0])
    return r.results[0]["out_0"]
```
